# Optimizing a Trainium2 kernel written in Bass

```python
import numpy as np
import jax
import jax.numpy as jnp

def _softmax(x, axis=-1):
    return jax.nn.softmax(x, axis=axis)

def _gelu(x):
    return jax.nn.gelu(x, approximate=True)

def _silu(x):
    return jax.nn.silu(x)

def _sigmoid(x):
    return jax.nn.sigmoid(x)

def _layernorm(x, axis=-1, eps=1e-05):
    m = jnp.mean(x, axis=axis, keepdims=True)
    v = jnp.var(x, axis=axis, keepdims=True)
    return (x - m) / jnp.sqrt(v + eps)

def _scatter_add(tgt, idx, src, axis=0):
    return tgt.at[idx].add(src)

def _segment_sum(src, seg, n):
    return jax.ops.segment_sum(src, seg, n)
kernel_name = 'mk_macaron_d2_jaxref_r8_8a0c21'

def setup_inputs(seed: int=0):
    np.random.seed(seed)
    _w = jnp.asarray

    def _L0_attn_setup():
        import jax, jax.numpy as jnp
        import numpy as np
        C = 8.0
        B, S, D = (4, 512, 256)
        key = jax.random.key(seed)
        k1, k2, k3, k4 = jax.random.split(key, 4)
        x = jax.random.normal(k1, (B, S, D), dtype=jnp.float32)
        std = 1.0 / np.sqrt(D)
        Wa = jax.random.normal(k2, (D, D), dtype=jnp.float32) * std
        Wx = jax.random.normal(k3, (D, D), dtype=jnp.float32) * std
        ba = jnp.zeros((D,), dtype=jnp.float32)
        bx = jnp.zeros((D,), dtype=jnp.float32)
        u = jax.random.uniform(k4, (D,), minval=0.9, maxval=0.999, dtype=jnp.float32)
        Lam = -jnp.log(u ** (-1.0 / C) - 1.0)
        return {'x': x, 'Wa': Wa, 'Wx': Wx, 'ba': ba, 'bx': bx, 'Lam': Lam}
    _L0_attn_in = _L0_attn_setup()

    def _L0_ffn_setup():
        import jax, jax.numpy as jnp
        import numpy as np
        E = 32
        G = 8
        TKG = 4
        K = 4
        D = 256
        H = 128
        HS = 512
        SCALE = 2.5
        CAP = 128

        def relu2(x):
            r = jnp.maximum(x, 0.0)
            return r * r

        def route_tokens(scores, bias_corr):
            T = scores.shape[0]
            scores_c = scores + bias_corr
            group_scores = jax.lax.top_k(scores_c.reshape(T, G, E // G), 2)[0].sum(-1)
            _, group_idx = jax.lax.top_k(group_scores, TKG)
            group_mask = jnp.zeros((T, G), scores.dtype).at[jnp.arange(T)[:, None], group_idx].set(1.0)
            score_mask = jnp.repeat(group_mask, E // G, axis=1)
            masked = jnp.where(score_mask > 0, scores_c, 0.0)
            _, topk_idx = jax.lax.top_k(masked, K)
            topk_w = jnp.take_along_axis(scores, topk_idx, axis=1)
            topk_w = topk_w / (topk_w.sum(-1, keepdims=True) + 1e-20)
            return (topk_idx, topk_w * SCALE)
        key = jax.random.key(seed)
        ks = jax.random.split(key, 6)
        B, S = (2, 256)
        return dict(hidden_states=jax.random.normal(ks[0], (B, S, D), jnp.float32), gate_w=jax.random.normal(ks[1], (E, D), jnp.float32) * 0.02, bias_corr=jnp.zeros((E,), jnp.float32), up_w=jax.random.normal(ks[2], (E, H, D), jnp.float32) * 0.02, down_w=jax.random.normal(ks[3], (E, D, H), jnp.float32) * 0.02, shared_up_w=jax.random.normal(ks[4], (HS, D), jnp.float32) * 0.02, shared_down_w=jax.random.normal(ks[5], (D, HS), jnp.float32) * 0.02)
    _L0_ffn_in = _L0_ffn_setup()

    def _L1_attn_setup():
        import jax, jax.numpy as jnp
        import numpy as np
        DIM = 256
        NUM_HEADS = 16
        HEAD_DIM = DIM // NUM_HEADS
        NEG = -10000.0
        key = jax.random.key(seed)
        k1, k2, k3, k4, k5 = jax.random.split(key, 5)
        B, S = (2, 256)
        x = jax.random.normal(k1, (B, S, DIM), dtype=jnp.float32)
        s = 1.0 / np.sqrt(DIM)
        W_qkv = jax.random.normal(k2, (DIM, 3 * DIM), dtype=jnp.float32) * s
        b_qkv = jax.random.normal(k3, (3 * DIM,), dtype=jnp.float32) * 0.01
        W_out = jax.random.normal(k4, (DIM, DIM), dtype=jnp.float32) * s
        b_out = jax.random.normal(k5, (DIM,), dtype=jnp.float32) * 0.01
        return {'x': x, 'W_qkv': W_qkv, 'b_qkv': b_qkv, 'W_out': W_out, 'b_out': b_out}
    _L1_attn_in = _L1_attn_setup()

    def _L1_ffn_setup():
        import jax, jax.numpy as jnp
        import numpy as np
        DIM = 256
        HID = 704
        ZERO_POINT = 128.0

        def _qlinear(x, wq, scale):
            W = (wq.astype(jnp.float32) - ZERO_POINT) * scale[:, None]
            return jnp.einsum('bsd,hd->bsh', x, W)
        key = jax.random.key(seed)
        ks = jax.random.split(key, 7)
        B, S = (4, 256)
        sg = jax.random.uniform(ks[1], (HID,)) * (0.02 / np.sqrt(DIM)) + 0.0001
        su = jax.random.uniform(ks[3], (HID,)) * (0.02 / np.sqrt(DIM)) + 0.0001
        sd = jax.random.uniform(ks[5], (DIM,)) * (0.02 / np.sqrt(HID)) + 0.0001
        return {'x': jax.random.normal(ks[0], (B, S, DIM), dtype=jnp.float32), 'wq_gate': jax.random.randint(ks[2], (HID, DIM), 0, 32, dtype=jnp.int32), 's_gate': sg, 'wq_up': jax.random.randint(ks[4], (HID, DIM), 0, 32, dtype=jnp.int32), 's_up': su, 'wq_down': jax.random.randint(ks[6], (DIM, HID), 0, 32, dtype=jnp.int32), 's_down': sd}
    _L1_ffn_in = _L1_ffn_setup()
    _d = {'L0_attn_x': _L0_attn_in['x'], 'L0_attn_Wa': _L0_attn_in['Wa'], 'L0_attn_Wx': _L0_attn_in['Wx'], 'L0_attn_ba': _L0_attn_in['ba'], 'L0_attn_bx': _L0_attn_in['bx'], 'L0_attn_Lam': _L0_attn_in['Lam'], 'L0_ffn_gate_w': _L0_ffn_in['gate_w'], 'L0_ffn_bias_corr': _L0_ffn_in['bias_corr'], 'L0_ffn_up_w': _L0_ffn_in['up_w'], 'L0_ffn_down_w': _L0_ffn_in['down_w'], 'L0_ffn_shared_up_w': _L0_ffn_in['shared_up_w'], 'L0_ffn_shared_down_w': _L0_ffn_in['shared_down_w'], 'L1_attn_W_qkv': _L1_attn_in['W_qkv'], 'L1_attn_b_qkv': _L1_attn_in['b_qkv'], 'L1_attn_W_out': _L1_attn_in['W_out'], 'L1_attn_b_out': _L1_attn_in['b_out'], 'L1_ffn_wq_gate': _L1_ffn_in['wq_gate'], 'L1_ffn_s_gate': _L1_ffn_in['s_gate'], 'L1_ffn_wq_up': _L1_ffn_in['wq_up'], 'L1_ffn_s_up': _L1_ffn_in['s_up'], 'L1_ffn_wq_down': _L1_ffn_in['wq_down'], 'L1_ffn_s_down': _L1_ffn_in['s_down']}
    _x0 = _d['L0_attn_x']
    _d['L0_attn_x'] = jax.random.normal(jax.random.fold_in(jax.random.key(seed), 1), (2, 512, 256), dtype=_x0.dtype)
    del _x0
    return _d

def reference(L0_attn_x, L0_attn_Wa, L0_attn_Wx, L0_attn_ba, L0_attn_bx, L0_attn_Lam, L0_ffn_gate_w, L0_ffn_bias_corr, L0_ffn_up_w, L0_ffn_down_w, L0_ffn_shared_up_w, L0_ffn_shared_down_w, L1_attn_W_qkv, L1_attn_b_qkv, L1_attn_W_out, L1_attn_b_out, L1_ffn_wq_gate, L1_ffn_s_gate, L1_ffn_wq_up, L1_ffn_s_up, L1_ffn_wq_down, L1_ffn_s_down):

    def _L0_attn_ref(x, Wa, Wx, ba, bx, Lam):
        import jax, jax.numpy as jnp
        import numpy as np
        C = 8.0
        B, S, D = (4, 512, 256)
        r = jax.nn.sigmoid(jnp.einsum('bsd,hd->bsh', x, Wa) + ba)
        i = jax.nn.sigmoid(jnp.einsum('bsd,hd->bsh', x, Wx) + bx)
        log_a = -C * jax.nn.softplus(-Lam) * r
        a = jnp.exp(log_a)
        u = jnp.sqrt(1.0 - a ** 2) * (i * x)
        a_t = jnp.moveaxis(a, 1, 0)
        u_t = jnp.moveaxis(u, 1, 0)

        def step(h, au):
            at, ut = au
            h = at * h + ut
            return (h, h)
        h0 = jnp.zeros((x.shape[0], x.shape[2]), dtype=x.dtype)
        _, y = jax.lax.scan(step, h0, (a_t, u_t))
        return jnp.moveaxis(y, 0, 1)

    def _L0_ffn_ref(hidden_states, gate_w, bias_corr, up_w, down_w, shared_up_w, shared_down_w):
        import jax, jax.numpy as jnp
        import numpy as np
        E = 32
        G = 8
        TKG = 4
        K = 4
        D = 256
        H = 128
        HS = 512
        SCALE = 2.5
        CAP = 128

        def relu2(x):
            r = jnp.maximum(x, 0.0)
            return r * r

        def route_tokens(scores, bias_corr):
            T = scores.shape[0]
            scores_c = scores + bias_corr
            group_scores = jax.lax.top_k(scores_c.reshape(T, G, E // G), 2)[0].sum(-1)
            _, group_idx = jax.lax.top_k(group_scores, TKG)
            group_mask = jnp.zeros((T, G), scores.dtype).at[jnp.arange(T)[:, None], group_idx].set(1.0)
            score_mask = jnp.repeat(group_mask, E // G, axis=1)
            masked = jnp.where(score_mask > 0, scores_c, 0.0)
            _, topk_idx = jax.lax.top_k(masked, K)
            topk_w = jnp.take_along_axis(scores, topk_idx, axis=1)
            topk_w = topk_w / (topk_w.sum(-1, keepdims=True) + 1e-20)
            return (topk_idx, topk_w * SCALE)
        B, S, _ = hidden_states.shape
        T = B * S
        flat = hidden_states.reshape(T, D)
        logits = flat @ gate_w.T
        scores = jax.nn.sigmoid(logits)
        topk_idx, topk_w = route_tokens(scores, bias_corr)
        e_flat = topk_idx.reshape(-1)
        oh = jax.nn.one_hot(e_flat, E, dtype=jnp.int32)
        pos = jnp.take_along_axis(jnp.cumsum(oh, axis=0) - 1, e_flat[:, None], axis=1)[:, 0]
        tok = jnp.repeat(jnp.arange(T), K)
        valid = pos < CAP
        xe = jnp.zeros((E, CAP, D), flat.dtype).at[e_flat, pos].set(flat[tok], mode='drop')
        h = relu2(jnp.einsum('ecd,ehd->ech', xe, up_w))
        ye = jnp.einsum('ech,edh->ecd', h, down_w)
        gathered = ye[e_flat, jnp.minimum(pos, CAP - 1)]
        gathered = jnp.where(valid[:, None], gathered, 0.0) * topk_w.reshape(-1)[:, None]
        routed = gathered.reshape(T, K, D).sum(axis=1).reshape(B, S, D)
        shared = relu2(hidden_states @ shared_up_w.T) @ shared_down_w.T
        return routed + shared

    def _L1_attn_ref(x, W_qkv, b_qkv, W_out, b_out):
        import jax, jax.numpy as jnp
        import numpy as np
        DIM = 256
        NUM_HEADS = 16
        HEAD_DIM = DIM // NUM_HEADS
        NEG = -10000.0
        B, S, _ = x.shape
        qkv = x @ W_qkv + b_qkv
        qkv = qkv.reshape(B, S, NUM_HEADS, 3 * HEAD_DIM).transpose(0, 2, 1, 3)
        q, k, v = jnp.split(qkv, 3, axis=-1)
        scores = jnp.einsum('bhqd,bhkd->bhqk', q, k) / np.sqrt(HEAD_DIM)
        causal = jnp.tril(jnp.ones((S, S), dtype=bool))[None, None]
        scores = jnp.where(causal, scores, NEG)
        probs = jax.nn.softmax(scores, axis=-1)
        ctx = jnp.einsum('bhqk,bhkd->bhqd', probs, v)
        ctx = ctx.transpose(0, 2, 1, 3).reshape(B, S, DIM)
        return ctx @ W_out + b_out

    def _L1_ffn_ref(x, wq_gate, s_gate, wq_up, s_up, wq_down, s_down):
        import jax, jax.numpy as jnp
        import numpy as np
        DIM = 256
        HID = 704
        ZERO_POINT = 128.0

        def _qlinear(x, wq, scale):
            W = (wq.astype(jnp.float32) - ZERO_POINT) * scale[:, None]
            return jnp.einsum('bsd,hd->bsh', x, W)
        gate = _qlinear(x, wq_gate, s_gate)
        gate = jax.nn.silu(gate)
        up = _qlinear(x, wq_up, s_up)
        return _qlinear(gate * up, wq_down, s_down)
    x = L0_attn_x
    x = x + 0.5 * _L0_ffn_ref(_layernorm(x, axis=-1), L0_ffn_gate_w, L0_ffn_bias_corr, L0_ffn_up_w, L0_ffn_down_w, L0_ffn_shared_up_w, L0_ffn_shared_down_w)
    x = x + _L0_attn_ref(_layernorm(x, axis=-1), L0_attn_Wa, L0_attn_Wx, L0_attn_ba, L0_attn_bx, L0_attn_Lam)
    x = x + 0.5 * _L0_ffn_ref(_layernorm(x, axis=-1), L0_ffn_gate_w, L0_ffn_bias_corr, L0_ffn_up_w, L0_ffn_down_w, L0_ffn_shared_up_w, L0_ffn_shared_down_w)
    x = x + 0.5 * _L1_ffn_ref(_layernorm(x, axis=-1), L1_ffn_wq_gate, L1_ffn_s_gate, L1_ffn_wq_up, L1_ffn_s_up, L1_ffn_wq_down, L1_ffn_s_down)
    x = x + _L1_attn_ref(_layernorm(x, axis=-1), L1_attn_W_qkv, L1_attn_b_qkv, L1_attn_W_out, L1_attn_b_out)
    x = x + 0.5 * _L1_ffn_ref(_layernorm(x, axis=-1), L1_ffn_wq_gate, L1_ffn_s_gate, L1_ffn_wq_up, L1_ffn_s_up, L1_ffn_wq_down, L1_ffn_s_down)
    return x

_drawn_inputs = setup_inputs


def setup_inputs(seed=0):
    import zlib

    import numpy as np

    out = dict(_drawn_inputs(seed))
    spreads = {'L0_attn_ba': (0.0, 0.8), 'L0_attn_bx': (0.0, 0.463), 'L0_ffn_bias_corr': (0.0, 0.276)}
    factors = {'L0_ffn_gate_w': 3.201,
     'L0_ffn_up_w': 2.989,
     'L1_attn_b_qkv': 6.47,
     'L1_attn_b_out': 7.374,
     'L1_ffn_s_gate': 8.0,
     'L1_ffn_s_up': 8.0,
     'L1_ffn_s_down': 8.0}
    for name, (base, spread) in spreads.items():
        noise = np.random.default_rng([zlib.crc32(name.encode()), seed]).standard_normal(out[name].shape)
        drawn = base * np.exp(spread * noise) if base else spread * noise
        out[name] = jnp.asarray(drawn.astype(out[name].dtype))
    for name, factor in factors.items():
        out[name] = (out[name] * factor).astype(out[name].dtype)
    return out
```

```python
from contextlib import ExitStack

import numpy as np
import concourse.bass as bass
from concourse import mybir

F32 = mybir.dt.float32
F16 = mybir.dt.float16
BF16 = mybir.dt.bfloat16
I32 = mybir.dt.int32
ALU = mybir.AluOpType
ACT = mybir.ActivationFunctionType
AX = mybir.AxisListType

P = 128
D = 256
KD = D // P
T = 1024
NT = T // P
SEQ = 512
NB = T // SEQ
TH = NT // NB
EPS = 1e-5

E = 32
EG = 8
EPG = E // EG
TOPK = 4
CAP = 128
H = 128
HS = 512
MS = HS // P
SCALE = 2.5
SLOT_A = 8
SLOT_B = CAP // SLOT_A
EH = E // 2
SENTINEL = -3.0e38
PICKED = 3.0e38
FAR = 512.0

NH = 16
HD = D // NH
MASKED = -1.0e30

HID = 704
HID_TILES = [128, 128, 112, 112, 112, 112]
HID_AT = [sum(HID_TILES[:i]) for i in range(len(HID_TILES))]
NHID = len(HID_TILES)
ZERO_POINT = 128.0

MOE, RECUR, QFFN, ATTN = "moe", "recur", "qffn", "attn"
STAGES = [MOE, RECUR, MOE, QFFN, ATTN, QFFN]
LAST = len(STAGES)


class Counts:

    def __init__(self):
        self.values = {}
        self.sems = {}
        self.total = {}

    def start(self, make):
        self.make, self.sems, self.total = make, {}, {}

    def sem(self, name):
        if name not in self.sems:
            self.sems[name] = self.make(name)
        return self.sems[name]

    def mark(self, name, *which, by=1):
        self.total[name] = self.total.get(name, 0) + by
        self.values[(name, *which)] = self.total[name]
        return self.sem(name), by

    def at(self, name, *which):
        return self.sem(name), self.values.get((name, *which), 1)


def build(nc, a, counts):
    with ExitStack() as ctx:
        counts.start(lambda name: ctx.enter_context(nc.semaphore(name)))
        mark, at = counts.mark, counts.at

        def mark16(name, *which):
            return mark(name, *which, by=16)

        def sb(name, shape, dt=F32):
            return ctx.enter_context(nc.sbuf_tensor(name, shape, dt))

        x = sb("x", [P, NT, D])
        xn = sb("xn", [P, NT, D])
        xnT = sb("xnT", [P, KD, T])

        big = sb("big", [P, 2, 8192])
        xt = sb("xt", [P, 8192])
        rt = sb("rt", [P, 4096])
        rg = sb("rg", [P, 6144])
        sh = sb("sh", [P, 4480])
        gs = sb("gs", [P, 2176])

        up_w = big[:, 0, :].rearrange("p (k e h) -> p k e h", k=KD, e=E)
        down_w = big[:, 1, :].rearrange("p (e d) -> p e d", e=E)
        gate_w = gs[:, 0:KD * E].rearrange("p (k e) -> p k e", k=KD)
        sup_w = gs[:, 64:64 + KD * HS].rearrange("p (k h) -> p k h", k=KD)
        sdown_w = gs[:, 64 + KD * HS:64 + KD * HS + MS * D].rearrange("p (m d) -> p m d", m=MS)
        wa = sb("wa", [P, KD, D])
        wx = sb("wx", [P, KD, D])
        qg_w = sh[:, 0:KD * HID].rearrange("p (k h) -> p k h", k=KD)
        qu_w = sh[:, KD * HID:2 * KD * HID].rearrange("p (k h) -> p k h", k=KD)
        qd_w = sh[:, 2 * KD * HID:2 * KD * HID + NHID * D].rearrange("p (m d) -> p m d", m=NHID)
        wqkv = rt[:, 0:KD * 3 * D].rearrange("p (k h) -> p k h", k=KD)
        wout = rt[:, KD * 3 * D:KD * 4 * D].rearrange("p (k h) -> p k h", k=KD)

        ident = sb("ident", [P, P])
        identb = sb("identb", [P, P], BF16)
        earlier = sb("earlier", [P, P], BF16)
        ones = sb("ones", [P, P], BF16)
        hide_qk = sb("hide_qk", [P, P], BF16)
        hide_kq = sb("hide_kq", [P, P], BF16)
        iota_a = sb("iota_a", [P, SLOT_A, E], F16)
        iota_b = sb("iota_b", [P, SLOT_B, E], F16)
        token_id = sb("token_id", [P, NT, E], F16)
        own_expert = sb("own_expert", [P, EH])
        row_base = sb("row_base", [P, E])
        minus_half = sb("minus_half", [P, TH])
        bias_corr = sb("bias_corr", [P, E])
        v_bias = sb("v_bias", [P, D])
        out_bias = sb("out_bias", [P, D])
        sd_row = sb("sd_row", [P, D])
        qk_bias = sb("qk_bias", [P, 2, KD])
        sg_col = sb("sg_col", [P, NHID])
        su_col = sb("su_col", [P, NHID])
        sg_half = sb("sg_half", [P, NHID])
        sgu_half = sb("sgu_half", [P, NHID])
        rec_in = sb("rec_in", [P, 3, KD])
        lam = sb("lam", [P, 12, KD])

        stats = sb("stats", [P, NT, 6])
        mv = sb("mv", [P, NT, 2])
        veps = sb("veps", [P, NT])
        rstd = sb("rstd", [P, NT])

        def rt_view(lo, n):
            return rt[:, lo:lo + n]

        scores = rt_view(0, 256).rearrange("p (j e) -> p j e", j=NT)
        corrected = rt_view(256, 256).rearrange("p (j e) -> p j e", j=NT)
        hi = rt_view(512, 128)
        lo = rt_view(640, 128)
        m1 = rt_view(768, 64)
        mh = rt_view(832, 64)
        ml = rt_view(896, 64)
        gscore = rt_view(960, NT * 12).rearrange("p (j g) -> p j g", j=NT)
        gpick = rt_view(1056, NT * 12).rearrange("p (j g) -> p j g", j=NT)
        top8 = rt_view(1152, 64).rearrange("p (j g) -> p j g", j=NT)
        gmask = rt_view(1216, 64).rearrange("p (j g) -> p j g", j=NT)
        masked = rt_view(1280, NT * 36).rearrange("p (j g) -> p j g", j=NT)
        epick = rt_view(1568, NT * 36).rearrange("p (j g) -> p j g", j=NT)
        used = rt_view(1856, 256).rearrange("p (j e) -> p j e", j=NT)
        wsum = rt_view(2112, 8)
        wrec = rt_view(2120, 8)
        weight = rt_view(2128, 256).rearrange("p (j e) -> p j e", j=NT)
        slot = rt_view(2384, 256).rearrange("p (j e) -> p j e", j=NT)
        slot_i = rt_view(2640, 256).bitcast(I32)
        slot_a = rt_view(2896, 128).bitcast(F16).rearrange("p (j e) -> p j e", j=NT)
        slot_b = rt_view(3024, 128).bitcast(F16).rearrange("p (j e) -> p j e", j=NT)
        part_i = rt_view(3152, 256).bitcast(I32)
        row_code = rt_view(3408, 256).rearrange("p (j e) -> p j e", j=NT)
        used_b = rt_view(3664, 128).bitcast(BF16).rearrange("p (j e) -> p j e", j=NT)
        from_token = rt_view(3792, 32).bitcast(I32)
        ye_row = rt_view(3824, 32).bitcast(I32)
        kweight = rt_view(3856, 32)
        is_a = xt[:, 0:1024].bitcast(F16).rearrange("p (h j a e) -> p h j a e", h=2, j=NT, a=SLOT_A)
        is_b = xt[:, 1024:3072].bitcast(F16).rearrange("p (j b e) -> p j b e", j=NT, b=SLOT_B)
        inv = xt[:, 3072:3584].rearrange("p (h b e) -> p h b e", h=2, b=SLOT_B)
        inv_sum = xt[:, 3584:3616]
        ksel = xt[:, 4096:5120].rearrange("p (j k e) -> p j k e", j=NT, k=TOPK)
        xeT = [xt[:, h * 4096:(h + 1) * 4096].rearrange("p (k e b a) -> p k e b a", k=KD, e=EH, b=SLOT_B)
               for h in range(2)]
        picked = xt[:, :].rearrange("p (j k d) -> p j k d", j=NT, k=TOPK)
        RING_XE = 8
        xe = rg[:, 0:2048].rearrange("p (r d) -> p r d", r=RING_XE)
        relu_e = rg[:, 2048:3072].rearrange("p (r c) -> p r c", r=2)
        hid_e = rg[:, 3072:4096].rearrange("p (r c) -> p r c", r=2)
        ye = rg[:, 4096:6144].rearrange("p (r e d) -> p r e d", r=2, e=4)
        relu_s = sb("relu_s", [P, 2, SEQ])
        hid_s = sh[:, 0:MS * T].rearrange("p (m t) -> p m t", m=MS)

        decay = rg[:, 0:2048].rearrange("p (m t) -> p m t", m=KD)
        drive = rg[:, 2048:4096].rearrange("p (m t) -> p m t", m=KD)
        state = rg[:, 4096:6144].rearrange("p (m t) -> p m t", m=KD)

        tanh_q = relu_s
        gated = rg[:, 0:1024].rearrange("p (r t) -> p r t", r=2)
        hid_q = big[:, 0, 0:NHID * T].rearrange("p (m t) -> p m t", m=NHID)
        scaled = gs[:, 0:512].rearrange("p (j d) -> p j d", j=2)

        MAX_UNITS = [(qt, h0, n) for qt, n in ((3, 2), (2, 2), (1, 4), (0, 8)) for h0 in range(0, NH, n)]
        Q, K = 0, 1
        stack = [big[:, i, :].bitcast(BF16).rearrange("p (h t) -> p h t", h=NH) for i in range(2)]
        SLOTS = [[0, 1, 2, 0, 1, 0], [0, 0, 0, 1, 1, 2]]
        KS = len(SLOTS[0]) * HD
        parts = [xt[:, i * 3072:(i + 1) * 3072].bitcast(BF16)
                 .rearrange("p (m s t) -> p m s t", m=KD, s=3) for i in range(2)]
        qk_f = rt[:, 2048:4096].rearrange("p (r t) -> p r t", r=4)
        VW = HD + 1
        val = gs[:, 0:NT * NH * VW].rearrange("p (j h c) -> p j h c", j=NT, h=NH)
        smax = sb("smax", [P, NB, TH, NH])
        smax_r = sb("smax_r", [P, TH, NH])
        smax_p = sb("smax_p", [P, NB, TH, 3, NH], BF16)
        smax_t = sb("smax_t", [3 * NH, NB, SEQ], BF16)
        prob = rg[:, 0:5120].rearrange("p (r s t) -> p r s t", r=2, s=5)
        den = sb("den", [P, 2, TH, 2])
        ctx_n = xn

        xn_dram = [nc.dram_tensor(f"xn_dram{i}", [T, D], F32).ap() for i in range(2)]
        ye_dram = [nc.dram_tensor(f"ye_dram{i}", [E * CAP, D], F32).ap() for i in range(2)]
        part_dram = nc.dram_tensor("part_dram", [2, 3, NH, HD, T], BF16).ap()
        smax_dram = nc.dram_tensor("smax_dram", [NB, 3 * NH, SEQ], BF16).ap()

        ps = ctx.enter_context(nc.psum_tensor("ps", [P, 8, 512], F32))

        out_v = a["out"].rearrange("b (j p) d -> p (b j) d", p=P)
        x_v = a["x"].rearrange("b (j p) d -> p (b j) d", p=P)

        moe_at = {0: 0, 2: 1}


        def xeT_src(u, k):
            return ps[:, u % 2, :].rearrange("p (b k a e) -> p b k a e", b=2, k=KD, a=SLOT_A)[:, :, k, :, :]

        def xeT_dst(u, k):
            h, q = divmod(u, 8)
            return xeT[h][:, k, :, 2 * q:2 * q + 2, :].rearrange("p e b a -> p b a e")

        def max_view(u, qt):
            two = ps[:, 2 * (u % 2):2 * (u % 2) + 2, :]
            if qt == 2:
                return two[:, :, 0:3 * P]
            return two.rearrange("p b c -> p (b c)").rearrange("p (h w) -> p h w", w=(qt + 1) * P)

        smax_bank = ps[0:3 * NH, 7, 0:SEQ // 2].bitcast(BF16)
        PIECES = [[(0, 0, 0)], [(0, 1, 0), (0, 3, 384)], [(0, 2, 0), (1, 2, 256)],
                  [(1, 0, 0)], [(1, 1, 0), (1, 3, 384)]]
        PLACE = {(hh, kt): (c, col) for c, piece in enumerate(PIECES) for hh, kt, col in piece}

        block = ctx.enter_context(nc.Block())

        @block.sync
        def _(sp):
            for j in range(NT):
                sp.dma_start(x[:, j, :], x_v[:, j, :]).then_inc(*mark16(f"x_in{j}"))
            sp.dma_start(gate_w, a["gate"]).then_inc(*mark16("gate_in"))
            sp.dma_start(bias_corr[:], a["bias_corr"].partition_broadcast(P)).then_inc(*mark16("bias_in"))
            sp.dma_start(sup_w, a["sup"]).then_inc(*mark16("sup_in"))
            sp.dma_start(sdown_w, a["sdown"]).then_inc(*mark16("sdown_in"))
            for i, name in enumerate(("ba", "bx", "lam")):
                sp.dma_start(rec_in[:, i, :], a[name]).then_inc(*mark16("rec_in"))
            for q in range(4):
                sp.dma_start(up_w[:, :, 8 * q:8 * q + 8, :], a["up"][:, :, 8 * q:8 * q + 8, :])\
                    .then_inc(*mark16(f"up_in{q}"))
                sp.dma_start(down_w[:, 8 * q:8 * q + 8, :], a["down"][:, 8 * q:8 * q + 8, :])\
                    .then_inc(*mark16(f"down_in{q}"))
            sp.dma_start(wa[:], a["wa"]).then_inc(*mark16("wa_in"))
            sp.dma_start(wx[:], a["wx"]).then_inc(*mark16("wx_in"))
            for w, name in ((v_bias, "bv"), (out_bias, "bout"), (sd_row, "s_down")):
                sp.dma_start(w[:], a[name].partition_broadcast(P)).then_inc(*mark16("rows_in"))
            for i, name in enumerate(("bq", "bk")):
                sp.dma_start(qk_bias[:, i, :], a[name]).then_inc(*mark16("qkb_in"))
            for m, (r0, n) in enumerate(zip(HID_AT, HID_TILES)):
                sp.dma_start(sg_col[0:n, m:m + 1], a["s_gate"][r0:r0 + n, :]).then_inc(*mark16("scol_in"))
                sp.dma_start(su_col[0:n, m:m + 1], a["s_up"][r0:r0 + n, :]).then_inc(*mark16("scol_in"))

            def expert_stores(n):
                f = moe_at[n]
                xn_rows = xn_dram[f].rearrange("(j p) d -> p j d", p=P)
                for h in range(NB):
                    sp.wait_ge(*at("xn", n, TH * h + TH - 1))
                    sp.dma_start(xn_rows[:, TH * h:TH * h + TH, :], xn[:, TH * h:TH * h + TH, :])\
                        .then_inc(*mark16(f"xn_out{h}", n))
                if n == 2:
                    sp.wait_ge(*at("shared_out", 2, NT // 2 - 1))
                    sp.dma_start(qg_w.bitcast(I32), a["wq_gate"]).then_inc(*mark16("qg_in"))
                    sp.dma_start(qu_w.bitcast(I32), a["wq_up"]).then_inc(*mark16("qu_in"))
                    for m, (r0, w) in enumerate(zip(HID_AT, HID_TILES)):
                        sp.dma_start(qd_w[0:w, m, :].bitcast(I32), a["wq_down"][r0:r0 + w, :])\
                            .then_inc(*mark16("qd_in"))
                ye_rows = ye_dram[f].rearrange("(e c) d -> c e d", c=CAP)
                for g in range(E // 4):
                    sp.wait_ge(*at("ye", n, g, 1))
                    sp.dma_start(ye_rows[:, 4 * g:4 * g + 4, :], ye[:, g % 2, :, :])\
                        .then_inc(*mark16(f"ye_out{g % 2}", n, g))

            expert_stores(0)
            expert_stores(2)
            sp.wait_ge(*at("x", 3, NT - 1))
            sp.dma_start(wqkv, a["wqkv"]).then_inc(*mark16("wqkv_in"))
            sp.dma_start(wout, a["wout"]).then_inc(*mark16("wout_in"))

            for b in range(NB):
                tok = slice(b * SEQ, (b + 1) * SEQ)
                for i in (Q, K):
                    for m in range(KD):
                        sp.wait_ge(*at("qk_parts", (b * 2 + i) * KD + m))
                        dst = part_dram[i, :, 8 * m:8 * m + 8, :, tok].rearrange("s h r t -> (h r) s t")
                        sp.dma_start(dst, parts[i][:, m, :, tok]).then_inc(*mark16(f"part_out{b}{i}"))
                for i in (Q, K):
                    sp.wait_ge(*at(f"part_out{b}{i}"))
                    if b == 0:
                        sp.wait_ge(*at("x", 4, NT - 1))
                    for s, which in enumerate(SLOTS[i]):
                        sp.dma_start(stack[i][s * HD:(s + 1) * HD, :, tok],
                                     part_dram[i, which, :, :, tok].rearrange("h r t -> r h t"))\
                            .then_inc(*mark16(f"stack_in{b}{i}"))
            for b in range(NB):
                sp.wait_ge(*at("smax_t", b))
                sp.dma_start(smax_dram[b], smax_t[:, b, :]).then_inc(*mark16(f"smax_out{b}"))
                sp.wait_ge(*at(f"smax_out{b}"))
                sp.dma_start(stack[Q][KS:KS + 3, :, b * SEQ:(b + 1) * SEQ],
                             smax_dram[b].rearrange("(s h) t -> s h t", s=3)).then_inc(*mark16(f"smax_in{b}"))

            for j in range(NT):
                sp.wait_ge(*at("x", LAST, j))
                sp.dma_start(out_v[:, j, :], x[:, j, :]).then_inc(*mark16("out"))
            sp.wait_ge(*at("out"))

        @block.gpsimd
        def _(pool):
            g = nc.gpsimd

            def triangle(dst, cmp, mult, step, fill):
                g.affine_select(out=dst, in_=dst, compare_op=cmp, fill=fill, base=0,
                                pattern=[[step, P]], channel_multiplier=mult).then_inc(*mark("const"))

            g.memset(ident[:], 0.0).then_inc(*mark("cleared"))
            g.memset(identb[:], 0.0).then_inc(*mark("cleared"))
            g.memset(earlier[:], 1.0).then_inc(*mark("cleared"))
            g.memset(hide_qk[:], 0.0).then_inc(*mark("cleared"))
            g.memset(hide_kq[:], 0.0).then_inc(*mark("cleared"))
            g.memset(own_expert[:], 0.0).then_inc(*mark("cleared"))
            g.memset(minus_half[:], -0.5).then_inc(*mark("cleared"))
            g.memset(ones[:], 1.0).then_inc(*mark("const"))
            pool.wait_ge(*at("cleared"))
            triangle(ident[:], ALU.not_equal, 1, -1, 1.0)
            g.affine_select(out=identb[:], in_=identb[:], compare_op=ALU.not_equal, fill=1.0, base=0,
                            pattern=[[-1, P]], channel_multiplier=1).then_inc(*mark("const", "ident"))
            triangle(earlier[:], ALU.is_gt, -1, 1, 0.0)
            triangle(hide_qk[:], ALU.is_ge, 1, -1, MASKED)
            triangle(hide_kq[:], ALU.is_ge, -1, 1, MASKED)
            own = own_expert[:]
            for r in range(P // EH):
                g.affine_select(out=own, in_=own, compare_op=ALU.not_equal, fill=1.0, base=-EH * r,
                                pattern=[[-1, EH]], channel_multiplier=1).then_inc(*mark("own", r))
                pool.wait_ge(*at("own", r))
            g.iota(iota_a[:], pattern=[[1, SLOT_A], [0, E]], base=0, channel_multiplier=0,
                   allow_small_or_imprecise_dtypes=True).then_inc(*mark("const"))
            g.iota(iota_b[:], pattern=[[1, SLOT_B], [0, E]], base=0, channel_multiplier=0,
                   allow_small_or_imprecise_dtypes=True).then_inc(*mark("const"))
            g.iota(token_id[:], pattern=[[P, NT], [0, E]], base=0, channel_multiplier=1,
                   allow_small_or_imprecise_dtypes=True).then_inc(*mark("const"))
            g.iota(row_base[:], pattern=[[-CAP, E]], base=E * CAP, channel_multiplier=0,
                   allow_small_or_imprecise_dtypes=True).then_inc(*mark("const"))

            def rstd_half(n, h):
                pool.wait_ge(*at("veps", n, h))
                g.tensor_tensor(rstd[:, TH * h:TH * h + TH], veps[:, TH * h:TH * h + TH], minus_half[:],
                                ALU.pow).then_inc(*mark("rstd", n, h))

            def square_shared(n):
                for u in range(NB * MS):
                    h, m = divmod(u, MS)
                    pool.wait_ge(*at("relu_s", n, u))
                    r = relu_s[:, u % 2, :]
                    g.tensor_tensor(hid_s[:, m, h * SEQ:(h + 1) * SEQ], r, r, ALU.mult)\
                        .then_inc(*mark("hid_s", n, u))

            def gathers(n):
                f = moe_at[n]
                pool.wait_ge(*at("from_token", n))
                for h in range(NB):
                    pool.wait_ge(*at(f"xn_out{h}", n))
                for u in range(2 * SLOT_B):
                    if u >= RING_XE:
                        pool.wait_ge(*at("xe_t", n, (u - RING_XE) // 2))
                    elif n == 2:
                        pool.wait_ge(*at("state", NB * KD - 1))
                    g.indirect_dma_start(xe[:, u % RING_XE, :], None, xn_dram[f][:, :],
                                         bass.IndirectOffsetOnAxis(ap=from_token[:, u:u + 1], axis=0))\
                        .then_inc(*mark16(f"xe{u % RING_XE}", n, u))
                for g8 in range(E // 4 - 2, E // 4):
                    pool.wait_ge(*at(f"ye_out{g8 % 2}", n, g8))
                pool.wait_ge(*at("up_e", n, E // 4 - 1))
                pool.wait_ge(*at("kweight", n))
                for j in range(NT):
                    for k in range(TOPK):
                        i = j * TOPK + k
                        g.indirect_dma_start(picked[:, j, k, :], None, ye_dram[f][:, :],
                                             bass.IndirectOffsetOnAxis(ap=ye_row[:, i:i + 1], axis=0))\
                            .then_inc(*mark16(f"picked{j}", n))
                    if j == NT - 3:
                        rstd_half(n + 1, 0)

            rstd_half(0, 0)
            rstd_half(0, 1)
            square_shared(0)
            gathers(0)
            rstd_half(1, 1)
            rstd_half(2, 0)
            rstd_half(2, 1)
            square_shared(2)
            gathers(2)
            rstd_half(3, 1)
            pool.wait_ge(*at("down_e", 2, E // 2 - 1))
            pool.wait_ge(*at("rstd", 3, 1))
            g.memset(stack[K][KS:KS + 3, :, :], 1.0).then_inc(*mark("k_ones"))
            pool.wait_ge(*at("k_ones"))
            rstd_half(4, 0)
            rstd_half(4, 1)
            pool.wait_ge(*at("rows_in"))
            for j in range(NT):
                pool.wait_ge(*at("xn", 4, j))
                g.tensor_tensor(x[:, j, :], x[:, j, :], out_bias[:], ALU.add).then_inc(*mark("x_bias", j))
            rstd_half(5, 0)
            rstd_half(5, 1)

        @block.scalar
        def _(act):
            s = nc.scalar

            def evac_xnT(n):
                for u in range(NT // 2):
                    act.wait_ge(*at("tr", n, u))
                    src = ps[:, u % 2, :].rearrange("p (k t) -> p k t", k=KD)
                    s.activation(xnT[:, :, u * 256:(u + 1) * 256], src, ACT.Copy).then_inc(*mark("xnT", n, u))

            def evac_ye(n, g):
                for q in range(2):
                    u = 2 * g + q
                    act.wait_ge(*at("down_e", n, u))
                    if g >= 2:
                        act.wait_ge(*at(f"ye_out{g % 2}", n, g - 2))
                    s.activation(ye[:, g % 2, 2 * q:2 * q + 2, :],
                                 ps[:, 5 + u % 3, :].rearrange("p (e d) -> p e d", e=2), ACT.Copy)\
                        .then_inc(*mark("ye", n, g, q))

            def expert_layer(n):
                evac_xnT(n)
                act.wait_ge(*at("logits", n))
                s.activation(scores, ps[:, 2, 0:NT * E].rearrange("p (j e) -> p j e", j=NT), ACT.Tanh,
                             scale=0.5).then_inc(*mark("tanh_s", n))
                for u in range(NB * MS):
                    act.wait_ge(*at("up_s", n, u))
                    if u >= 2:
                        act.wait_ge(*at("hid_s", n, u - 2))
                    s.activation(relu_s[:, u % 2, :], ps[:, 3 + u % 3, :], ACT.Relu)\
                        .then_inc(*mark("relu_s", n, u))
                for h in range(2):
                    if h == 1:
                        act.wait_ge(*at("kweight", n))
                    for u in range(8 * h, 8 * h + 8, 2):
                        act.wait_ge(*at("xe_t", n, u))
                        for k in range(KD):
                            s.activation(xeT_dst(u, k), xeT_src(u, k), ACT.Copy)\
                                .then_inc(*mark("xeT_act", n, u, k))
                    for g in range(4 * h, 4 * h + 4):
                        act.wait_ge(*at("up_e", n, g))
                        if g >= 2:
                            act.wait_ge(*at("hid_e", n, g - 2))
                        s.activation(relu_e[:, g % 2, :], ps[:, 3 + g % 2, :], ACT.Relu)\
                            .then_inc(*mark("relu_e", n, g))
                        if g > 4 * h:
                            evac_ye(n, g - 1)
                    evac_ye(n, 4 * h + 3)

            act.wait_ge(*at("rec_in"))
            s.activation(lam[:, 0, :], rec_in[:, 2, :], ACT.Abs).then_inc(*mark("lam_act", 0))
            act.wait_ge(*at("lam_act", 0))
            s.activation(lam[:, 1, :], lam[:, 0, :], ACT.Exp, scale=-1.0).then_inc(*mark("lam_act", 1))
            s.activation(lam[:, 2, :], rec_in[:, 2, :], ACT.Relu, scale=-1.0).then_inc(*mark("lam_act", 2))

            expert_layer(0)

            evac_xnT(1)
            act.wait_ge(*at("rec_vec"))
            for g8 in range(E // 4 - 2, E // 4):
                act.wait_ge(*at(f"ye_out{g8 % 2}", 0, g8))
            for u in range(NB * KD):
                b, m = divmod(u, KD)
                tok = slice(b * SEQ, (b + 1) * SEQ)
                act.wait_ge(*at("proj_r", u))
                s.activation(decay[:, m, tok], ps[:, 2 + 2 * (u % 2), :], ACT.Tanh, scale=0.5,
                             bias=lam[:, 8, m:m + 1]).then_inc(*mark("tanh_r", u))
                act.wait_ge(*at("proj_i", u))
                s.activation(drive[:, m, tok], ps[:, 3 + 2 * (u % 2), :], ACT.Tanh, scale=0.5,
                             bias=lam[:, 9, m:m + 1]).then_inc(*mark("tanh_i", u))
                act.wait_ge(*at("tanh_r", u))
                s.activation(decay[:, m, tok], decay[:, m, tok], ACT.Exp, scale=lam[:, 10, m:m + 1],
                             bias=lam[:, 10, m:m + 1]).then_inc(*mark("decay", u))
                act.wait_ge(*at("decay", u))
                s.activation(state[:, m, tok], decay[:, m, tok], ACT.Square).then_inc(*mark("decay2", u))
            for u in range(NB * KD):
                b, m = divmod(u, KD)
                tok = slice(b * SEQ, (b + 1) * SEQ)
                act.wait_ge(*at("decay2", u))
                s.activation(state[:, m, tok], state[:, m, tok], ACT.Sqrt, scale=-1.0, bias=1.0)\
                    .then_inc(*mark("gain", u))

            expert_layer(2)

            def quantised(n):
                evac_xnT(n)
                act.wait_ge(*at("scol"))
                for u in range(NB * NHID):
                    m = u % NHID
                    w = HID_TILES[m]
                    act.wait_ge(*at("q_gate", n, u))
                    if u >= 2:
                        act.wait_ge(*at("gated", n, u - 2))
                    s.activation(tanh_q[0:w, u % 2, :], ps[0:w, 2 + 2 * (u % 2), :], ACT.Tanh,
                                 scale=sg_half[0:w, m:m + 1]).then_inc(*mark("tanh_q", n, u))

            quantised(3)

            evac_xnT(4)
            act.wait_ge(*at("qkb"))
            for u in range(NB * 2 * KD):
                b, i, m = u // 4, u // 2 % 2, u % 2
                act.wait_ge(*at("proj_qk", u))
                if u >= 4:
                    act.wait_ge(*at("qk_parts", u - 4))
                s.activation(qk_f[:, u % 4, :], ps[:, 2 + u % 2, :], ACT.Identity,
                             scale=(0.25 if i == Q else 1.0), bias=qk_bias[:, i, m:m + 1])\
                    .then_inc(*mark("qk_f", u))
                act.wait_ge(*at("qk_f", u))
                s.activation(parts[i][:, m, 0, b * SEQ:(b + 1) * SEQ], qk_f[:, u % 4, :], ACT.Copy)\
                    .then_inc(*mark("qk_p0", u))
            for pair in range(NB * NH // 2):
                for c in range(5):
                    u = pair * 5 + c
                    act.wait_ge(*at("st", u))
                    if pair >= 2:
                        act.wait_ge(*at("pv", pair - 2))
                    s.activation(prob[:, pair % 2, c, :], ps[:, 4 + u % 3, :], ACT.Exp)\
                        .then_inc(*mark("prob", u))
            for u in range(NT // 2):
                act.wait_ge(*at("ctx_tr", u))
                src = ps[:, u % 2, :].rearrange("p (k t) -> p k t", k=KD)
                s.activation(xnT[:, :, u * 256:(u + 1) * 256], src, ACT.Copy).then_inc(*mark("ctxT", u))
            quantised(5)

        @block.vector
        def _(dve):
            v = nc.vector
            links = [0]

            def link(ins):
                links[0] += 1
                ins.then_inc(*mark("dve_step"))
                dve.wait_ge(counts.sem("dve_step"), links[0])

            def ln_stats(n, h):
                for j in range(TH * h, TH * h + TH):
                    dve.wait_ge(*(at("x", n, j) if n else at(f"x_in{j}")))
                    last = v.bn_stats(stats[:, j, :], x[:, j, :])
                link(last)
                for j in range(TH * h, TH * h + TH):
                    last = v.bn_aggr(mv[:, j, :], stats[:, j, :])
                link(last)
                half = slice(TH * h, TH * h + TH)
                v.tensor_scalar(veps[:, half], mv[:, half, 1], EPS, None, ALU.add).then_inc(*mark("veps", n, h))

            def ln_norm(n, h):
                dve.wait_ge(*at("rstd", n, h))
                if n - 1 in moe_at:
                    dve.wait_ge(*at(f"xn_out{h}", n - 1))
                if n == 5:
                    dve.wait_ge(*at("ctx_tr", NT // 2 - 1))
                for j in range(TH * h, TH * h + TH):
                    v.tensor_scalar(xn[:, j, :], x[:, j, :], mv[:, j, 0:1], rstd[:, j:j + 1],
                                    ALU.subtract, ALU.mult).then_inc(*mark("xn", n, j))

            def halves(n, update):
                update(0)
                update(1)
                if n < LAST:
                    ln_stats(n, 0)
                update(2)
                if n < LAST:
                    ln_norm(n, 0)
                update(3)
                if n < LAST:
                    ln_stats(n, 1)
                    ln_norm(n, 1)

            def route(n):
                dve.wait_ge(*at("tanh_s", n))
                link(v.tensor_scalar(scores, scores, 0.5, 0.5, ALU.mult, ALU.add))
                dve.wait_ge(*at("bias_in"))
                link(v.tensor_tensor(corrected, scores, bias_corr[:].unsqueeze(1).to_broadcast([P, NT, E]), ALU.add))
                pairs = corrected.rearrange("p j (g q) -> p (j g) q", q=2)
                v.tensor_tensor(hi, pairs[:, :, 0], pairs[:, :, 1], ALU.max)
                link(v.tensor_tensor(lo, pairs[:, :, 0], pairs[:, :, 1], ALU.min))
                hi2 = hi.rearrange("p (g q) -> p g q", q=2)
                lo2 = lo.rearrange("p (g q) -> p g q", q=2)
                v.tensor_tensor(m1, hi2[:, :, 0], hi2[:, :, 1], ALU.max)
                v.tensor_tensor(mh, hi2[:, :, 0], hi2[:, :, 1], ALU.min)
                link(v.tensor_tensor(ml, lo2[:, :, 0], lo2[:, :, 1], ALU.max))
                link(v.tensor_tensor(mh, mh, ml, ALU.max))
                v.memset(gscore[:, :, EG:12], SENTINEL)
                link(v.tensor_tensor(gscore[:, :, 0:EG], m1.rearrange("p (j g) -> p j g", j=NT),
                                     mh.rearrange("p (j g) -> p j g", j=NT), ALU.add))
                for j in range(NT):
                    last = v.max(top8[:, j, :], gscore[:, j, 0:EG])
                link(last)
                link(v.memset(top8[:, :, TOPK:8], SENTINEL))
                for j in range(NT):
                    last = v.match_replace(gpick[:, j, :], top8[:, j, :], gscore[:, j, :], PICKED)
                link(last)
                link(v.tensor_scalar(gmask, gpick[:, :, 0:EG], PICKED, None, ALU.is_equal))
                v.memset(masked[:, :, E:36], SENTINEL)
                link(v.tensor_tensor(masked[:, :, 0:E].rearrange("p j (g q) -> p j g q", q=EPG),
                                     corrected.rearrange("p j (g q) -> p j g q", q=EPG),
                                     gmask.unsqueeze(3).to_broadcast([P, NT, EG, EPG]), ALU.mult))
                for j in range(NT):
                    last = v.max(top8[:, j, :], masked[:, j, 0:E])
                link(last)
                link(v.memset(top8[:, :, TOPK:8], SENTINEL))
                for j in range(NT):
                    last = v.match_replace(epick[:, j, :], top8[:, j, :], masked[:, j, :], PICKED)
                link(last)
                v.tensor_scalar(used_b, epick[:, :, 0:E], PICKED, None, ALU.is_equal).then_inc(*mark("used_b", n))
                link(v.tensor_scalar(used, epick[:, :, 0:E], PICKED, None, ALU.is_equal))
                link(v.tensor_tensor(weight, used, scores, ALU.mult))
                link(v.tensor_reduce(wsum, weight, AX.X, ALU.add))
                link(v.tensor_scalar(wsum, wsum, 1e-20, None, ALU.add))
                link(v.reciprocal(wrec, wsum))
                link(v.tensor_scalar(wrec, wrec, 0.5 * SCALE, None, ALU.mult))
                v.tensor_tensor(weight, weight, wrec.unsqueeze(2).to_broadcast([P, NT, E]), ALU.mult)
                link(v.tensor_scalar(row_code, used, -FAR, FAR, ALU.mult, ALU.add))
                dve.wait_ge(*at("pos", n))
                v.tensor_tensor(slot, ps[:, 2, 0:NT * E].rearrange("p (j e) -> p j e", j=NT), row_code, ALU.add)\
                    .then_inc(*mark("slot", n))
                dve.wait_ge(*at("slot", n))
                link(v.tensor_copy(slot_i, slot.rearrange("p j e -> p (j e)")))
                link(v.tensor_scalar(part_i, slot_i, SLOT_A - 1, None, ALU.bitwise_and))
                v.tensor_copy(slot_a, part_i.rearrange("p (j e) -> p j e", j=NT))
                link(v.tensor_scalar(slot_i, slot_i, 3, None, ALU.logical_shift_right))
                link(v.tensor_copy(slot_b, slot_i.rearrange("p (j e) -> p j e", j=NT)))
                for h in range(2):
                    own = slice(EH * h, EH * (h + 1))
                    shape = [P, NT, SLOT_A, EH]
                    link(v.tensor_tensor(is_a[:, h], slot_a[:, :, own].unsqueeze(2).to_broadcast(shape),
                                         iota_a[:, :, own].unsqueeze(1).to_broadcast(shape), ALU.is_equal))
                    v.tensor_tensor(is_a[:, h], is_a[:, h], token_id[:, :, own].unsqueeze(2).to_broadcast(shape),
                                    ALU.mult)
                v.tensor_tensor(is_b, slot_b.unsqueeze(2).to_broadcast([P, NT, SLOT_B, E]),
                                iota_b[:].unsqueeze(1).to_broadcast([P, NT, SLOT_B, E]), ALU.is_equal)\
                    .then_inc(*mark("onehot", n))
                link(v.tensor_scalar(row_code, slot, CAP - 1.0, None, ALU.min))
                link(v.tensor_tensor(row_code, row_base[:].unsqueeze(1).to_broadcast([P, NT, E]), row_code,
                                     ALU.subtract))
                link(v.tensor_tensor(row_code, row_code, used, ALU.mult))
                for j in range(NT):
                    last = v.max(top8[:, j, :], row_code[:, j, :])
                link(last)
                link(v.tensor_scalar(slot, slot, float(CAP), None, ALU.is_lt))
                link(v.tensor_tensor(weight, weight, slot, ALU.mult))
                dve.wait_ge(*at("inv_mm", n))
                v.tensor_tensor(inv.rearrange("p h b e -> p (h b) e"),
                                ps[:, 2, :].rearrange("p (hb e) -> p hb e", e=EH),
                                own_expert[:].unsqueeze(1).to_broadcast([P, 2 * SLOT_B, EH]), ALU.mult)\
                    .then_inc(*mark("inv", n))
                dve.wait_ge(*at("inv", n))
                link(v.tensor_reduce(inv_sum, inv.rearrange("p h b e -> p (h b) e"), AX.X, ALU.add))
                v.tensor_copy(from_token, inv_sum).then_inc(*mark("from_token", n))
                v.tensor_scalar(ye_row.rearrange("p (j k) -> p j k", j=NT), top8[:, :, 0:TOPK], -1.0,
                                float(E * CAP), ALU.mult, ALU.add)
                link(v.tensor_tensor(ksel, row_code.unsqueeze(2).to_broadcast([P, NT, TOPK, E]),
                                     top8[:, :, 0:TOPK].unsqueeze(3).to_broadcast([P, NT, TOPK, E]), ALU.is_equal))
                link(v.tensor_tensor(ksel, ksel, weight.unsqueeze(2).to_broadcast([P, NT, TOPK, E]), ALU.mult))
                v.tensor_reduce(kweight.rearrange("p (j k) -> p j k", j=NT), ksel, AX.X, ALU.add)\
                    .then_inc(*mark("kweight", n))

            def expert_layer(n):
                route(n)
                for u in range(NT // 2):
                    dve.wait_ge(*at("down_s", n, u))
                    v.scalar_tensor_tensor(x[:, 2 * u:2 * u + 2, :],
                                           ps[:, 3 + (NB * MS + u) % 3, :].rearrange("p (j d) -> p j d", j=2),
                                           0.5, x[:, 2 * u:2 * u + 2, :], ALU.mult, ALU.add)\
                        .then_inc(*mark("shared_out", n, u))
                for h in range(2):
                    for u in range(8 * h + 1, 8 * h + 8, 2):
                        dve.wait_ge(*at("xe_t", n, u))
                        for k in range(KD):
                            v.tensor_copy(xeT_dst(u, k), xeT_src(u, k)).then_inc(*mark("xeT_dve", n, u, k))
                    for g in range(4 * h, 4 * h + 4):
                        dve.wait_ge(*at("relu_e", n, g))
                        if g >= 2:
                            dve.wait_ge(*at("down_e", n, 2 * (g - 2) + 1))
                        v.tensor_tensor(hid_e[:, g % 2, :], relu_e[:, g % 2, :], relu_e[:, g % 2, :], ALU.mult)\
                            .then_inc(*mark("hid_e", n, g))
                if n == 2:
                    quantised_weights()

                def combine(u):
                    for j in (2 * u, 2 * u + 1):
                        dve.wait_ge(*at(f"picked{j}", n))
                        if j == 0:
                            dve.wait_ge(*at("shared_out", n, NT // 2 - 1))
                            dve.wait_ge(*at("kweight", n))
                        for k in range(TOPK):
                            i = j * TOPK + k
                            last = v.scalar_tensor_tensor(x[:, j, :], picked[:, j, k, :], kweight[:, i:i + 1],
                                                          x[:, j, :], ALU.mult, ALU.add)
                            if k < TOPK - 1:
                                link(last)
                        last.then_inc(*mark("x", n + 1, j))

                halves(n + 1, combine)

            def quantised_weights():
                for name, w in (("qg_in", qg_w), ("qu_in", qu_w)):
                    dve.wait_ge(*at(name))
                    flat = w.rearrange("p k h -> p (k h)")
                    v.tensor_scalar(flat, flat.bitcast(I32), -ZERO_POINT, None, ALU.add).then_inc(*mark("q_weights"))
                dve.wait_ge(*at("qd_in"))
                for lo_, n_, w in ((0, 2, 128), (2, 4, 112)):
                    part = qd_w[0:w, lo_:lo_ + n_, :].rearrange("p m d -> p (m d)")
                    v.tensor_scalar(part, part.bitcast(I32), -ZERO_POINT, None, ALU.add).then_inc(*mark("q_weights"))

            dve.wait_ge(*at("rec_in"))
            v.tensor_scalar(lam[:, 8, :], rec_in[:, 0, :], 0.5, None, ALU.mult)
            v.tensor_scalar(lam[:, 9, :], rec_in[:, 1, :], 0.5, None, ALU.mult)
            dve.wait_ge(*at("lam_act", 2))
            link(v.tensor_scalar(lam[:, 3, :], lam[:, 1, :], 2.0, None, ALU.add))
            link(v.reciprocal(lam[:, 4, :], lam[:, 3, :]))
            link(v.tensor_tensor(lam[:, 5, :], lam[:, 1, :], lam[:, 4, :], ALU.mult))
            link(v.tensor_tensor(lam[:, 6, :], lam[:, 5, :], lam[:, 5, :], ALU.mult))
            link(v.tensor_scalar(lam[:, 7, :], lam[:, 6, :], 1.0 / 19.0, None, ALU.mult))
            for i in range(8, 0, -1):
                link(v.scalar_tensor_tensor(lam[:, 7, :], lam[:, 7, :], 1.0 / (2 * i + 1), lam[:, 6, :],
                                            ALU.add, ALU.mult))
            link(v.scalar_tensor_tensor(lam[:, 7, :], lam[:, 7, :], 1.0, lam[:, 5, :], ALU.add, ALU.mult))
            link(v.scalar_tensor_tensor(lam[:, 11, :], lam[:, 7, :], 2.0, lam[:, 2, :], ALU.mult, ALU.add))
            v.tensor_scalar(lam[:, 10, :], lam[:, 11, :], -4.0, None, ALU.mult).then_inc(*mark("rec_vec"))

            ln_stats(0, 0)
            ln_stats(0, 1)
            ln_norm(0, 0)
            ln_norm(0, 1)

            dve.wait_ge(*at("rows_in"))
            v.tensor_scalar(sd_row[:], sd_row[:], 0.5, None, ALU.mult)
            dve.wait_ge(*at("qkb_in"))
            v.tensor_scalar(qk_bias[:, 0, :], qk_bias[:, 0, :], 0.25, None, ALU.mult).then_inc(*mark("qkb"))
            dve.wait_ge(*at("scol_in"))
            for w, c0, c1 in ((128, 0, 2), (112, 2, NHID)):
                link(v.tensor_scalar(sg_half[0:w, c0:c1], sg_col[0:w, c0:c1], 0.5, None, ALU.mult))
                v.tensor_tensor(sgu_half[0:w, c0:c1], sg_half[0:w, c0:c1], su_col[0:w, c0:c1], ALU.mult)\
                    .then_inc(*mark("scol"))

            expert_layer(0)

            for u in range(NB * KD):
                b, m = divmod(u, KD)
                tok = slice(b * SEQ, (b + 1) * SEQ)
                dve.wait_ge(*at("tanh_i", u))
                v.scalar_tensor_tensor(drive[:, m, tok], drive[:, m, tok], 1.0, xnT[:, m, tok],
                                       ALU.add, ALU.mult).then_inc(*mark("drive0", u))

            def recur(q):
                b, half = divmod(q, 2)
                if half == 0:
                    for m in range(KD):
                        u = KD * b + m
                        tok = slice(b * SEQ, (b + 1) * SEQ)
                        dve.wait_ge(*at("gain", u))
                        dve.wait_ge(*at("drive0", u))
                        link(v.scalar_tensor_tensor(drive[:, m, tok], drive[:, m, tok], 0.5, state[:, m, tok],
                                                    ALU.mult, ALU.mult))
                        v.tensor_tensor_scan(state[:, m, tok], decay[:, m, tok], drive[:, m, tok], 0.0,
                                             ALU.mult, ALU.add).then_inc(*mark("state", u))
                dve.wait_ge(*at("state_t", q))
                for j in (2 * q, 2 * q + 1):
                    v.tensor_tensor(x[:, j, :], x[:, j, :], ps[:, 6 + q % 2, (j % 2) * D:(j % 2 + 1) * D], ALU.add)\
                        .then_inc(*mark("x", 2, j))

            halves(2, recur)

            expert_layer(2)

            def quantised(n):
                for b in range(NB):
                    for u in range(b * NHID, (b + 1) * NHID):
                        m = u % NHID
                        w = HID_TILES[m]
                        dve.wait_ge(*at("tanh_q", n, u))
                        v.scalar_tensor_tensor(gated[0:w, u % 2, :], tanh_q[0:w, u % 2, :], 1.0,
                                               ps[0:w, 2 + 2 * (u % 2), :], ALU.add, ALU.mult)\
                            .then_inc(*mark("gated", n, u))
                        dve.wait_ge(*at("q_up", n, u))
                        dve.wait_ge(*at("gated", n, u))
                        v.scalar_tensor_tensor(hid_q[0:w, m, b * SEQ:(b + 1) * SEQ], ps[0:w, 3 + 2 * (u % 2), :],
                                               sgu_half[0:w, m:m + 1], gated[0:w, u % 2, :],
                                               ALU.mult, ALU.mult).then_inc(*mark("hid_q", n, u))

                def update(q):
                    dve.wait_ge(*at("q_down", n, q))
                    if q:
                        dve.wait_ge(*at("x", n + 1, 2 * q - 1))
                    link(v.tensor_tensor(scaled, ps[:, 6 + q % 2, :].rearrange("p (j d) -> p j d", j=2),
                                         sd_row[:].unsqueeze(1).to_broadcast([P, 2, D]), ALU.mult))
                    for j in (2 * q, 2 * q + 1):
                        v.tensor_tensor(x[:, j, :], x[:, j, :], scaled[:, j % 2, :], ALU.add)\
                            .then_inc(*mark("x", n + 1, j))

                halves(n + 1, update)

            quantised(3)

            v.memset(val[:, :, :, HD:VW], 1.0).then_inc(*mark("val"))

            def split_qk(u):
                b, i, m = u // 4, u // 2 % 2, u % 2
                tok = slice(b * SEQ, (b + 1) * SEQ)
                f = qk_f[:, u % 4, :]
                dve.wait_ge(*at("qk_p0", u))
                link(v.tensor_tensor(f, f, parts[i][:, m, 0, tok], ALU.subtract))
                link(v.tensor_copy(parts[i][:, m, 1, tok], f))
                v.tensor_tensor(parts[i][:, m, 2, tok], f, parts[i][:, m, 1, tok], ALU.subtract)\
                    .then_inc(*mark("qk_parts", u))

            def values(w):
                dve.wait_ge(*at("proj_v", w))
                v.tensor_tensor(val[:, 2 * w:2 * w + 2, :, 0:HD],
                                ps[:, 6 + w % 2, :].rearrange("p (j h c) -> p j h c", j=2, h=NH),
                                v_bias[:].rearrange("p (h c) -> p h c", h=NH).unsqueeze(1)
                                .to_broadcast([P, 2, NH, HD]), ALU.add).then_inc(*mark("val", w))

            for b in range(NB):
                for u in range(4 * b, 4 * b + 4):
                    split_qk(u)
                values(2 * b)
                values(2 * b + 1)

            def maxima(b, i):
                qt, h0, k = MAX_UNITS[i]
                u = b * len(MAX_UNITS) + i
                dve.wait_ge(*at("s_max", u))
                v.tensor_reduce(smax[:, b, qt, h0:h0 + k], max_view(u, qt), AX.X, ALU.max)\
                    .then_inc(*mark("smax", u))

            def split_maxima(b):
                dve.wait_ge(*at("smax", (b + 1) * len(MAX_UNITS) - 1))
                link(v.tensor_scalar(smax_p[:, b, :, 0, :], smax[:, b, :, :], -1.0, None, ALU.mult))
                link(v.scalar_tensor_tensor(smax_r[:], smax[:, b, :, :], -1.0, smax_p[:, b, :, 0, :],
                                            ALU.mult, ALU.subtract))
                link(v.tensor_copy(smax_p[:, b, :, 1, :], smax_r[:]))
                v.tensor_tensor(smax_p[:, b, :, 2, :], smax_r[:], smax_p[:, b, :, 1, :], ALU.subtract)\
                    .then_inc(*mark("smax_p", b))
                dve.wait_ge(*at("smax_tr", b))
                v.tensor_copy(smax_t[:, b, :], smax_bank).then_inc(*mark("smax_t", b))

            def context(pair):
                b, p = divmod(pair, NH // 2)
                dve.wait_ge(*at("pv", pair))
                src = ps[:, 7, 0:TH * 2 * VW].rearrange("p (q h c) -> p q h c", q=TH, h=2)
                link(v.reciprocal(den[:, pair % 2, :, :], src[:, :, :, HD]))
                dst = ctx_n[:, TH * b:TH * b + TH, 2 * HD * p:2 * HD * (p + 1)]\
                    .rearrange("p q (h c) -> p q h c", h=2)
                v.tensor_tensor(dst, src[:, :, :, 0:HD],
                                den[:, pair % 2, :, :].unsqueeze(3).to_broadcast([P, TH, 2, HD]), ALU.mult)\
                    .then_inc(*mark("ctx", pair))

            for i in range(len(MAX_UNITS)):
                maxima(0, i)
            split_maxima(0)
            for p in range(NH // 2):
                if p:
                    context(p - 1)
                for i in range(3 * p, min(3 * p + 3, len(MAX_UNITS))):
                    maxima(1, i)
            context(NH // 2 - 1)
            split_maxima(1)
            for p in range(NH // 2, NH):
                context(p)

            def attended(q):
                dve.wait_ge(*at("attn_out", q))
                dve.wait_ge(*at("x_bias", NT - 1))
                for j in (2 * q, 2 * q + 1):
                    v.tensor_tensor(x[:, j, :], x[:, j, :], ps[:, 2 + q % 2, (j % 2) * D:(j % 2 + 1) * D], ALU.add)\
                        .then_inc(*mark("x", 5, j))

            halves(5, attended)
            quantised(5)

        @block.tensor
        def _(pe):
            t = nc.tensor
            reader = {}

            def take(bank, *read):
                if bank in reader:
                    pe.wait_ge(*at(*reader[bank]))
                reader[bank] = read

            def transposes(n):
                for u in range(NT // 2):
                    take(u % 2, "xnT", n, u)
                    for j in (2 * u, 2 * u + 1):
                        pe.wait_ge(*at("xn", n, j))
                        for k in range(KD):
                            last = t.transpose(ps[:, u % 2, k * 256 + (j % 2) * P:k * 256 + (j % 2 + 1) * P],
                                               xn[:, j, k * P:(k + 1) * P], ident[:])
                    last.then_inc(*mark("tr", n, u))

            def expert_layer(n):
                f = moe_at[n]
                if n == 0:
                    pe.wait_ge(*at("const", "ident"))
                transposes(n)
                pe.wait_ge(*at("gate_in"))
                take(2, "tanh_s", n)
                for j in range(NT):
                    pe.wait_ge(*at("xnT", n, j // 2))
                    for k in range(KD):
                        last = t.matmul(ps[:, 2, j * E:(j + 1) * E], xnT[:, k, j * P:(j + 1) * P], gate_w[:, k, :],
                                        start=(k == 0), stop=(k == KD - 1))
                last.then_inc(*mark("logits", n))

                def shared_up(u):
                    h, m = divmod(u, MS)
                    take(3 + u % 3, "relu_s", n, u)
                    for k in range(KD):
                        last = t.matmul(ps[:, 3 + u % 3, :], sup_w[:, k, m * P:(m + 1) * P],
                                        xnT[:, k, h * SEQ:(h + 1) * SEQ], start=(k == 0), stop=(k == KD - 1))
                    last.then_inc(*mark("up_s", n, u))

                pe.wait_ge(*at("sup_in"))
                for u in range(MS):
                    shared_up(u)
                pe.wait_ge(*at("const"))
                pe.wait_ge(*at("used_b", n))
                take(2, "slot", n)
                for j in range(NT):
                    for i in range(j):
                        t.matmul(ps[:, 2, j * E:(j + 1) * E], ones[:], used_b[:, i, :], start=(i == 0), stop=False)
                    last = t.matmul(ps[:, 2, j * E:(j + 1) * E], earlier[:], used_b[:, j, :],
                                    start=(j == 0), stop=True)
                last.then_inc(*mark("pos", n))
                for u in range(MS, NB * MS):
                    shared_up(u)
                pe.wait_ge(*at("onehot", n))
                take(2, "inv", n)
                for h in range(2):
                    own = slice(EH * h, EH * (h + 1))
                    for j in range(NT):
                        last = t.matmul(ps[:, 2, h * 256:(h + 1) * 256], is_a[:, h, j].rearrange("p a e -> p (a e)"), is_b[:, j, :, own],
                                        start=(j == 0), stop=(j == NT - 1))
                last.then_inc(*mark("inv_mm", n))
                pe.wait_ge(*at("sdown_in"))
                for u in range(NT // 2):
                    bank = 3 + (NB * MS + u) % 3
                    take(bank, "shared_out", n, u)
                    pe.wait_ge(*at("hid_s", n, NB * MS - 1 if u >= 2 else MS - 1))
                    for j in (2 * u, 2 * u + 1):
                        for m in range(MS):
                            last = t.matmul(ps[:, bank, (j % 2) * D:(j % 2 + 1) * D], hid_s[:, m, j * P:(j + 1) * P],
                                            sdown_w[:, m, :], start=(m == 0), stop=(m == MS - 1))
                    last.then_inc(*mark("down_s", n, u))

                def up(g):
                    take(3 + g % 2, "relu_e", n, g)
                    pe.wait_ge(*at(f"up_in{g // 2}"))
                    for e in range(4 * g, 4 * g + 4):
                        rhs = xeT[e // EH][:, :, e % EH, :, :].rearrange("p k b a -> p k (b a)")
                        for k in range(KD):
                            last = t.matmul(ps[:, 3 + g % 2, (e % 4) * CAP:(e % 4 + 1) * CAP], up_w[:, k, e, :],
                                            rhs[:, k, :], start=(k == 0), stop=(k == KD - 1))
                    last.then_inc(*mark("up_e", n, g))

                def down(g):
                    pe.wait_ge(*at("hid_e", n, g))
                    pe.wait_ge(*at(f"down_in{g // 2}"))
                    for q in range(2):
                        u = 2 * g + q
                        take(5 + u % 3, "ye", n, g, q)
                        for e in (4 * g + 2 * q, 4 * g + 2 * q + 1):
                            last = t.matmul(ps[:, 5 + u % 3, (e % 2) * D:(e % 2 + 1) * D],
                                            hid_e[:, g % 2, (e % 4) * CAP:(e % 4 + 1) * CAP], down_w[:, e, :],
                                            start=True, stop=True)
                        last.then_inc(*mark("down_e", n, u))

                for h in range(2):
                    for u in range(8 * h, 8 * h + 8):
                        take(u % 2, *(("xeT_dve" if u % 2 else "xeT_act"), n, u, KD - 1))
                        for g in (2 * u, 2 * u + 1):
                            pe.wait_ge(*at(f"xe{g % RING_XE}", n, g))
                            for k in range(KD):
                                c = (g % 2) * 256 + k * P
                                last = t.transpose(ps[:, u % 2, c:c + P], xe[:, g % RING_XE, k * P:(k + 1) * P],
                                                   ident[:])
                        last.then_inc(*mark("xe_t", n, u))
                    pe.wait_ge(*at("xeT_act", n, 8 * h + 6, KD - 1))
                    pe.wait_ge(*at("xeT_dve", n, 8 * h + 7, KD - 1))
                    for g in range(4 * h, 4 * h + 4):
                        up(g)
                        if g > 4 * h:
                            down(g - 1)
                    down(4 * h + 3)

            expert_layer(0)

            transposes(1)
            pe.wait_ge(*at("wa_in"))
            pe.wait_ge(*at("wx_in"))
            for u in range(NB * KD):
                b, m = divmod(u, KD)
                pe.wait_ge(*at("xnT", 1, 2 * b + 1))
                for w, name, bank, read in ((wa, "proj_r", 2 + 2 * (u % 2), "tanh_r"),
                                            (wx, "proj_i", 3 + 2 * (u % 2), "tanh_i")):
                    take(bank, read, u)
                    for k in range(KD):
                        last = t.matmul(ps[:, bank, :], w[:, k, m * P:(m + 1) * P], xnT[:, k, b * SEQ:(b + 1) * SEQ],
                                        start=(k == 0), stop=(k == KD - 1))
                    last.then_inc(*mark(name, u))
            for q in range(NT // 2):
                pe.wait_ge(*at("state", KD * (q // 2) + KD - 1))
                take(6 + q % 2, "x", 2, 2 * q + 1)
                for j in (2 * q, 2 * q + 1):
                    for m in range(KD):
                        c = (j % 2) * D + m * P
                        last = t.transpose(ps[:, 6 + q % 2, c:c + P], state[:, m, j * P:(j + 1) * P], ident[:])
                last.then_inc(*mark("state_t", q))

            expert_layer(2)

            def quantised(n):
                transposes(n)
                pe.wait_ge(*at("q_weights"))
                for b in range(NB):
                    pe.wait_ge(*at("xnT", n, 2 * b + 1))
                    for u in range(b * NHID, (b + 1) * NHID):
                        m = u % NHID
                        c, w = HID_AT[m], HID_TILES[m]
                        for wt, name, bank, read in ((qg_w, "q_gate", 2 + 2 * (u % 2), "gated"),
                                                     (qu_w, "q_up", 3 + 2 * (u % 2), "hid_q")):
                            take(bank, read, n, u)
                            for k in range(KD):
                                last = t.matmul(ps[0:w, bank, :], wt[:, k, c:c + w],
                                                xnT[:, k, b * SEQ:(b + 1) * SEQ],
                                                start=(k == 0), stop=(k == KD - 1))
                            last.then_inc(*mark(name, n, u))
                    for q in (2 * b, 2 * b + 1):
                        take(6 + q % 2, "x", n + 1, 2 * q + 1)
                        pe.wait_ge(*at("hid_q", n, (b + 1) * NHID - 1))
                        for j in (2 * q, 2 * q + 1):
                            for m, w in enumerate(HID_TILES):
                                last = t.matmul(ps[:, 6 + q % 2, (j % 2) * D:(j % 2 + 1) * D],
                                                hid_q[0:w, m, j * P:(j + 1) * P], qd_w[0:w, m, :],
                                                start=(m == 0), stop=(m == NHID - 1))
                        last.then_inc(*mark("q_down", n, q))

            quantised(3)

            transposes(4)
            pe.wait_ge(*at("wqkv_in"))
            for b in range(NB):
                pe.wait_ge(*at("xnT", 4, 2 * b + 1))
                for u in range(4 * b, 4 * b + 4):
                    i, m = u // 2 % 2, u % 2
                    take(2 + u % 2, "qk_f", u)
                    for k in range(KD):
                        c = i * D + m * P
                        last = t.matmul(ps[:, 2 + u % 2, :], wqkv[:, k, c:c + P], xnT[:, k, b * SEQ:(b + 1) * SEQ],
                                        start=(k == 0), stop=(k == KD - 1))
                    last.then_inc(*mark("proj_qk", u))
                for w in (2 * b, 2 * b + 1):
                    take(6 + w % 2, "val", w)
                    for j in (2 * w, 2 * w + 1):
                        for k in range(KD):
                            last = t.matmul(ps[:, 6 + w % 2, (j % 2) * D:(j % 2 + 1) * D],
                                            xnT[:, k, j * P:(j + 1) * P], wqkv[:, k, 2 * D:3 * D],
                                            start=(k == 0), stop=(k == KD - 1))
                    last.then_inc(*mark("proj_v", w))

            def scores_max(b, i):
                qt, h0, count = MAX_UNITS[i]
                u = b * len(MAX_UNITS) + i
                if i == 0:
                    pe.wait_ge(*at(f"stack_in{b}{Q}"))
                    pe.wait_ge(*at(f"stack_in{b}{K}"))
                first = 2 * (u % 2)
                take(first, "smax", u)
                take(first + 1, "smax", u)
                width = (qt + 1) * P
                per_bank = max(1, count // 2)
                q0 = b * SEQ + qt * P
                for c in range(count):
                    bank, col = first + c // per_bank, (c % per_bank) * width
                    t.matmul(ps[:, bank, col:col + width], stack[Q][0:KS, h0 + c, q0:q0 + P],
                             stack[K][0:KS, h0 + c, b * SEQ:b * SEQ + width], start=True, stop=False)
                    last = t.matmul(ps[:, bank, col + width - P:col + width], identb[:], hide_qk[:],
                                    start=False, stop=True)
                last.then_inc(*mark("s_max", u))

            def transpose_maxima(b):
                pe.wait_ge(*at("smax_p", b))
                take(7, "smax_t", b)
                for qt in range(TH):
                    last = t.transpose(smax_bank[:, qt * P:(qt + 1) * P],
                                       smax_p[:, b, qt, :, :].rearrange("p s h -> p (s h)"), identb[:])
                last.then_inc(*mark("smax_tr", b))

            def scores_exp(pair):
                b, p = divmod(pair, NH // 2)
                h = 2 * p
                if p == 0:
                    pe.wait_ge(*at(f"smax_in{b}"))
                    pe.wait_ge(*at("k_ones"))
                for c, pieces in enumerate(PIECES):
                    u = pair * 5 + c
                    bank = 4 + u % 3
                    take(bank, "prob", u)
                    for hh, kt, col in pieces:
                        k0 = b * SEQ + kt * P
                        width = SEQ - kt * P
                        t.matmul(ps[:, bank, col:col + width], stack[K][0:KS + 3, h + hh, k0:k0 + P],
                                 stack[Q][0:KS + 3, h + hh, k0:k0 + width], start=True, stop=False)
                        last = t.matmul(ps[:, bank, col:col + P], identb[:], hide_kq[:], start=False, stop=True)
                    last.then_inc(*mark("st", u))

            def weighted_values(pair):
                b, p = divmod(pair, NH // 2)
                pe.wait_ge(*at("prob", pair * 5 + 4))
                pe.wait_ge(*at("val", 2 * b + 1))
                take(7, "ctx", pair)
                for hh in range(2):
                    for qt in range(TH):
                        c = (qt * 2 + hh) * VW
                        for kt in range(qt + 1):
                            piece, col = PLACE[hh, kt]
                            at_q = col + (qt - kt) * P
                            last = t.matmul(ps[:, 7, c:c + VW], prob[:, pair % 2, piece, at_q:at_q + P],
                                            val[:, TH * b + kt, 2 * p + hh, :], start=(kt == 0), stop=(kt == qt))
                last.then_inc(*mark("pv", pair))

            for i in range(len(MAX_UNITS)):
                scores_max(0, i)
            transpose_maxima(0)
            for p in range(NH // 2):
                scores_exp(p)
                if p:
                    weighted_values(p - 1)
                for i in range(3 * p, min(3 * p + 3, len(MAX_UNITS))):
                    scores_max(1, i)
            weighted_values(NH // 2 - 1)
            transpose_maxima(1)
            for p in range(NH // 2, NH):
                scores_exp(p)
                if p > NH // 2:
                    weighted_values(p - 1)
            weighted_values(NH - 1)

            pe.wait_ge(*at("wout_in"))
            for u in range(NT // 2):
                take(u % 2, "ctxT", u)
                pe.wait_ge(*at("ctx", (u // 2 + 1) * (NH // 2) - 1))
                for j in (2 * u, 2 * u + 1):
                    for k in range(KD):
                        last = t.transpose(ps[:, u % 2, k * 256 + (j % 2) * P:k * 256 + (j % 2 + 1) * P],
                                           ctx_n[:, j, k * P:(k + 1) * P], ident[:])
                last.then_inc(*mark("ctx_tr", u))
            for q in range(NT // 2):
                take(2 + q % 2, "x", 5, 2 * q + 1)
                pe.wait_ge(*at("ctxT", q))
                for j in (2 * q, 2 * q + 1):
                    for k in range(KD):
                        last = t.matmul(ps[:, 2 + q % 2, (j % 2) * D:(j % 2 + 1) * D], xnT[:, k, j * P:(j + 1) * P],
                                        wout[:, k, :], start=(k == 0), stop=(k == KD - 1))
                last.then_inc(*mark("attn_out", q))

            quantised(5)


def _layouts(inputs):
    def rows(w, k):
        return w.reshape(k, P, *w.shape[1:]).swapaxes(0, 1)

    f = {k: np.asarray(v) for k, v in inputs.items()}
    wqkv = f["L1_attn_W_qkv"].reshape(D, NH, 3, HD).transpose(0, 2, 1, 3).reshape(D, 3 * D)
    bqkv = f["L1_attn_b_qkv"].reshape(NH, 3, HD).transpose(1, 0, 2).reshape(3, D)
    out = {
        "x": f["L0_attn_x"],
        "gate": rows(f["L0_ffn_gate_w"].T, KD),
        "bias_corr": f["L0_ffn_bias_corr"],
        "sup": rows(f["L0_ffn_shared_up_w"].T, KD),
        "sdown": rows(f["L0_ffn_shared_down_w"].T, MS),
        "up": rows(f["L0_ffn_up_w"].transpose(2, 0, 1), KD),
        "down": f["L0_ffn_down_w"].transpose(2, 0, 1),
        "wa": rows(f["L0_attn_Wa"].T, KD),
        "wx": rows(f["L0_attn_Wx"].T, KD),
        "ba": rows(f["L0_attn_ba"], KD),
        "bx": rows(f["L0_attn_bx"], KD),
        "lam": rows(f["L0_attn_Lam"], KD),
        "wqkv": rows(wqkv, KD),
        "bq": rows(bqkv[0], KD),
        "bk": rows(bqkv[1], KD),
        "bv": bqkv[2],
        "wout": rows(f["L1_attn_W_out"], KD),
        "bout": f["L1_attn_b_out"],
        "wq_gate": rows(f["L1_ffn_wq_gate"].T, KD),
        "wq_up": rows(f["L1_ffn_wq_up"].T, KD),
        "wq_down": f["L1_ffn_wq_down"].T,
        "s_gate": f["L1_ffn_s_gate"].reshape(HID, 1),
        "s_up": f["L1_ffn_s_up"].reshape(HID, 1),
        "s_down": f["L1_ffn_s_down"],
    }
    return {k: np.ascontiguousarray(v) for k, v in out.items()}


def kernel(**inputs):
    import concourse.bacc as bacc
    from concourse.bass_utils import run_bass_kernel_spmd

    arrays = _layouts(inputs)
    counts = Counts()
    for _ in range(2):
        nc = bacc.Bacc("TRN2", target_bir_lowering=False, num_devices=1)
        args = {k: nc.dram_tensor(f"in_{k}", v.shape, mybir.dt.from_np(v.dtype), kind="ExternalInput").ap()
                for k, v in arrays.items()}
        args["out"] = nc.dram_tensor("out_0", (NB, SEQ, D), F32, kind="ExternalOutput").ap()
        build(nc, args, counts)
    r = run_bass_kernel_spmd(nc, [{f"in_{k}": v for k, v in arrays.items()}], core_ids=[0])
    return r.results[0]["out_0"]
```

```python
from contextlib import ExitStack

import numpy as np
import concourse.bass as bass
from concourse import mybir

F32 = mybir.dt.float32
F16 = mybir.dt.float16
BF16 = mybir.dt.bfloat16
I32 = mybir.dt.int32
F32R = mybir.dt.float32r
ALU = mybir.AluOpType
ACT = mybir.ActivationFunctionType
AX = mybir.AxisListType

P = 128
D = 256
KD = D // P
T = 1024
NT = T // P
SEQ = 512
NB = T // SEQ
TH = NT // NB
EPS = 1e-5

E = 32
EG = 8
EPG = E // EG
TOPK = 4
CAP = 128
H = 128
HS = 512
MS = HS // P
SCALE = 2.5
NQ = 4
EQ = E // NQ
SLOT_A = P // EQ
SLOT_B = CAP // SLOT_A
UQ = SLOT_B // 2
SENTINEL = -3.0e38
PICKED = 3.0e38
FAR = 512.0

NH = 16
HD = D // NH
MASKED = -1.0e30

HID = 704
HID_TILES = [128, 128, 112, 112, 112, 112]
HID_AT = [sum(HID_TILES[:i]) for i in range(len(HID_TILES))]
NHID = len(HID_TILES)
ZERO_POINT = 128.0

MOE, RECUR, QFFN, ATTN = "moe", "recur", "qffn", "attn"
STAGES = [MOE, RECUR, MOE, QFFN, ATTN, QFFN]
LAST = len(STAGES)


class Counts:

    def __init__(self):
        self.values = {}
        self.sems = {}
        self.total = {}

    def start(self, make):
        self.make, self.sems, self.total = make, {}, {}

    def sem(self, name):
        if name not in self.sems:
            self.sems[name] = self.make(name)
        return self.sems[name]

    def mark(self, name, *which, by=1):
        self.total[name] = self.total.get(name, 0) + by
        self.values[(name, *which)] = self.total[name]
        return self.sem(name), by

    def at(self, name, *which):
        return self.sem(name), self.values.get((name, *which), 1)


def build(nc, a, counts):
    with ExitStack() as ctx:
        counts.start(lambda name: ctx.enter_context(nc.semaphore(name)))
        mark, at = counts.mark, counts.at

        def mark16(name, *which):
            return mark(name, *which, by=16)

        def sb(name, shape, dt=F32):
            return ctx.enter_context(nc.sbuf_tensor(name, shape, dt))

        x = sb("x", [P, NT, D])
        xn = sb("xn", [P, NT, D])
        xnT = sb("xnT", [P, KD, T])
        wa = sb("wa", [P, KD, D])
        wx = sb("wx", [P, KD, D])

        pools = ExitStack()

        def pool_sb(name, shape):
            return pools.enter_context(nc.sbuf_tensor(name, shape, F32))

        big = pool_sb("big", [P, 2, 8192])
        xt = pool_sb("xt", [P, 8192])
        rt = pool_sb("rt", [P, 4096])
        rg = pool_sb("rg", [P, 6144])
        sh = pool_sb("sh", [P, 4480])
        gs = pool_sb("gs", [P, 2304])

        up_w = big[:, 0, :].rearrange("p (k e h) -> p k e h", k=KD, e=E)
        down_w = big[:, 1, :].rearrange("p (e d) -> p e d", e=E)
        gate_w = gs[:, 0:KD * E].rearrange("p (k e) -> p k e", k=KD)
        sup_w = gs[:, 64:64 + KD * HS].rearrange("p (k h) -> p k h", k=KD)
        sdown_w = gs[:, 64 + KD * HS:64 + KD * HS + MS * D].rearrange("p (m d) -> p m d", m=MS)
        q_in = big[:, 0, :].bitcast(I32)
        wqkv = rt[:, 0:KD * 3 * D].rearrange("p (k h) -> p k h", k=KD)
        wout = rt[:, KD * 3 * D:KD * 4 * D].rearrange("p (k h) -> p k h", k=KD)

        pools.close()
        base = ExitStack()
        with base:
            hid_r = base.enter_context(nc.sbuf_tensor("hid_r", [P, 2, NHID, T], F32R))
            base.enter_context(nc.sbuf_tensor("pad_a", [P, 2 * 8192 - 2 * NHID * T + 8192 + 4096], F32))
            xr = base.enter_context(nc.sbuf_tensor("xr", [P, 2, KD, T], F32R))
            base.enter_context(nc.sbuf_tensor("pad_b", [P, 6144 - 2 * KD * T], F32))
            qw = base.enter_context(nc.sbuf_tensor("qw", [P, 4480], F32R))
        again = [ctx.enter_context(nc.sbuf_tensor(f"pool{i}", [P, n], F32))
                 for i, n in enumerate((16384, 8192, 4096, 6144, 4480, 2304))]
        qg_w = qw[:, 0:KD * HID].rearrange("p (k h) -> p k h", k=KD)
        qu_w = qw[:, KD * HID:2 * KD * HID].rearrange("p (k h) -> p k h", k=KD)
        qd_w = qw[:, 2 * KD * HID:2 * KD * HID + NHID * D].rearrange("p (m d) -> p m d", m=NHID)

        ident = sb("ident", [P, P])
        identb = sb("identb", [P, P], BF16)
        earlier = sb("earlier", [P, P], BF16)
        ones = sb("ones", [P, P], BF16)
        hide_qk = sb("hide_qk", [P, P], BF16)
        hide_kq = sb("hide_kq", [P, P], BF16)
        iota_a = sb("iota_a", [P, SLOT_A, E], F16)
        iota_b = sb("iota_b", [P, SLOT_B, E], F16)
        token_id = sb("token_id", [P, NT, E], F16)
        own_expert = sb("own_expert", [P, EQ])
        row_base = sb("row_base", [P, E])
        minus_half = sb("minus_half", [P, TH])
        bias_corr = sb("bias_corr", [P, E])
        v_bias = sb("v_bias", [P, D])
        out_bias = sb("out_bias", [P, D])
        sd_row = sb("sd_row", [P, D])
        qk_bias = sb("qk_bias", [P, 2, KD])
        sg_col = sb("sg_col", [P, NHID])
        su_col = sb("su_col", [P, NHID])
        sg_half = sb("sg_half", [P, NHID])
        sgu_half = sb("sgu_half", [P, NHID])
        rec_in = sb("rec_in", [P, 3, KD])
        lam = sb("lam", [P, 12, KD])

        stats = sb("stats", [P, NT, 6])
        mv = sb("mv", [P, NT, 2])
        veps = sb("veps", [P, NT])
        rstd = sb("rstd", [P, NT])

        def rt_view(lo, n):
            return rt[:, lo:lo + n]

        scores = rt_view(0, 256).rearrange("p (j e) -> p j e", j=NT)
        corrected = rt_view(256, 256).rearrange("p (j e) -> p j e", j=NT)
        hi = rt_view(512, 128)
        lo = rt_view(640, 128)
        m1 = rt_view(768, 64)
        mh = rt_view(832, 64)
        ml = rt_view(896, 64)
        gscore = rt_view(960, NT * 12).rearrange("p (j g) -> p j g", j=NT)
        gpick = rt_view(1056, NT * 12).rearrange("p (j g) -> p j g", j=NT)
        top8 = rt_view(1152, 64).rearrange("p (j g) -> p j g", j=NT)
        gmask = rt_view(1216, 64).rearrange("p (j g) -> p j g", j=NT)
        masked = rt_view(1280, NT * 36).rearrange("p (j g) -> p j g", j=NT)
        epick = rt_view(1568, NT * 36).rearrange("p (j g) -> p j g", j=NT)
        used = rt_view(1856, 256).rearrange("p (j e) -> p j e", j=NT)
        wsum = rt_view(2112, 8)
        wrec = rt_view(2120, 8)
        weight = rt_view(2128, 256).rearrange("p (j e) -> p j e", j=NT)
        slot = rt_view(2384, 256).rearrange("p (j e) -> p j e", j=NT)
        slot_i = rt_view(2640, 256).bitcast(I32)
        slot_a = rt_view(2896, 128).bitcast(F16).rearrange("p (j e) -> p j e", j=NT)
        slot_b = rt_view(3024, 128).bitcast(F16).rearrange("p (j e) -> p j e", j=NT)
        part_i = rt_view(3152, 256).bitcast(I32)
        row_code = rt_view(3408, 256).rearrange("p (j e) -> p j e", j=NT)
        used_b = rt_view(3664, 128).bitcast(BF16).rearrange("p (j e) -> p j e", j=NT)
        from_token = rt_view(3792, 32).bitcast(I32)
        ye_row = rt_view(3824, 32).bitcast(I32)
        kweight = rt_view(3856, 32)
        is_a = xt[:, 0:2048].bitcast(F16).rearrange("p (q j a e) -> p q j a e", q=NQ, j=NT, a=SLOT_A)
        is_b = xt[:, 2048:3072].bitcast(F16).rearrange("p (j b e) -> p j b e", j=NT, b=SLOT_B)
        inv = xt[:, 3072:3328].rearrange("p (u e) -> p u e", e=EQ)
        inv_sum = xt[:, 3328:3360]
        ksel = xt[:, 4096:5120].rearrange("p (j k e) -> p j k e", j=NT, k=TOPK)
        xeT = [xt[:, q * 2048:(q + 1) * 2048].rearrange("p (k e b a) -> p k e b a", k=KD, e=EQ, b=SLOT_B)
               for q in range(NQ)]
        picked = xt[:, :].rearrange("p (j k d) -> p j k d", j=NT, k=TOPK)
        RING_XE = 8
        xe = rg[:, 0:2048].rearrange("p (r d) -> p r d", r=RING_XE)
        relu_e = rg[:, 2048:3072].rearrange("p (r c) -> p r c", r=2)
        hid_e = rg[:, 3072:4096].rearrange("p (r c) -> p r c", r=2)
        ye = rg[:, 4096:6144].rearrange("p (r e d) -> p r e d", r=2, e=4)
        relu_s = sb("relu_s", [P, 2, SEQ])
        hid_s = sh[:, 0:MS * T].rearrange("p (m t) -> p m t", m=MS)

        decay = rg[:, 0:2048].rearrange("p (m t) -> p m t", m=KD)
        drive = rg[:, 2048:4096].rearrange("p (m t) -> p m t", m=KD)
        state = rg[:, 4096:6144].rearrange("p (m t) -> p m t", m=KD)

        tanh_q = relu_s
        gated = rg[:, 4096:5120].rearrange("p (r t) -> p r t", r=2)
        hid32 = rg[:, 5120:6144].rearrange("p (r t) -> p r t", r=2)
        scaled = gs[:, 0:512].rearrange("p (j d) -> p j d", j=2)

        HG = 4
        NG = NB * NH // HG
        MAX_UNITS = [(3, 0, 2), (3, 2, 2), (2, 0, 2), (2, 2, 2), (1, 0, 4), (0, 0, 4)]
        NMU = len(MAX_UNITS)
        Q, K = 0, 1
        stack = [big[:, i, :].bitcast(BF16).rearrange("p (h t) -> p h t", h=NH) for i in range(2)]
        SLOTS = [[0, 1, 2, 0, 1, 0], [0, 0, 0, 1, 1, 2]]
        KS = len(SLOTS[0]) * HD
        parts = [xt[:, i * 3072:(i + 1) * 3072].bitcast(BF16)
                 .rearrange("p (m s t) -> p m s t", m=KD, s=3) for i in range(2)]
        qk_f = rt[:, 2048:4096].rearrange("p (r t) -> p r t", r=4)
        VW = HD + 1
        VROW = NH * VW + 16
        val = gs[:, 0:NT * VROW].rearrange("p (j c) -> p j c", j=NT)
        smax = sb("smax", [P, 2, TH, HG])
        smax_r = sb("smax_r", [P, TH, HG])
        smax_p = sb("smax_p", [P, 2, TH, 3, HG], BF16)
        smax_t = sb("smax_t", [3 * HG, 2, SEQ], BF16)
        prob = rg[:, 0:5120].rearrange("p (r s t) -> p r s t", r=2, s=5)
        ctx_u = rg[:, 5120:6144].rearrange("p (r t) -> p r t", r=2)
        den = sb("den", [P, 2, TH, HG])
        ctx_n = xn

        xn_dram = [nc.dram_tensor(f"xn_dram{i}", [T, D], F32).ap() for i in range(2)]
        ye_dram = [nc.dram_tensor(f"ye_dram{i}", [E * CAP, D], F32).ap() for i in range(2)]
        part_dram = nc.dram_tensor("part_dram", [2, 3, NH, HD, T], BF16).ap()
        smax_dram = nc.dram_tensor("smax_dram", [NG, 3 * HG, SEQ], BF16).ap()

        ps = ctx.enter_context(nc.psum_tensor("ps", [P, 8, 512], F32))

        out_v = a["out"].rearrange("b (j p) d -> p (b j) d", p=P)
        x_v = a["x"].rearrange("b (j p) d -> p (b j) d", p=P)

        moe_at = {0: 0, 2: 1}


        def xeT_src(u, k):
            return ps[:, u % 2, :].rearrange("p (b k a e) -> p b k a e", b=2, k=KD, a=SLOT_A)[:, :, k, :, :]

        def xeT_dst(u, k):
            q, b2 = divmod(u, UQ)
            return xeT[q][:, k, :, 2 * b2:2 * b2 + 2, :].rearrange("p e b a -> p b a e")

        def max_view(u, qt):
            two = ps[:, 2 * (u % 2):2 * (u % 2) + 2, :]
            if qt == 2:
                return two[:, :, 0:3 * P]
            if qt == 0:
                return two[:, 0, :].rearrange("p (h w) -> p h w", w=P)
            return two.rearrange("p b c -> p (b c)").rearrange("p (h w) -> p h w", w=(qt + 1) * P)

        smax_bank = ps[0:3 * HG, 7, 0:SEQ // 2].bitcast(BF16)
        LAG = 2
        PIECES = [[(0, 0, 0)], [(0, 1, 0), (0, 3, 384)], [(0, 2, 0), (1, 2, 256)],
                  [(1, 0, 0)], [(1, 1, 0), (1, 3, 384)]]
        PLACE = {(hh, kt): (c, col) for c, piece in enumerate(PIECES) for hh, kt, col in piece}

        block = ctx.enter_context(nc.Block())

        @block.sync
        def _(sp):
            for j in range(NT):
                sp.dma_start(x[:, j, :], x_v[:, j, :]).then_inc(*mark16(f"x_in{j}"))
            sp.dma_start(bias_corr[:], a["bias_corr"].partition_broadcast(P)).then_inc(*mark16("bias_in"))
            sp.dma_start(gate_w, a["gate"]).then_inc(*mark16("gate_in"))
            sp.dma_start(sup_w, a["sup"]).then_inc(*mark16("sup_in"))
            sp.dma_start(sdown_w, a["sdown"]).then_inc(*mark16("sdown_in"))
            for q in range(4):
                sp.dma_start(up_w[:, :, 8 * q:8 * q + 8, :], a["up"][:, :, 8 * q:8 * q + 8, :])\
                    .then_inc(*mark16(f"up_in{q}"))
                sp.dma_start(down_w[:, 8 * q:8 * q + 8, :], a["down"][:, 8 * q:8 * q + 8, :])\
                    .then_inc(*mark16(f"down_in{q}"))
            for i, name in enumerate(("ba", "bx", "lam")):
                sp.dma_start(rec_in[:, i, :], a[name]).then_inc(*mark16("rec_in"))
            sp.dma_start(wa[:], a["wa"]).then_inc(*mark16("wa_in"))
            sp.dma_start(wx[:], a["wx"]).then_inc(*mark16("wx_in"))
            for w, name in ((v_bias, "bv"), (out_bias, "bout"), (sd_row, "s_down")):
                sp.dma_start(w[:], a[name].partition_broadcast(P)).then_inc(*mark16("rows_in"))
            for i, name in enumerate(("bq", "bk")):
                sp.dma_start(qk_bias[:, i, :], a[name]).then_inc(*mark16("qkb_in"))
            for m, (r0, n) in enumerate(zip(HID_AT, HID_TILES)):
                sp.dma_start(sg_col[0:n, m:m + 1], a["s_gate"][r0:r0 + n, :]).then_inc(*mark16("scol_in"))
                sp.dma_start(su_col[0:n, m:m + 1], a["s_up"][r0:r0 + n, :]).then_inc(*mark16("scol_in"))

            def expert_stores(n):
                f = moe_at[n]
                xn_rows = xn_dram[f].rearrange("(j p) d -> p j d", p=P)
                for h in range(NB):
                    sp.wait_ge(*at("xn", n, TH * h + TH - 1))
                    sp.dma_start(xn_rows[:, TH * h:TH * h + TH, :], xn[:, TH * h:TH * h + TH, :])\
                        .then_inc(*mark16(f"xn_out{h}", n))
                ye_rows = ye_dram[f].rearrange("(e c) d -> c e d", c=CAP)
                for g in range(E // 4):
                    sp.wait_ge(*at("ye", n, g, 1))
                    sp.dma_start(ye_rows[:, 4 * g:4 * g + 4, :], ye[:, g % 2, :, :])\
                        .then_inc(*mark16(f"ye_out{g % 2}", n, g))

            expert_stores(0)
            expert_stores(2)
            sp.wait_ge(*at("down_e", 2, E // 2 - 1))
            sp.dma_start(q_in[:, 0:KD * HID].rearrange("p (k h) -> p k h", k=KD), a["wq_gate"])\
                .then_inc(*mark16("qg_in"))
            sp.dma_start(q_in[:, KD * HID:2 * KD * HID].rearrange("p (k h) -> p k h", k=KD), a["wq_up"])\
                .then_inc(*mark16("qu_in"))
            for m, (r0, w) in enumerate(zip(HID_AT, HID_TILES)):
                c = 2 * KD * HID + m * D
                sp.dma_start(q_in[0:w, c:c + D], a["wq_down"][r0:r0 + w, :]).then_inc(*mark16("qd_in"))
            sp.wait_ge(*at("x", 3, NT - 1))
            sp.dma_start(wqkv, a["wqkv"]).then_inc(*mark16("wqkv_in"))
            sp.dma_start(wout, a["wout"]).then_inc(*mark16("wout_in"))

            for c in range(NB * KD):
                b, m = divmod(c, KD)
                tok = slice(b * SEQ, (b + 1) * SEQ)
                heads = slice(8 * m, 8 * m + 8)
                for i in (Q, K):
                    sp.wait_ge(*at("qk_parts", 2 * c + i))
                    dst = part_dram[i, :, heads, :, tok].rearrange("s h r t -> (h r) s t")
                    sp.dma_start(dst, parts[i][:, m, :, tok]).then_inc(*mark16(f"part_out{c}{i}"))
                for i in (Q, K):
                    sp.wait_ge(*at(f"part_out{c}{i}"))
                    if c == 0:
                        sp.wait_ge(*at("x", 4, NT - 1))
                    for s, which in enumerate(SLOTS[i]):
                        sp.dma_start(stack[i][s * HD:(s + 1) * HD, heads, tok],
                                     part_dram[i, which, heads, :, tok].rearrange("h r t -> r h t"))\
                            .then_inc(*mark16(f"stack_in{c}{i}"))

            for gr in range(NG):
                b, h0 = gr * HG // NH, gr * HG % NH
                sp.wait_ge(*at("smax_t", gr))
                sp.dma_start(smax_dram[gr], smax_t[:, gr % 2, :]).then_inc(*mark16(f"smax_out{gr % 2}", gr))
                sp.wait_ge(*at(f"smax_out{gr % 2}", gr))
                sp.dma_start(stack[Q][KS:KS + 3, h0:h0 + HG, b * SEQ:(b + 1) * SEQ],
                            smax_dram[gr].rearrange("(s h) t -> s h t", s=3)).then_inc(*mark16(f"smax_in{gr % 2}", gr))

            for j in range(NT):
                sp.wait_ge(*at("x", LAST, j))
                sp.dma_start(out_v[:, j, :], x[:, j, :]).then_inc(*mark16("out"))
            sp.wait_ge(*at("out"))

        @block.gpsimd
        def _(pool):
            g = nc.gpsimd

            def triangle(dst, cmp, mult, step, fill):
                g.affine_select(out=dst, in_=dst, compare_op=cmp, fill=fill, base=0,
                                pattern=[[step, P]], channel_multiplier=mult).then_inc(*mark("const"))

            g.memset(ident[:], 0.0).then_inc(*mark("cleared"))
            g.memset(identb[:], 0.0).then_inc(*mark("cleared"))
            g.memset(earlier[:], 1.0).then_inc(*mark("cleared"))
            g.memset(hide_qk[:], 0.0).then_inc(*mark("cleared"))
            g.memset(hide_kq[:], 0.0).then_inc(*mark("cleared"))
            g.memset(own_expert[:], 0.0).then_inc(*mark("cleared"))
            g.memset(minus_half[:], -0.5).then_inc(*mark("cleared"))
            g.memset(ones[:], 1.0).then_inc(*mark("const"))
            pool.wait_ge(*at("cleared"))
            triangle(ident[:], ALU.not_equal, 1, -1, 1.0)
            g.affine_select(out=identb[:], in_=identb[:], compare_op=ALU.not_equal, fill=1.0, base=0,
                            pattern=[[-1, P]], channel_multiplier=1).then_inc(*mark("const", "ident"))
            triangle(earlier[:], ALU.is_gt, -1, 1, 0.0)
            triangle(hide_qk[:], ALU.is_ge, 1, -1, MASKED)
            triangle(hide_kq[:], ALU.is_ge, -1, 1, MASKED)
            own = own_expert[:]
            for r in range(P // EQ):
                g.affine_select(out=own, in_=own, compare_op=ALU.not_equal, fill=1.0, base=-EQ * r,
                                pattern=[[-1, EQ]], channel_multiplier=1).then_inc(*mark("own", r))
                pool.wait_ge(*at("own", r))
            g.iota(iota_a[:], pattern=[[1, SLOT_A], [0, E]], base=0, channel_multiplier=0,
                   allow_small_or_imprecise_dtypes=True).then_inc(*mark("const"))
            g.iota(iota_b[:], pattern=[[1, SLOT_B], [0, E]], base=0, channel_multiplier=0,
                   allow_small_or_imprecise_dtypes=True).then_inc(*mark("const"))
            g.iota(token_id[:], pattern=[[P, NT], [0, E]], base=0, channel_multiplier=1,
                   allow_small_or_imprecise_dtypes=True).then_inc(*mark("const"))
            g.iota(row_base[:], pattern=[[-CAP, E]], base=E * CAP, channel_multiplier=0,
                   allow_small_or_imprecise_dtypes=True).then_inc(*mark("const"))

            def rstd_half(n, h):
                pool.wait_ge(*at("veps", n, h))
                g.tensor_tensor(rstd[:, TH * h:TH * h + TH], veps[:, TH * h:TH * h + TH], minus_half[:],
                                ALU.pow).then_inc(*mark("rstd", n, h))

            def square_shared(n):
                for u in range(NB * MS):
                    h, m = divmod(u, MS)
                    pool.wait_ge(*at("relu_s", n, u))
                    r = relu_s[:, u % 2, :]
                    g.tensor_tensor(hid_s[:, m, h * SEQ:(h + 1) * SEQ], r, r, ALU.mult)\
                        .then_inc(*mark("hid_s", n, u))

            def gathers(n):
                f = moe_at[n]
                pool.wait_ge(*at("from_token", n))
                for h in range(NB):
                    pool.wait_ge(*at(f"xn_out{h}", n))
                for u in range(NQ * SLOT_B):
                    if u >= RING_XE:
                        pool.wait_ge(*at("xe_t", n, (u - RING_XE) // 2))
                    elif n == 2:
                        pool.wait_ge(*at("state", NB * KD - 1))
                    g.indirect_dma_start(xe[:, u % RING_XE, :], None, xn_dram[f][:, :],
                                         bass.IndirectOffsetOnAxis(ap=from_token[:, u:u + 1], axis=0))\
                        .then_inc(*mark16(f"xe{u % RING_XE}", n, u))
                for g8 in range(E // 4 - 2, E // 4):
                    pool.wait_ge(*at(f"ye_out{g8 % 2}", n, g8))
                pool.wait_ge(*at("up_e", n, E // 4 - 1))
                pool.wait_ge(*at("kweight", n))
                for j in range(NT):
                    for k in range(TOPK):
                        i = j * TOPK + k
                        g.indirect_dma_start(picked[:, j, k, :], None, ye_dram[f][:, :],
                                             bass.IndirectOffsetOnAxis(ap=ye_row[:, i:i + 1], axis=0))\
                            .then_inc(*mark16(f"picked{j}", n))
                    if j == NT - 3:
                        rstd_half(n + 1, 0)

            def q_low(n):
                for u in range(NB * NHID):
                    b, m = divmod(u, NHID)
                    w = HID_TILES[m]
                    tok = slice(b * SEQ, (b + 1) * SEQ)
                    pool.wait_ge(*at("hid_hi", n, u))
                    g.tensor_tensor(hid_r[0:w, 1, m, tok], hid32[0:w, u % 2, :], hid_r[0:w, 0, m, tok].bitcast(F32),
                                    ALU.subtract).then_inc(*mark("hid_lo", n, u))
                    if n < LAST and u == NB * NHID - 2:
                        rstd_half(n + 1, 0)

            rstd_half(0, 0)
            rstd_half(0, 1)
            square_shared(0)
            gathers(0)
            rstd_half(1, 1)
            rstd_half(2, 0)
            rstd_half(2, 1)
            square_shared(2)
            gathers(2)
            rstd_half(3, 1)
            q_low(3)
            pool.wait_ge(*at("x", 4, NT - 1))
            pool.wait_ge(*at("hid_lo", 3, NB * NHID - 1))
            g.memset(stack[K][KS:KS + 3, :, :], 1.0).then_inc(*mark("k_ones"))
            pool.wait_ge(*at("k_ones"))
            rstd_half(4, 1)
            pool.wait_ge(*at("rows_in"))
            for j in range(NT):
                pool.wait_ge(*at("xn", 4, j))
                g.tensor_tensor(x[:, j, :], x[:, j, :], out_bias[:], ALU.add).then_inc(*mark("x_bias", j))
            rstd_half(5, 0)
            rstd_half(5, 1)
            q_low(5)

        @block.scalar
        def _(act):
            s = nc.scalar

            def evac_xnT(n):
                for u in range(NT // 2):
                    act.wait_ge(*at("tr", n, u))
                    src = ps[:, u % 2, :].rearrange("p (k t) -> p k t", k=KD)
                    s.activation(xnT[:, :, u * 256:(u + 1) * 256], src, ACT.Copy).then_inc(*mark("xnT", n, u))

            def evac_ye(n, g):
                for q in range(2):
                    u = 2 * g + q
                    act.wait_ge(*at("down_e", n, u))
                    if g >= 2:
                        act.wait_ge(*at(f"ye_out{g % 2}", n, g - 2))
                    s.activation(ye[:, g % 2, 2 * q:2 * q + 2, :],
                                 ps[:, 5 + u % 3, :].rearrange("p (e d) -> p e d", e=2), ACT.Copy)\
                        .then_inc(*mark("ye", n, g, q))

            def expert_layer(n):
                evac_xnT(n)
                act.wait_ge(*at("logits", n))
                s.activation(scores, ps[:, 2, 0:NT * E].rearrange("p (j e) -> p j e", j=NT), ACT.Tanh,
                             scale=0.5).then_inc(*mark("tanh_s", n))
                for u in range(NB * MS):
                    act.wait_ge(*at("up_s", n, u))
                    if u >= 2:
                        act.wait_ge(*at("hid_s", n, u - 2))
                    s.activation(relu_s[:, u % 2, :], ps[:, 3 + u % 3, :], ACT.Relu)\
                        .then_inc(*mark("relu_s", n, u))

                def evac_xeT(u):
                    act.wait_ge(*at("xe_t", n, u))
                    for k in range(KD):
                        s.activation(xeT_dst(u, k), xeT_src(u, k), ACT.Copy).then_inc(*mark("xeT_act", n, u, k))

                for u in range(0, UQ, 2):
                    evac_xeT(u)
                act.wait_ge(*at("kweight", n))
                for g in range(E // 4):
                    act.wait_ge(*at("up_e", n, g))
                    if g >= 2:
                        act.wait_ge(*at("hid_e", n, g - 2))
                    s.activation(relu_e[:, g % 2, :], ps[:, 3 + g % 2, :], ACT.Relu)\
                        .then_inc(*mark("relu_e", n, g))
                    if UQ + 2 * g < NQ * UQ:
                        evac_xeT(UQ + 2 * g)
                    if g:
                        evac_ye(n, g - 1)
                evac_ye(n, E // 4 - 1)

            expert_layer(0)

            act.wait_ge(*at("rec_in"))
            s.activation(lam[:, 0, :], rec_in[:, 2, :], ACT.Abs).then_inc(*mark("lam_act", 0))
            act.wait_ge(*at("lam_act", 0))
            s.activation(lam[:, 1, :], lam[:, 0, :], ACT.Exp, scale=-1.0).then_inc(*mark("lam_act", 1))
            s.activation(lam[:, 2, :], rec_in[:, 2, :], ACT.Relu, scale=-1.0).then_inc(*mark("lam_act", 2))


            evac_xnT(1)
            act.wait_ge(*at("rec_vec"))
            for g8 in range(E // 4 - 2, E // 4):
                act.wait_ge(*at(f"ye_out{g8 % 2}", 0, g8))
            for u in range(NB * KD):
                b, m = divmod(u, KD)
                tok = slice(b * SEQ, (b + 1) * SEQ)
                act.wait_ge(*at("proj_r", u))
                s.activation(decay[:, m, tok], ps[:, 2 + 2 * (u % 2), :], ACT.Tanh, scale=0.5,
                             bias=lam[:, 8, m:m + 1]).then_inc(*mark("tanh_r", u))
                act.wait_ge(*at("proj_i", u))
                s.activation(drive[:, m, tok], ps[:, 3 + 2 * (u % 2), :], ACT.Tanh, scale=0.5,
                             bias=lam[:, 9, m:m + 1]).then_inc(*mark("tanh_i", u))
                act.wait_ge(*at("tanh_r", u))
                s.activation(decay[:, m, tok], decay[:, m, tok], ACT.Exp, scale=lam[:, 10, m:m + 1],
                             bias=lam[:, 10, m:m + 1]).then_inc(*mark("decay", u))
                act.wait_ge(*at("decay", u))
                s.activation(state[:, m, tok], decay[:, m, tok], ACT.Square).then_inc(*mark("decay2", u))
            for u in range(NB * KD):
                b, m = divmod(u, KD)
                tok = slice(b * SEQ, (b + 1) * SEQ)
                act.wait_ge(*at("decay2", u))
                s.activation(state[:, m, tok], state[:, m, tok], ACT.Sqrt, scale=-1.0, bias=1.0)\
                    .then_inc(*mark("gain", u))

            expert_layer(2)

            def quantised(n):
                for u in range(NT // 2):
                    act.wait_ge(*at("tr", n, u))
                    s.activation(xr[:, 0, :, u * 256:(u + 1) * 256],
                                 ps[:, u % 2, :].rearrange("p (k t) -> p k t", k=KD), ACT.Copy)\
                        .then_inc(*mark("x_hi", n, u))
                act.wait_ge(*at("scol"))
                for u in range(NB * NHID + 1):
                    if u < NB * NHID:
                        w = HID_TILES[u % NHID]
                        act.wait_ge(*at("q_gate", n, u))
                        if u >= 2:
                            act.wait_ge(*at("gated", n, u - 2))
                        s.activation(tanh_q[0:w, u % 2, :], ps[0:w, 2 + 2 * (u % 2), :], ACT.Tanh,
                                     scale=sg_half[0:w, u % NHID:u % NHID + 1]).then_inc(*mark("tanh_q", n, u))
                    if u:
                        b, m = divmod(u - 1, NHID)
                        w = HID_TILES[m]
                        act.wait_ge(*at("hid32", n, u - 1))
                        s.activation(hid_r[0:w, 0, m, b * SEQ:(b + 1) * SEQ], hid32[0:w, (u - 1) % 2, :], ACT.Copy)\
                            .then_inc(*mark("hid_hi", n, u - 1))

            quantised(3)

            evac_xnT(4)
            act.wait_ge(*at("qkb"))
            for u in range(NB * 2 * KD):
                b, m, i = u // 4, u // 2 % 2, u % 2
                act.wait_ge(*at("proj_qk", u))
                if u >= 4:
                    act.wait_ge(*at("qk_parts", u - 4))
                s.activation(qk_f[:, u % 4, :], ps[:, 2 + u % 2, :], ACT.Identity,
                             scale=(0.25 if i == Q else 1.0), bias=qk_bias[:, i, m:m + 1])\
                    .then_inc(*mark("qk_f", u))
                act.wait_ge(*at("qk_f", u))
                s.activation(parts[i][:, m, 0, b * SEQ:(b + 1) * SEQ], qk_f[:, u % 4, :], ACT.Copy)\
                    .then_inc(*mark("qk_p0", u))

            def evac_ctx(gr):
                act.wait_ge(*at("pv", 2 * gr + 1))
                if gr >= 2:
                    act.wait_ge(*at("ctx_mm", gr - 2))
                s.activation(ctx_u[:, gr % 2, :], ps[:, 6, :], ACT.Copy).then_inc(*mark("ctx_u", gr))

            for pair in range(NB * NH // 2):
                for c in range(5):
                    u = pair * 5 + c
                    act.wait_ge(*at("st", u))
                    if pair >= 2:
                        act.wait_ge(*at("pv", pair - 2))
                    s.activation(prob[:, pair % 2, c, :], ps[:, 4 + u % 2, :], ACT.Exp)\
                        .then_inc(*mark("prob", u))
                    if c == 3 and pair % 2 == 0 and pair:
                        evac_ctx(pair // 2 - 1)
            evac_ctx(NG - 1)
            for u in range(NT // 2):
                act.wait_ge(*at("ctx_tr", u))
                src = ps[:, u % 2, :].rearrange("p (k t) -> p k t", k=KD)
                s.activation(xnT[:, :, u * 256:(u + 1) * 256], src, ACT.Copy).then_inc(*mark("ctxT", u))
            quantised(5)

        @block.vector
        def _(dve):
            v = nc.vector
            links = [0]

            def link(ins):
                links[0] += 1
                ins.then_inc(*mark("dve_step"))
                dve.wait_ge(counts.sem("dve_step"), links[0])

            def ln_stats(n, h):
                for j in range(TH * h, TH * h + TH):
                    dve.wait_ge(*(at("x", n, j) if n else at(f"x_in{j}")))
                    last = v.bn_stats(stats[:, j, :], x[:, j, :])
                link(last)
                for j in range(TH * h, TH * h + TH):
                    last = v.bn_aggr(mv[:, j, :], stats[:, j, :])
                link(last)
                half = slice(TH * h, TH * h + TH)
                v.tensor_scalar(veps[:, half], mv[:, half, 1], EPS, None, ALU.add).then_inc(*mark("veps", n, h))

            def ln_norm(n, h):
                dve.wait_ge(*at("rstd", n, h))
                if n - 1 in moe_at:
                    dve.wait_ge(*at(f"xn_out{h}", n - 1))
                if n == 5:
                    dve.wait_ge(*at("ctx_tr", NT // 2 - 1))
                for j in range(TH * h, TH * h + TH):
                    v.tensor_scalar(xn[:, j, :], x[:, j, :], mv[:, j, 0:1], rstd[:, j:j + 1],
                                    ALU.subtract, ALU.mult).then_inc(*mark("xn", n, j))

            def halves(n, update):
                update(0)
                update(1)
                if n < LAST:
                    ln_stats(n, 0)
                update(2)
                if n < LAST:
                    ln_norm(n, 0)
                update(3)
                if n < LAST:
                    ln_stats(n, 1)
                    ln_norm(n, 1)

            def route(n):
                dve.wait_ge(*at("tanh_s", n))
                link(v.tensor_scalar(scores, scores, 0.5, 0.5, ALU.mult, ALU.add))
                dve.wait_ge(*at("bias_in"))
                link(v.tensor_tensor(corrected, scores, bias_corr[:].unsqueeze(1).to_broadcast([P, NT, E]), ALU.add))
                pairs = corrected.rearrange("p j (g q) -> p (j g) q", q=2)
                v.tensor_tensor(hi, pairs[:, :, 0], pairs[:, :, 1], ALU.max)
                link(v.tensor_tensor(lo, pairs[:, :, 0], pairs[:, :, 1], ALU.min))
                hi2 = hi.rearrange("p (g q) -> p g q", q=2)
                lo2 = lo.rearrange("p (g q) -> p g q", q=2)
                v.tensor_tensor(m1, hi2[:, :, 0], hi2[:, :, 1], ALU.max)
                v.tensor_tensor(mh, hi2[:, :, 0], hi2[:, :, 1], ALU.min)
                link(v.tensor_tensor(ml, lo2[:, :, 0], lo2[:, :, 1], ALU.max))
                link(v.tensor_tensor(mh, mh, ml, ALU.max))
                v.memset(gscore[:, :, EG:12], SENTINEL)
                link(v.tensor_tensor(gscore[:, :, 0:EG], m1.rearrange("p (j g) -> p j g", j=NT),
                                     mh.rearrange("p (j g) -> p j g", j=NT), ALU.add))
                for j in range(NT):
                    last = v.max(top8[:, j, :], gscore[:, j, 0:EG])
                link(last)
                link(v.memset(top8[:, :, TOPK:8], SENTINEL))
                for j in range(NT):
                    last = v.match_replace(gpick[:, j, :], top8[:, j, :], gscore[:, j, :], PICKED)
                link(last)
                link(v.tensor_scalar(gmask, gpick[:, :, 0:EG], PICKED, None, ALU.is_equal))
                v.memset(masked[:, :, E:36], SENTINEL)
                link(v.tensor_tensor(masked[:, :, 0:E].rearrange("p j (g q) -> p j g q", q=EPG),
                                     corrected.rearrange("p j (g q) -> p j g q", q=EPG),
                                     gmask.unsqueeze(3).to_broadcast([P, NT, EG, EPG]), ALU.mult))
                for j in range(NT):
                    last = v.max(top8[:, j, :], masked[:, j, 0:E])
                link(last)
                link(v.memset(top8[:, :, TOPK:8], SENTINEL))
                for j in range(NT):
                    last = v.match_replace(epick[:, j, :], top8[:, j, :], masked[:, j, :], PICKED)
                link(last)
                v.tensor_scalar(used_b, epick[:, :, 0:E], PICKED, None, ALU.is_equal).then_inc(*mark("used_b", n))
                link(v.tensor_scalar(used, epick[:, :, 0:E], PICKED, None, ALU.is_equal))
                link(v.tensor_tensor(weight, used, scores, ALU.mult))
                link(v.tensor_reduce(wsum, weight, AX.X, ALU.add))
                link(v.tensor_scalar(wsum, wsum, 1e-20, None, ALU.add))
                link(v.reciprocal(wrec, wsum))
                link(v.tensor_scalar(wrec, wrec, 0.5 * SCALE, None, ALU.mult))
                v.tensor_tensor(weight, weight, wrec.unsqueeze(2).to_broadcast([P, NT, E]), ALU.mult)
                link(v.tensor_scalar(row_code, used, -FAR, FAR, ALU.mult, ALU.add))
                dve.wait_ge(*at("pos", n))
                v.tensor_tensor(slot, ps[:, 2, 0:NT * E].rearrange("p (j e) -> p j e", j=NT), row_code, ALU.add)\
                    .then_inc(*mark("slot", n))
                dve.wait_ge(*at("slot", n))
                link(v.tensor_copy(slot_i, slot.rearrange("p j e -> p (j e)")))
                link(v.tensor_scalar(part_i, slot_i, SLOT_A - 1, None, ALU.bitwise_and))
                v.tensor_copy(slot_a, part_i.rearrange("p (j e) -> p j e", j=NT))
                link(v.tensor_scalar(slot_i, slot_i, SLOT_A.bit_length() - 1, None, ALU.logical_shift_right))
                link(v.tensor_copy(slot_b, slot_i.rearrange("p (j e) -> p j e", j=NT)))
                for q in range(NQ):
                    own = slice(EQ * q, EQ * (q + 1))
                    shape = [P, NT, SLOT_A, EQ]
                    v.tensor_tensor(is_a[:, q], slot_a[:, :, own].unsqueeze(2).to_broadcast(shape),
                                    iota_a[:, :, own].unsqueeze(1).to_broadcast(shape), ALU.is_equal)
                shape = [P, NT, SLOT_B, E]
                link(v.tensor_tensor(is_b, slot_b.unsqueeze(2).to_broadcast(shape),
                                     iota_b[:].unsqueeze(1).to_broadcast(shape), ALU.is_equal))
                v.tensor_tensor(is_b, is_b, token_id[:].unsqueeze(2).to_broadcast(shape), ALU.mult)\
                    .then_inc(*mark("onehot", n))
                link(v.tensor_scalar(row_code, slot, CAP - 1.0, None, ALU.min))
                link(v.tensor_tensor(row_code, row_base[:].unsqueeze(1).to_broadcast([P, NT, E]), row_code,
                                     ALU.subtract))
                link(v.tensor_tensor(row_code, row_code, used, ALU.mult))
                for j in range(NT):
                    last = v.max(top8[:, j, :], row_code[:, j, :])
                link(last)
                link(v.tensor_scalar(slot, slot, float(CAP), None, ALU.is_lt))
                link(v.tensor_tensor(weight, weight, slot, ALU.mult))
                dve.wait_ge(*at("inv_mm", n))
                v.tensor_tensor(inv, ps[:, 2, 0:NQ * SLOT_B * EQ].rearrange("p (u e) -> p u e", e=EQ),
                                own_expert[:].unsqueeze(1).to_broadcast([P, NQ * SLOT_B, EQ]), ALU.mult)\
                    .then_inc(*mark("inv", n))
                dve.wait_ge(*at("inv", n))
                link(v.tensor_reduce(inv_sum, inv, AX.X, ALU.add))
                v.tensor_copy(from_token, inv_sum).then_inc(*mark("from_token", n))
                v.tensor_scalar(ye_row.rearrange("p (j k) -> p j k", j=NT), top8[:, :, 0:TOPK], -1.0,
                                float(E * CAP), ALU.mult, ALU.add)
                link(v.tensor_tensor(ksel, row_code.unsqueeze(2).to_broadcast([P, NT, TOPK, E]),
                                     top8[:, :, 0:TOPK].unsqueeze(3).to_broadcast([P, NT, TOPK, E]), ALU.is_equal))
                link(v.tensor_tensor(ksel, ksel, weight.unsqueeze(2).to_broadcast([P, NT, TOPK, E]), ALU.mult))
                v.tensor_reduce(kweight.rearrange("p (j k) -> p j k", j=NT), ksel, AX.X, ALU.add)\
                    .then_inc(*mark("kweight", n))

            def expert_layer(n):
                route(n)
                for u in range(NT // 2):
                    dve.wait_ge(*at("down_s", n, u))
                    v.scalar_tensor_tensor(x[:, 2 * u:2 * u + 2, :],
                                           ps[:, 3 + (NB * MS + u) % 3, :].rearrange("p (j d) -> p j d", j=2),
                                           0.5, x[:, 2 * u:2 * u + 2, :], ALU.mult, ALU.add)\
                        .then_inc(*mark("shared_out", n, u))

                def evac_xeT(u):
                    dve.wait_ge(*at("xe_t", n, u))
                    for k in range(KD):
                        v.tensor_copy(xeT_dst(u, k), xeT_src(u, k)).then_inc(*mark("xeT_dve", n, u, k))

                for u in range(1, UQ, 2):
                    evac_xeT(u)
                for g in range(E // 4):
                    dve.wait_ge(*at("relu_e", n, g))
                    if g >= 2:
                        dve.wait_ge(*at("down_e", n, 2 * (g - 2) + 1))
                    v.tensor_tensor(hid_e[:, g % 2, :], relu_e[:, g % 2, :], relu_e[:, g % 2, :], ALU.mult)\
                        .then_inc(*mark("hid_e", n, g))
                    if UQ + 2 * g < NQ * UQ:
                        evac_xeT(UQ + 2 * g + 1)
                if n == 0:
                    vectors()
                else:
                    quantised_weights()

                def combine(u):
                    for j in (2 * u, 2 * u + 1):
                        dve.wait_ge(*at(f"picked{j}", n))
                        if j == 0:
                            dve.wait_ge(*at("shared_out", n, NT // 2 - 1))
                            dve.wait_ge(*at("kweight", n))
                        for k in range(TOPK):
                            i = j * TOPK + k
                            last = v.scalar_tensor_tensor(x[:, j, :], picked[:, j, k, :], kweight[:, i:i + 1],
                                                          x[:, j, :], ALU.mult, ALU.add)
                            if k < TOPK - 1:
                                link(last)
                        last.then_inc(*mark("x", n + 1, j))

                halves(n + 1, combine)

            def quantised_weights():
                dve.wait_ge(*at("shared_out", 2, NT // 2 - 1))
                for i, name in enumerate(("qg_in", "qu_in")):
                    dve.wait_ge(*at(name))
                    part = slice(i * KD * HID, (i + 1) * KD * HID)
                    v.tensor_scalar(qw[:, part], q_in[:, part], -ZERO_POINT, None, ALU.add)\
                        .then_inc(*mark("q_weights"))
                dve.wait_ge(*at("qd_in"))
                for c0, n_, w in ((0, 2, 128), (2, 4, 112)):
                    part = slice(2 * KD * HID + c0 * D, 2 * KD * HID + (c0 + n_) * D)
                    v.tensor_scalar(qw[0:w, part], q_in[0:w, part], -ZERO_POINT, None, ALU.add)\
                        .then_inc(*mark("q_weights"))

            def vectors():
                dve.wait_ge(*at("rec_in"))
                v.tensor_scalar(lam[:, 8, :], rec_in[:, 0, :], 0.5, None, ALU.mult)
                v.tensor_scalar(lam[:, 9, :], rec_in[:, 1, :], 0.5, None, ALU.mult)
                dve.wait_ge(*at("lam_act", 2))
                link(v.tensor_scalar(lam[:, 3, :], lam[:, 1, :], 2.0, None, ALU.add))
                link(v.reciprocal(lam[:, 4, :], lam[:, 3, :]))
                link(v.tensor_tensor(lam[:, 5, :], lam[:, 1, :], lam[:, 4, :], ALU.mult))
                link(v.tensor_tensor(lam[:, 6, :], lam[:, 5, :], lam[:, 5, :], ALU.mult))
                link(v.tensor_scalar(lam[:, 7, :], lam[:, 6, :], 1.0 / 19.0, None, ALU.mult))
                for i in range(8, 0, -1):
                    link(v.scalar_tensor_tensor(lam[:, 7, :], lam[:, 7, :], 1.0 / (2 * i + 1), lam[:, 6, :],
                                                ALU.add, ALU.mult))
                link(v.scalar_tensor_tensor(lam[:, 7, :], lam[:, 7, :], 1.0, lam[:, 5, :], ALU.add, ALU.mult))
                link(v.scalar_tensor_tensor(lam[:, 11, :], lam[:, 7, :], 2.0, lam[:, 2, :], ALU.mult, ALU.add))
                v.tensor_scalar(lam[:, 10, :], lam[:, 11, :], -4.0, None, ALU.mult).then_inc(*mark("rec_vec"))

                dve.wait_ge(*at("rows_in"))
                v.tensor_scalar(sd_row[:], sd_row[:], 0.5, None, ALU.mult)
                dve.wait_ge(*at("qkb_in"))
                v.tensor_scalar(qk_bias[:, 0, :], qk_bias[:, 0, :], 0.25, None, ALU.mult).then_inc(*mark("qkb"))
                dve.wait_ge(*at("scol_in"))
                for w, c0, c1 in ((128, 0, 2), (112, 2, NHID)):
                    link(v.tensor_scalar(sg_half[0:w, c0:c1], sg_col[0:w, c0:c1], 0.5, None, ALU.mult))
                    v.tensor_tensor(sgu_half[0:w, c0:c1], sg_half[0:w, c0:c1], su_col[0:w, c0:c1], ALU.mult)\
                        .then_inc(*mark("scol"))

            ln_stats(0, 0)
            ln_stats(0, 1)
            ln_norm(0, 0)
            ln_norm(0, 1)

            expert_layer(0)

            for u in range(NB * KD):
                b, m = divmod(u, KD)
                tok = slice(b * SEQ, (b + 1) * SEQ)
                dve.wait_ge(*at("tanh_i", u))
                v.scalar_tensor_tensor(drive[:, m, tok], drive[:, m, tok], 1.0, xnT[:, m, tok],
                                       ALU.add, ALU.mult).then_inc(*mark("drive0", u))

            def recur(q):
                b, half = divmod(q, 2)
                if half == 0:
                    for m in range(KD):
                        u = KD * b + m
                        tok = slice(b * SEQ, (b + 1) * SEQ)
                        dve.wait_ge(*at("gain", u))
                        dve.wait_ge(*at("drive0", u))
                        link(v.scalar_tensor_tensor(drive[:, m, tok], drive[:, m, tok], 0.5, state[:, m, tok],
                                                    ALU.mult, ALU.mult))
                        v.tensor_tensor_scan(state[:, m, tok], decay[:, m, tok], drive[:, m, tok], 0.0,
                                             ALU.mult, ALU.add).then_inc(*mark("state", u))
                dve.wait_ge(*at("state_t", q))
                for j in (2 * q, 2 * q + 1):
                    v.tensor_tensor(x[:, j, :], x[:, j, :], ps[:, 6 + q % 2, (j % 2) * D:(j % 2 + 1) * D], ALU.add)\
                        .then_inc(*mark("x", 2, j))

            halves(2, recur)

            expert_layer(2)

            def quantised(n):
                for u in range(NT // 2):
                    dve.wait_ge(*at("x_hi", n, u))
                    tok = slice(u * 256, (u + 1) * 256)
                    v.tensor_tensor(xr[:, 1, :, tok], ps[:, u % 2, :].rearrange("p (k t) -> p k t", k=KD),
                                    xr[:, 0, :, tok].bitcast(F32), ALU.subtract).then_inc(*mark("x_lo", n, u))

                def hidden(u):
                    m = u % NHID
                    w = HID_TILES[m]
                    dve.wait_ge(*at("tanh_q", n, u))
                    v.scalar_tensor_tensor(gated[0:w, u % 2, :], tanh_q[0:w, u % 2, :], 1.0,
                                           ps[0:w, 2 + 2 * (u % 2), :], ALU.add, ALU.mult)\
                        .then_inc(*mark("gated", n, u))
                    dve.wait_ge(*at("q_up", n, u))
                    dve.wait_ge(*at("gated", n, u))
                    if u >= 2:
                        dve.wait_ge(*at("hid_lo", n, u - 2))
                    v.scalar_tensor_tensor(hid32[0:w, u % 2, :], ps[0:w, 3 + 2 * (u % 2), :],
                                           sgu_half[0:w, m:m + 1], gated[0:w, u % 2, :],
                                           ALU.mult, ALU.mult).then_inc(*mark("hid32", n, u))

                def update(q):
                    dve.wait_ge(*at("q_down", n, q))
                    if q:
                        dve.wait_ge(*at("x", n + 1, 2 * q - 1))
                    link(v.tensor_tensor(scaled, ps[:, 6 + q % 2, :].rearrange("p (j d) -> p j d", j=2),
                                         sd_row[:].unsqueeze(1).to_broadcast([P, 2, D]), ALU.mult))
                    for j in (2 * q, 2 * q + 1):
                        v.tensor_tensor(x[:, j, :], x[:, j, :], scaled[:, j % 2, :], ALU.add)\
                            .then_inc(*mark("x", n + 1, j))

                for u in range(NB * NHID):
                    hidden(u)
                    if u == NHID + 2:
                        update(0)
                    if u == NHID + 3:
                        update(1)
                    if u == NHID + 4 and n < LAST:
                        ln_stats(n + 1, 0)
                if n < LAST:
                    ln_norm(n + 1, 0)
                update(2)
                update(3)
                if n < LAST:
                    ln_stats(n + 1, 1)
                    ln_norm(n + 1, 1)

            quantised(3)

            v.memset(val, 1.0).then_inc(*mark("val_ones"))
            dve.wait_ge(*at("val_ones"))

            def split_qk(u):
                b, m, i = u // 4, u // 2 % 2, u % 2
                tok = slice(b * SEQ, (b + 1) * SEQ)
                f = qk_f[:, u % 4, :]
                dve.wait_ge(*at("qk_p0", u))
                link(v.tensor_tensor(f, f, parts[i][:, m, 0, tok], ALU.subtract))
                link(v.tensor_copy(parts[i][:, m, 1, tok], f))
                v.tensor_tensor(parts[i][:, m, 2, tok], f, parts[i][:, m, 1, tok], ALU.subtract)\
                    .then_inc(*mark("qk_parts", u))

            def values(w):
                dve.wait_ge(*at("proj_v", w))
                v.tensor_tensor(val[:, 2 * w:2 * w + 2, 0:NH * VW].rearrange("p j (h c) -> p j h c", h=NH)[:, :, :, 0:HD],
                                ps[:, 6 + w % 2, :].rearrange("p (j h c) -> p j h c", j=2, h=NH),
                                v_bias[:].rearrange("p (h c) -> p h c", h=NH).unsqueeze(1)
                                .to_broadcast([P, 2, NH, HD]), ALU.add).then_inc(*mark("val", w))

            for b in range(NB):
                for u in range(4 * b, 4 * b + 4):
                    split_qk(u)
                values(2 * b)
                values(2 * b + 1)

            def maxima(gr, i):
                qt, h0, k = MAX_UNITS[i]
                u = gr * NMU + i
                dve.wait_ge(*at("s_max", u))
                v.tensor_reduce(smax[:, gr % 2, qt, h0:h0 + k], max_view(u, qt), AX.X, ALU.max)\
                    .then_inc(*mark("smax", u))

            def split_maxima(gr):
                r = gr % 2
                dve.wait_ge(*at("smax", (gr + 1) * NMU - 1))
                if gr >= 2:
                    dve.wait_ge(*at("smax_tr", gr - 2))
                link(v.tensor_scalar(smax_p[:, r, :, 0, :], smax[:, r], -1.0, None, ALU.mult))
                link(v.scalar_tensor_tensor(smax_r[:], smax[:, r], -1.0, smax_p[:, r, :, 0, :],
                                            ALU.mult, ALU.subtract))
                link(v.tensor_copy(smax_p[:, r, :, 1, :], smax_r[:]))
                v.tensor_tensor(smax_p[:, r, :, 2, :], smax_r[:], smax_p[:, r, :, 1, :], ALU.subtract)\
                    .then_inc(*mark("smax_p", gr))

            def store_maxima(gr):
                dve.wait_ge(*at("smax_tr", gr))
                if gr >= 2:
                    dve.wait_ge(*at(f"smax_out{gr % 2}", gr - 2))
                v.tensor_copy(smax_t[:, gr % 2, :], smax_bank).then_inc(*mark("smax_t", gr))

            def context(gr):
                b, h0 = gr * HG // NH, gr * HG % NH
                dve.wait_ge(*at("ctx_mm", gr))
                src = ps[:, 7, :].rearrange("p (q h c) -> p q h c", q=TH, h=HG)
                link(v.reciprocal(den[:, gr % 2], src[:, :, :, HD]))
                dst = ctx_n[:, TH * b:TH * b + TH, HD * h0:HD * (h0 + HG)].rearrange("p q (h c) -> p q h c", h=HG)
                v.tensor_tensor(dst, src[:, :, :, 0:HD], den[:, gr % 2].unsqueeze(3).to_broadcast([P, TH, HG, HD]),
                                ALU.mult).then_inc(*mark("ctx", gr))

            for gr in range(NG + LAG + 1):
                if gr < NG:
                    for i in range(NMU):
                        maxima(gr, i)
                    split_maxima(gr)
                if gr > LAG:
                    context(gr - LAG - 1)
                if gr < NG:
                    store_maxima(gr)

            def attended(q):
                dve.wait_ge(*at("attn_out", q))
                dve.wait_ge(*at("x_bias", NT - 1))
                for j in (2 * q, 2 * q + 1):
                    v.tensor_tensor(x[:, j, :], x[:, j, :], ps[:, 2 + q % 2, (j % 2) * D:(j % 2 + 1) * D], ALU.add)\
                        .then_inc(*mark("x", 5, j))

            halves(5, attended)
            quantised(5)

        @block.tensor
        def _(pe):
            t = nc.tensor
            reader = {}

            def take(bank, *read):
                if bank in reader:
                    pe.wait_ge(*at(*reader[bank]))
                reader[bank] = read

            def transposes(n, read="xnT"):
                for u in range(NT // 2):
                    take(u % 2, read, n, u)
                    for j in (2 * u, 2 * u + 1):
                        pe.wait_ge(*at("xn", n, j))
                        for k in range(KD):
                            last = t.transpose(ps[:, u % 2, k * 256 + (j % 2) * P:k * 256 + (j % 2 + 1) * P],
                                               xn[:, j, k * P:(k + 1) * P], ident[:])
                    last.then_inc(*mark("tr", n, u))

            def expert_layer(n):
                f = moe_at[n]
                if n == 0:
                    pe.wait_ge(*at("const", "ident"))
                transposes(n)
                pe.wait_ge(*at("gate_in"))
                take(2, "tanh_s", n)
                for j in range(NT):
                    pe.wait_ge(*at("xnT", n, j // 2))
                    for k in range(KD):
                        last = t.matmul(ps[:, 2, j * E:(j + 1) * E], xnT[:, k, j * P:(j + 1) * P], gate_w[:, k, :],
                                        start=(k == 0), stop=(k == KD - 1))
                last.then_inc(*mark("logits", n))

                def shared_up(u):
                    h, m = divmod(u, MS)
                    take(3 + u % 3, "relu_s", n, u)
                    for k in range(KD):
                        last = t.matmul(ps[:, 3 + u % 3, :], sup_w[:, k, m * P:(m + 1) * P],
                                        xnT[:, k, h * SEQ:(h + 1) * SEQ], start=(k == 0), stop=(k == KD - 1))
                    last.then_inc(*mark("up_s", n, u))

                pe.wait_ge(*at("sup_in"))
                for u in range(MS):
                    shared_up(u)
                pe.wait_ge(*at("const"))
                pe.wait_ge(*at("used_b", n))
                take(2, "slot", n)
                for j in range(NT):
                    for i in range(j):
                        t.matmul(ps[:, 2, j * E:(j + 1) * E], ones[:], used_b[:, i, :], start=(i == 0), stop=False)
                    last = t.matmul(ps[:, 2, j * E:(j + 1) * E], earlier[:], used_b[:, j, :],
                                    start=(j == 0), stop=True)
                last.then_inc(*mark("pos", n))
                for u in range(MS, NB * MS):
                    shared_up(u)
                pe.wait_ge(*at("onehot", n))
                take(2, "inv", n)
                for q in range(NQ):
                    own = slice(EQ * q, EQ * (q + 1))
                    for j in range(NT):
                        last = t.matmul(ps[:, 2, q * SLOT_B * EQ:(q + 1) * SLOT_B * EQ],
                                        is_a[:, q, j].rearrange("p a e -> p (a e)"), is_b[:, j, :, own],
                                        start=(j == 0), stop=(j == NT - 1))
                last.then_inc(*mark("inv_mm", n))
                pe.wait_ge(*at("sdown_in"))
                for u in range(NT // 2):
                    bank = 3 + (NB * MS + u) % 3
                    take(bank, "shared_out", n, u)
                    pe.wait_ge(*at("hid_s", n, NB * MS - 1 if u >= 2 else MS - 1))
                    for j in (2 * u, 2 * u + 1):
                        for m in range(MS):
                            last = t.matmul(ps[:, bank, (j % 2) * D:(j % 2 + 1) * D], hid_s[:, m, j * P:(j + 1) * P],
                                            sdown_w[:, m, :], start=(m == 0), stop=(m == MS - 1))
                    last.then_inc(*mark("down_s", n, u))

                def up(g):
                    take(3 + g % 2, "relu_e", n, g)
                    pe.wait_ge(*at(f"up_in{g // 2}"))
                    if g % 2 == 0:
                        last_u = (g // 2 + 1) * UQ - 1
                        pe.wait_ge(*at("xeT_act", n, last_u - 1, KD - 1))
                        pe.wait_ge(*at("xeT_dve", n, last_u, KD - 1))
                    for e in range(4 * g, 4 * g + 4):
                        rhs = xeT[e // EQ][:, :, e % EQ, :, :].rearrange("p k b a -> p k (b a)")
                        for k in range(KD):
                            last = t.matmul(ps[:, 3 + g % 2, (e % 4) * CAP:(e % 4 + 1) * CAP], up_w[:, k, e, :],
                                            rhs[:, k, :], start=(k == 0), stop=(k == KD - 1))
                    last.then_inc(*mark("up_e", n, g))

                def down(g):
                    pe.wait_ge(*at("hid_e", n, g))
                    pe.wait_ge(*at(f"down_in{g // 2}"))
                    for q in range(2):
                        u = 2 * g + q
                        take(5 + u % 3, "ye", n, g, q)
                        for e in (4 * g + 2 * q, 4 * g + 2 * q + 1):
                            last = t.matmul(ps[:, 5 + u % 3, (e % 2) * D:(e % 2 + 1) * D],
                                            hid_e[:, g % 2, (e % 4) * CAP:(e % 4 + 1) * CAP], down_w[:, e, :],
                                            start=True, stop=True)
                        last.then_inc(*mark("down_e", n, u))

                def transpose_slots(u):
                    take(u % 2, *(("xeT_dve" if u % 2 else "xeT_act"), n, u, KD - 1))
                    for g in (2 * u, 2 * u + 1):
                        pe.wait_ge(*at(f"xe{g % RING_XE}", n, g))
                        for k in range(KD):
                            c = (g % 2) * 256 + k * P
                            last = t.transpose(ps[:, u % 2, c:c + P], xe[:, g % RING_XE, k * P:(k + 1) * P],
                                               ident[:])
                    last.then_inc(*mark("xe_t", n, u))

                for u in range(UQ):
                    transpose_slots(u)
                for g in range(E // 4):
                    up(g)
                    for u in range(UQ + 2 * g, min(UQ + 2 * g + 2, NQ * UQ)):
                        transpose_slots(u)
                    if g:
                        down(g - 1)
                down(E // 4 - 1)

            expert_layer(0)

            transposes(1)
            pe.wait_ge(*at("wa_in"))
            pe.wait_ge(*at("wx_in"))
            for u in range(NB * KD):
                b, m = divmod(u, KD)
                pe.wait_ge(*at("xnT", 1, 2 * b + 1))
                for w, name, bank, read in ((wa, "proj_r", 2 + 2 * (u % 2), "tanh_r"),
                                            (wx, "proj_i", 3 + 2 * (u % 2), "tanh_i")):
                    take(bank, read, u)
                    for k in range(KD):
                        last = t.matmul(ps[:, bank, :], w[:, k, m * P:(m + 1) * P], xnT[:, k, b * SEQ:(b + 1) * SEQ],
                                        start=(k == 0), stop=(k == KD - 1))
                    last.then_inc(*mark(name, u))
            for q in range(NT // 2):
                pe.wait_ge(*at("state", KD * (q // 2) + KD - 1))
                take(6 + q % 2, "x", 2, 2 * q + 1)
                for j in (2 * q, 2 * q + 1):
                    for m in range(KD):
                        c = (j % 2) * D + m * P
                        last = t.transpose(ps[:, 6 + q % 2, c:c + P], state[:, m, j * P:(j + 1) * P], ident[:])
                last.then_inc(*mark("state_t", q))

            expert_layer(2)

            def quantised(n):
                transposes(n, "x_lo")
                pe.wait_ge(*at("q_weights"))

                def down(q):
                    take(6 + q % 2, "x", n + 1, 2 * q + 1)
                    pe.wait_ge(*at("hid_lo", n, (q // 2 + 1) * NHID - 1))
                    for j in (2 * q, 2 * q + 1):
                        for m, w in enumerate(HID_TILES):
                            for part in range(2):
                                last = t.matmul(ps[:, 6 + q % 2, (j % 2) * D:(j % 2 + 1) * D],
                                                hid_r[0:w, part, m, j * P:(j + 1) * P], qd_w[0:w, m, :],
                                                start=(m == 0 and part == 0),
                                                stop=(m == NHID - 1 and part == 1))
                    last.then_inc(*mark("q_down", n, q))

                for u in range(NB * NHID):
                    b, m = divmod(u, NHID)
                    if m == 0:
                        pe.wait_ge(*at("x_lo", n, 2 * b + 1))
                    c, w = HID_AT[m], HID_TILES[m]
                    for wt, name, bank, read in ((qg_w, "q_gate", 2 + 2 * (u % 2), "gated"),
                                                 (qu_w, "q_up", 3 + 2 * (u % 2), "hid32")):
                        take(bank, read, n, u)
                        for k in range(KD):
                            for part in range(2):
                                last = t.matmul(ps[0:w, bank, :], wt[:, k, c:c + w],
                                                xr[:, part, k, b * SEQ:(b + 1) * SEQ],
                                                start=(k == 0 and part == 0), stop=(k == KD - 1 and part == 1))
                        last.then_inc(*mark(name, n, u))
                    if u in (NHID + 1, NHID + 2):
                        down(u - NHID - 1)
                down(2)
                down(3)

            quantised(3)

            transposes(4)
            pe.wait_ge(*at("wqkv_in"))
            for b in range(NB):
                pe.wait_ge(*at("xnT", 4, 2 * b + 1))
                for u in range(4 * b, 4 * b + 4):
                    m, i = u // 2 % 2, u % 2
                    take(2 + u % 2, "qk_f", u)
                    for k in range(KD):
                        c = i * D + m * P
                        last = t.matmul(ps[:, 2 + u % 2, :], wqkv[:, k, c:c + P], xnT[:, k, b * SEQ:(b + 1) * SEQ],
                                        start=(k == 0), stop=(k == KD - 1))
                    last.then_inc(*mark("proj_qk", u))
                for w in (2 * b, 2 * b + 1):
                    take(6 + w % 2, "val", w)
                    for j in (2 * w, 2 * w + 1):
                        for k in range(KD):
                            last = t.matmul(ps[:, 6 + w % 2, (j % 2) * D:(j % 2 + 1) * D],
                                            xnT[:, k, j * P:(j + 1) * P], wqkv[:, k, 2 * D:3 * D],
                                            start=(k == 0), stop=(k == KD - 1))
                    last.then_inc(*mark("proj_v", w))

            def scores_max(gr, i):
                qt, h0, count = MAX_UNITS[i]
                u = gr * NMU + i
                b, head = gr * HG // NH, gr * HG % NH + h0
                if i == 0 and gr % 2 == 0:
                    pe.wait_ge(*at(f"stack_in{gr // 2}{Q}"))
                    pe.wait_ge(*at(f"stack_in{gr // 2}{K}"))
                first = 2 * (u % 2)
                take(first, "smax", u)
                if qt:
                    take(first + 1, "smax", u)
                width = (qt + 1) * P
                per_bank = {3: 1, 2: 1, 1: 2, 0: 4}[qt]
                q0 = b * SEQ + qt * P
                for c in range(count):
                    bank, col = first + c // per_bank, (c % per_bank) * width
                    t.matmul(ps[:, bank, col:col + width], stack[Q][0:KS, head + c, q0:q0 + P],
                             stack[K][0:KS, head + c, b * SEQ:b * SEQ + width], start=True, stop=False)
                    last = t.matmul(ps[:, bank, col + width - P:col + width], identb[:], hide_qk[:],
                                    start=False, stop=True)
                last.then_inc(*mark("s_max", u))

            def transpose_maxima(gr):
                pe.wait_ge(*at("smax_p", gr))
                take(7, "smax_t", gr)
                for qt in range(TH):
                    last = t.transpose(smax_bank[:, qt * P:(qt + 1) * P],
                                       smax_p[:, gr % 2, qt, :, :].rearrange("p s h -> p (s h)"), identb[:])
                last.then_inc(*mark("smax_tr", gr))

            def scores_exp(pair, c):
                b, h = divmod(pair * 2, NH)
                if c == 0 and pair % 2 == 0:
                    pe.wait_ge(*at(f"smax_in{pair // 2 % 2}", pair // 2))
                    pe.wait_ge(*at("k_ones"))
                u = pair * 5 + c
                bank = 4 + u % 2
                take(bank, "prob", u)
                for hh, kt, col in PIECES[c]:
                    k0 = b * SEQ + kt * P
                    width = SEQ - kt * P
                    t.matmul(ps[:, bank, col:col + width], stack[K][0:KS + 3, h + hh, k0:k0 + P],
                             stack[Q][0:KS + 3, h + hh, k0:k0 + width], start=True, stop=False)
                    last = t.matmul(ps[:, bank, col:col + P], identb[:], hide_kq[:], start=False, stop=True)
                last.then_inc(*mark("st", u))

            def weighted_values(pair):
                b, h = divmod(pair * 2, NH)
                pe.wait_ge(*at("prob", pair * 5 + 4))
                pe.wait_ge(*at("val", 2 * b + 1))
                if pair % 2 == 0:
                    take(6, "ctx_u", pair // 2)
                for kt in range(TH):
                    for hh in range(2):
                        piece, col = PLACE[hh, kt]
                        row = 32 * ((h + hh) % HG)
                        first = (h + hh) * VW
                        last = t.matmul(ps[row:row + 32, 6, kt * P:SEQ], val[:, TH * b + kt, first:first + 32],
                                        prob[:, pair % 2, piece, col:col + SEQ - kt * P],
                                        start=(kt == 0), stop=(kt == TH - 1))
                last.then_inc(*mark("pv", pair))

            def transpose_context(gr):
                pe.wait_ge(*at("ctx_u", gr))
                take(7, "ctx", gr)
                for qt in range(TH):
                    last = t.transpose(ps[:, 7, qt * P:(qt + 1) * P], ctx_u[:, gr % 2, qt * P:(qt + 1) * P], ident[:])
                last.then_inc(*mark("ctx_mm", gr))

            for gr in range(NG + LAG + 1):
                pieces = [(2 * (gr - LAG) + n // 5, n % 5) for n in range(10)] if LAG <= gr < NG + LAG else []
                for i in range(NMU):
                    if gr < NG:
                        scores_max(gr, i)
                    for _ in range(2 if pieces and i < 4 else 1 if pieces else 0):
                        pair, c = pieces.pop(0)
                        scores_exp(pair, c)
                        if c == 2 and pair:
                            weighted_values(pair - 1)
                        if c == 4 and pair % 2 == 0 and pair:
                            transpose_context(pair // 2 - 1)
                if gr == NG + LAG:
                    weighted_values(2 * NG - 1)
                    transpose_context(NG - 1)
                if gr < NG:
                    transpose_maxima(gr)

            pe.wait_ge(*at("wout_in"))
            for u in range(NT // 2):
                take(u % 2, "ctxT", u)
                pe.wait_ge(*at("ctx", (u // 2 + 1) * (NG // NB) - 1))
                for j in (2 * u, 2 * u + 1):
                    for k in range(KD):
                        last = t.transpose(ps[:, u % 2, k * 256 + (j % 2) * P:k * 256 + (j % 2 + 1) * P],
                                           ctx_n[:, j, k * P:(k + 1) * P], ident[:])
                last.then_inc(*mark("ctx_tr", u))
            for q in range(NT // 2):
                take(2 + q % 2, "x", 5, 2 * q + 1)
                pe.wait_ge(*at("ctxT", q))
                for j in (2 * q, 2 * q + 1):
                    for k in range(KD):
                        last = t.matmul(ps[:, 2 + q % 2, (j % 2) * D:(j % 2 + 1) * D], xnT[:, k, j * P:(j + 1) * P],
                                        wout[:, k, :], start=(k == 0), stop=(k == KD - 1))
                last.then_inc(*mark("attn_out", q))

            quantised(5)


def _layouts(inputs):
    def rows(w, k):
        return w.reshape(k, P, *w.shape[1:]).swapaxes(0, 1)

    f = {k: np.asarray(v) for k, v in inputs.items()}
    wqkv = f["L1_attn_W_qkv"].reshape(D, NH, 3, HD).transpose(0, 2, 1, 3).reshape(D, 3 * D)
    bqkv = f["L1_attn_b_qkv"].reshape(NH, 3, HD).transpose(1, 0, 2).reshape(3, D)
    out = {
        "x": f["L0_attn_x"],
        "gate": rows(f["L0_ffn_gate_w"].T, KD),
        "bias_corr": f["L0_ffn_bias_corr"],
        "sup": rows(f["L0_ffn_shared_up_w"].T, KD),
        "sdown": rows(f["L0_ffn_shared_down_w"].T, MS),
        "up": rows(f["L0_ffn_up_w"].transpose(2, 0, 1), KD),
        "down": f["L0_ffn_down_w"].transpose(2, 0, 1),
        "wa": rows(f["L0_attn_Wa"].T, KD),
        "wx": rows(f["L0_attn_Wx"].T, KD),
        "ba": rows(f["L0_attn_ba"], KD),
        "bx": rows(f["L0_attn_bx"], KD),
        "lam": rows(f["L0_attn_Lam"], KD),
        "wqkv": rows(wqkv, KD),
        "bq": rows(bqkv[0], KD),
        "bk": rows(bqkv[1], KD),
        "bv": bqkv[2],
        "wout": rows(f["L1_attn_W_out"], KD),
        "bout": f["L1_attn_b_out"],
        "wq_gate": rows(f["L1_ffn_wq_gate"].T, KD),
        "wq_up": rows(f["L1_ffn_wq_up"].T, KD),
        "wq_down": f["L1_ffn_wq_down"].T,
        "s_gate": f["L1_ffn_s_gate"].reshape(HID, 1),
        "s_up": f["L1_ffn_s_up"].reshape(HID, 1),
        "s_down": f["L1_ffn_s_down"],
    }
    return {k: np.ascontiguousarray(v) for k, v in out.items()}


def kernel(**inputs):
    import concourse.bacc as bacc
    from concourse.bass_utils import run_bass_kernel_spmd

    arrays = _layouts(inputs)
    counts = Counts()
    for _ in range(2):
        nc = bacc.Bacc("TRN2", target_bir_lowering=False, num_devices=1)
        args = {k: nc.dram_tensor(f"in_{k}", v.shape, mybir.dt.from_np(v.dtype), kind="ExternalInput").ap()
                for k, v in arrays.items()}
        args["out"] = nc.dram_tensor("out_0", (NB, SEQ, D), F32, kind="ExternalOutput").ap()
        build(nc, args, counts)
    r = run_bass_kernel_spmd(nc, [{f"in_{k}": v for k, v in arrays.items()}], core_ids=[0])
    return r.results[0]["out_0"]
```

```python
from contextlib import ExitStack

import numpy as np
import concourse.bass as bass
from concourse import mybir

F32 = mybir.dt.float32
F16 = mybir.dt.float16
BF16 = mybir.dt.bfloat16
I32 = mybir.dt.int32
F32R = mybir.dt.float32r
ALU = mybir.AluOpType
ACT = mybir.ActivationFunctionType
AX = mybir.AxisListType

P = 128
D = 256
KD = D // P
T = 1024
NT = T // P
SEQ = 512
NB = T // SEQ
TH = NT // NB
EPS = 1e-5

E = 32
EG = 8
EPG = E // EG
TOPK = 4
CAP = 128
HS = 512
MS = HS // P
SCALE = 2.5
NQ = 8
EQ = E // NQ
SLOT_A = P // EQ
SLOT_B = CAP // SLOT_A
FILLED = ((0,), (1, 2), tuple(range(3, NQ)))
UQ = SLOT_B // 2
SENTINEL = -3.0e38
PICKED = 3.0e38
FAR = 512.0

NH = 16
HD = D // NH
TWO_ONES = float(np.array([0x3F803F80], np.uint32).view(np.float32)[0])
MASKED = -1.0e30

HID = 704
HID_TILES = [128, 128, 112, 112, 112, 112]
HID_AT = [sum(HID_TILES[:i]) for i in range(len(HID_TILES))]
NHID = len(HID_TILES)
ZERO_POINT = 128.0

MOE, RECUR, QFFN, ATTN = "moe", "recur", "qffn", "attn"
STAGES = [MOE, RECUR, MOE, QFFN, ATTN, QFFN]
LAST = len(STAGES)


class Counts:

    def __init__(self):
        self.values = {}
        self.sems = {}
        self.total = {}

    def start(self, make):
        self.make, self.sems, self.total = make, {}, {}

    def sem(self, name):
        if name not in self.sems:
            self.sems[name] = self.make(name)
        return self.sems[name]

    def mark(self, name, *which, by=1):
        self.total[name] = self.total.get(name, 0) + by
        self.values[(name, *which)] = self.total[name]
        return self.sem(name), by

    def at(self, name, *which):
        return self.sem(name), self.values.get((name, *which), 1)


def build(nc, a, counts):
    with ExitStack() as ctx:
        counts.start(lambda name: ctx.enter_context(nc.semaphore(name)))
        mark, at = counts.mark, counts.at

        def mark16(name, *which):
            return mark(name, *which, by=16)

        def sb(name, shape, dt=F32):
            return ctx.enter_context(nc.sbuf_tensor(name, shape, dt))

        x = sb("x", [P, NT, D])
        xn = sb("xn", [P, NT, D])
        xnT = sb("xnT", [P, KD, T])
        wa = sb("wa", [P, KD, D])
        wx = sb("wx", [P, KD, D])

        pools = ExitStack()

        def pool_sb(name, shape):
            return pools.enter_context(nc.sbuf_tensor(name, shape, F32))

        big = pool_sb("big", [P, 2, 8192])
        xt = pool_sb("xt", [P, 8192])
        rt = pool_sb("rt", [P, 4096])
        rg = pool_sb("rg", [P, 6144])
        sh = pool_sb("sh", [P, 4480])
        gs = pool_sb("gs", [P, 2304])

        up_w = big[:, 0, :].rearrange("p (k e h) -> p k e h", k=KD, e=E)
        down_w = big[:, 1, :].rearrange("p (e d) -> p e d", e=E)
        gate_w = gs[:, 0:KD * E].rearrange("p (k e) -> p k e", k=KD)
        sup_w = gs[:, 64:64 + KD * HS].rearrange("p (k h) -> p k h", k=KD)
        sdown_w = gs[:, 64 + KD * HS:64 + KD * HS + MS * D].rearrange("p (m d) -> p m d", m=MS)
        q_in = big[:, 0, :].bitcast(I32)
        wqkv = rt[:, 0:KD * 3 * D].rearrange("p (k h) -> p k h", k=KD)
        wout = rt[:, KD * 3 * D:KD * 4 * D].rearrange("p (k h) -> p k h", k=KD)

        pools.close()
        base = ExitStack()
        with base:
            hid_r = base.enter_context(nc.sbuf_tensor("hid_r", [P, 2, NHID, T], F32R))
            base.enter_context(nc.sbuf_tensor("pad_a", [P, 2 * 8192 - 2 * NHID * T], F32))
            xr_b = base.enter_context(nc.sbuf_tensor("xr_b", [P, 2, KD, T], F32R))
            base.enter_context(nc.sbuf_tensor("pad_c", [P, 8192 - 2 * KD * T + 4096], F32))
            xr_a = base.enter_context(nc.sbuf_tensor("xr_a", [P, 2, KD, T], F32R))
            base.enter_context(nc.sbuf_tensor("pad_b", [P, 6144 - 2 * KD * T], F32))
            qw = base.enter_context(nc.sbuf_tensor("qw", [P, 4480], F32R))
        again = [ctx.enter_context(nc.sbuf_tensor(f"pool{i}", [P, n], F32))
                 for i, n in enumerate((16384, 8192, 4096, 6144, 4480, 2304))]
        qg_w = qw[:, 0:KD * HID].rearrange("p (k h) -> p k h", k=KD)
        qu_w = qw[:, KD * HID:2 * KD * HID].rearrange("p (k h) -> p k h", k=KD)
        qd_w = qw[:, 2 * KD * HID:2 * KD * HID + NHID * D].rearrange("p (m d) -> p m d", m=NHID)

        ident = sb("ident", [P, P])
        identb = sb("identb", [P, P], BF16)
        earlier = sb("earlier", [P, P], BF16)
        ones = sb("ones", [P, P], BF16)
        hide_qk = sb("hide_qk", [P, P], BF16)
        iota_a = sb("iota_a", [P, SLOT_A, EQ], F16)
        iota_b = sb("iota_b", [P, SLOT_B, E], F16)
        token_id = sb("token_id", [P, NT, E], F16)
        own_expert = sb("own_expert", [P, EQ])
        own_int = sb("own_int", [P, EQ], I32)
        row_base = sb("row_base", [P, E])
        minus_half = sb("minus_half", [P, TH])
        bias_corr = sb("bias_corr", [P, E])
        v_bias = sb("v_bias", [P, D])
        out_bias = sb("out_bias", [P, D])
        sd_row = sb("sd_row", [P, D])
        qk_bias = sb("qk_bias", [P, 2, KD])
        sg_col = sb("sg_col", [P, NHID])
        su_col = sb("su_col", [P, NHID])
        sg_half = sb("sg_half", [P, NHID])
        sgu_half = sb("sgu_half", [P, NHID])
        rec_in = sb("rec_in", [P, 3, KD])
        lam = sb("lam", [P, 12, KD])

        stats = sb("stats", [P, NT, 6])
        mv = sb("mv", [P, NT, 2])
        veps = sb("veps", [P, NT])
        rstd = sb("rstd", [P, NT])

        def rt_view(lo, n):
            return rt[:, lo:lo + n]

        scores = rt_view(0, 256).rearrange("p (j e) -> p j e", j=NT)
        corrected = rt_view(256, 256).rearrange("p (j e) -> p j e", j=NT)
        hi = rt_view(512, 128)
        lo = rt_view(640, 128)
        m1 = rt_view(768, 64)
        mh = rt_view(832, 64)
        ml = rt_view(896, 64)
        gscore = rt_view(960, NT * 12).rearrange("p (j g) -> p j g", j=NT)
        gpick = rt_view(1056, NT * 12).rearrange("p (j g) -> p j g", j=NT)
        top8 = rt_view(1152, 64).rearrange("p (j g) -> p j g", j=NT)
        gmask = rt_view(1216, 64).rearrange("p (j g) -> p j g", j=NT)
        masked = rt_view(1280, NT * 36).rearrange("p (j g) -> p j g", j=NT)
        epick = rt_view(1568, NT * 36).rearrange("p (j g) -> p j g", j=NT)
        used = rt_view(1856, 256).rearrange("p (j e) -> p j e", j=NT)
        wsum = rt_view(2112, 8)
        wrec = rt_view(2120, 8)
        weight = rt_view(2128, 256).rearrange("p (j e) -> p j e", j=NT)
        slot = rt_view(2384, 256).rearrange("p (j e) -> p j e", j=NT)
        slot_i = rt_view(2640, 256).bitcast(I32)
        slot_a = rt_view(2896, 128).bitcast(F16).rearrange("p (j e) -> p j e", j=NT)
        slot_b = rt_view(3024, 128).bitcast(F16).rearrange("p (j e) -> p j e", j=NT)
        part_i = rt_view(3152, 256).bitcast(I32)
        row_code = rt_view(3408, 256).rearrange("p (j e) -> p j e", j=NT)
        used_b = rt_view(3664, 128).bitcast(BF16).rearrange("p (j e) -> p j e", j=NT)
        from_token = rt_view(3792, 32).bitcast(I32)
        ye_row = rt_view(3824, 32).bitcast(I32)
        kweight = rt_view(3856, 32)
        is_a = xt[:, 0:4096].bitcast(F16).rearrange("p (q j a e) -> p q j a e", q=NQ, j=NT, a=SLOT_A)
        is_b = xt[:, 4096:4608].bitcast(F16).rearrange("p (j b e) -> p j b e", j=NT, b=SLOT_B)
        inv = xt[:, 4608:4736].rearrange("p (u e) -> p u e", e=EQ)
        inv_sum = xt[:, 4736:4768]
        ksel = xt[:, 5120:6144].rearrange("p (j k e) -> p j k e", j=NT, k=TOPK)
        xeT = [xt[:, q * 1024:(q + 1) * 1024].rearrange("p (k e b a) -> p k e b a", k=KD, e=EQ, b=SLOT_B)
               for q in range(NQ)]
        picked = xt[:, :].rearrange("p (j k d) -> p j k d", j=NT, k=TOPK)
        RING_XE = 8
        xe = rg[:, 0:2048].rearrange("p (r d) -> p r d", r=RING_XE)
        relu_e = rg[:, 2048:3072].rearrange("p (r c) -> p r c", r=2)
        hid_e = rg[:, 3072:4096].rearrange("p (r c) -> p r c", r=2)
        ye = rg[:, 4096:6144].rearrange("p (r e d) -> p r e d", r=2, e=4)
        relu_s = sb("relu_s", [P, 2, SEQ])
        hid_s = sh[:, 0:MS * T].rearrange("p (m t) -> p m t", m=MS)

        decay = rg[:, 0:2048].rearrange("p (m t) -> p m t", m=KD)
        drive = rg[:, 2048:4096].rearrange("p (m t) -> p m t", m=KD)
        state = rg[:, 4096:6144].rearrange("p (m t) -> p m t", m=KD)

        tanh_q = relu_s
        xr = {3: xr_a, 5: xr_b}
        gated = {n: w[:, 4096:5120].rearrange("p (r t) -> p r t", r=2) for n, w in ((3, rg), (5, xt))}
        hid32 = {n: w[:, 5120:6144].rearrange("p (r t) -> p r t", r=2) for n, w in ((3, rg), (5, xt))}
        scaled = gs[:, 0:512].rearrange("p (j d) -> p j d", j=2)

        HG = 4
        NG = NB * NH // HG
        MAX_UNITS = [(3, 0, 2), (3, 2, 2), (2, 0, 2), (2, 2, 2), (1, 0, 4), (0, 0, 4)]
        NMU = len(MAX_UNITS)
        Q, K = 0, 1
        stack = [big[:, i, :].bitcast(BF16).rearrange("p (h t) -> p h t", h=NH) for i in range(2)]
        RUNS = [[(0, 0, 3), (3, 0, 1), (4, 0, 2)], [(0, 0, 2), (2, 0, 3), (5, 0, 1)]]
        KS = 6 * HD
        parts = [xt[:, i * 3072:(i + 1) * 3072].bitcast(BF16)
                 .rearrange("p (m s t) -> p m s t", m=KD, s=3) for i in range(2)]
        qk_f = rt[:, 2048:4096].rearrange("p (r t) -> p r t", r=4)
        VW = HD + 1
        VROW = NH * VW + 16
        val = gs[:, 0:NT * VROW].rearrange("p (j c) -> p j c", j=NT)
        smax = sb("smax", [P, 2, TH, HG])
        smax_r = sb("smax_r", [P, TH, HG])
        smax_p = sb("smax_p", [P, 2, TH, 3, HG], BF16)
        smax_t = sb("smax_t", [3 * HG, 2, SEQ], BF16)
        PAIRS = 3
        ctx_u = [w[:].rearrange("p k d -> p (k d)") for w in (wa, wx)]

        def prob(pair, c):
            r = pair % PAIRS
            if r == 2 and c < 4:
                return xt[:, 6144 + c * SEQ:6144 + (c + 1) * SEQ]
            at_ = 5120 if r == 2 else (5 * r + c) * SEQ
            return rg[:, at_:at_ + SEQ]
        den = sb("den", [P, 2, TH, HG])
        ctx_n = xn

        xn_dram = [nc.dram_tensor(f"xn_dram{i}", [T, D], F32).ap() for i in range(2)]
        ye_dram = [nc.dram_tensor(f"ye_dram{i}", [E * CAP, D], F32).ap() for i in range(2)]
        part_dram = nc.dram_tensor("part_dram", [2, NH, 3, HD, T], BF16).ap()
        smax_dram = nc.dram_tensor("smax_dram", [NG, 3 * HG, SEQ], BF16).ap()

        ps = ctx.enter_context(nc.psum_tensor("ps", [P, 8, 512], F32))

        out_v = a["out"].rearrange("b (j p) d -> p (b j) d", p=P)
        x_v = a["x"].rearrange("b (j p) d -> p (b j) d", p=P)

        moe_at = {0: 0, 2: 1}

        def xeT_src(u, k):
            return ps[:, u % 2, :].rearrange("p (b k a e) -> p b k a e", b=2, k=KD, a=SLOT_A)[:, :, k, :, :]

        def xeT_dst(u, k):
            q, b2 = divmod(u, UQ)
            return xeT[q][:, k, :, 2 * b2:2 * b2 + 2, :].rearrange("p e b a -> p b a e")

        def max_view(u, qt):
            two = ps[:, 2 * (u % 2):2 * (u % 2) + 2, :]
            if qt == 2:
                return two[:, :, 0:3 * P]
            if qt == 0:
                return two[:, 0, :].rearrange("p (h w) -> p h w", w=P)
            return two.rearrange("p b c -> p (b c)").rearrange("p (h w) -> p h w", w=(qt + 1) * P)

        smax_bank = ps[0:3 * HG, 7, 0:SEQ // 2].bitcast(BF16)
        OUT_BANK = (2, 3, 6, 7)
        SCHEDULE = "MEEWMEWTEMWEWMECEMEEME"
        EARLY, EARLY_AT = 2, 7
        LAG = 2
        PIECES = [[(0, 0, 0)], [(0, 1, 0), (0, 3, 384)], [(0, 2, 0), (1, 2, 256)],
                  [(1, 0, 0)], [(1, 1, 0), (1, 3, 384)]]
        PLACE = {(hh, kt): (c, col) for c, piece in enumerate(PIECES) for hh, kt, col in piece}

        DVE_LOWS = 2

        def hid_lo(n, u):
            return "hid_lo_dve" if n == 3 and u < DVE_LOWS else "hid_lo"

        block = ctx.enter_context(nc.Block())

        @block.sync
        def _(sp):
            for j in range(NT):
                sp.dma_start(x[:, j, :], x_v[:, j, :]).then_inc(*mark16(f"x_in{j}"))
            sp.dma_start(bias_corr[:], a["bias_corr"].partition_broadcast(P)).then_inc(*mark16("bias_in"))
            sp.dma_start(gate_w, a["gate"]).then_inc(*mark16("gate_in"))
            sp.dma_start(sup_w, a["sup"]).then_inc(*mark16("sup_in"))

            def expert_inputs(n):
                xn_rows = xn_dram[moe_at[n]].rearrange("(j p) d -> p j d", p=P)
                for h in range(NB):
                    sp.wait_ge(*at("xn", n, TH * h + TH - 1))
                    sp.dma_start(xn_rows[:, TH * h:TH * h + TH, :], xn[:, TH * h:TH * h + TH, :])\
                        .then_inc(*mark16(f"xn_out{h}", n))

            expert_inputs(0)
            sp.dma_start(sdown_w, a["sdown"]).then_inc(*mark16("sdown_in"))
            def small_inputs():
                for i, name in enumerate(("ba", "bx", "lam")):
                    sp.dma_start(rec_in[:, i, :], a[name]).then_inc(*mark16("rec_in"))
                sp.dma_start(wa[:], a["wa"]).then_inc(*mark16("wa_in"))
                sp.dma_start(wx[:], a["wx"]).then_inc(*mark16("wx_in"))
                for w, name in ((v_bias, "bv"), (out_bias, "bout"), (sd_row, "s_down")):
                    sp.dma_start(w[:], a[name].partition_broadcast(P)).then_inc(*mark16("rows_in"))
                for i, name in enumerate(("bq", "bk")):
                    sp.dma_start(qk_bias[:, i, :], a[name]).then_inc(*mark16("qkb_in"))
                for m, (r0, n) in enumerate(zip(HID_AT, HID_TILES)):
                    sp.dma_start(sg_col[0:n, m:m + 1], a["s_gate"][r0:r0 + n, :]).then_inc(*mark16("scol_in"))
                    sp.dma_start(su_col[0:n, m:m + 1], a["s_up"][r0:r0 + n, :]).then_inc(*mark16("scol_in"))

            for i in range(8):
                q, (name, w) = i // 2, (("up", up_w), ("down", down_w))[i % 2]
                if i == 5:
                    small_inputs()
                if i >= 5:
                    sp.wait_ge(*at("up_e", 0, i - 5))
                if name == "up":
                    sp.dma_start(up_w[:, :, 8 * q:8 * q + 8, :], a["up"][:, :, 8 * q:8 * q + 8, :])\
                        .then_inc(*mark16(f"up_in{q}"))
                else:
                    sp.dma_start(down_w[:, 8 * q:8 * q + 8, :], a["down"][:, 8 * q:8 * q + 8, :])\
                        .then_inc(*mark16(f"down_in{q}"))
            def expert_stores(n):
                ye_rows = ye_dram[moe_at[n]].rearrange("(e c) d -> c e d", c=CAP)
                for g in range(E // 4):
                    sp.wait_ge(*at("ye", n, g, 1))
                    sp.dma_start(ye_rows[:, 4 * g:4 * g + 4, :], ye[:, g % 2, :, :])\
                        .then_inc(*mark16(f"ye_out{g % 2}", n, g))

            expert_stores(0)
            expert_inputs(2)
            expert_stores(2)
            sp.wait_ge(*at("down_e", 2, E // 2 - 1))
            sp.dma_start(q_in[:, 0:KD * HID].rearrange("p (k h) -> p k h", k=KD), a["wq_gate"])\
                .then_inc(*mark16("qg_in"))
            sp.dma_start(q_in[:, KD * HID:2 * KD * HID].rearrange("p (k h) -> p k h", k=KD), a["wq_up"])\
                .then_inc(*mark16("qu_in"))
            for m, (r0, w) in enumerate(zip(HID_AT, HID_TILES)):
                c = 2 * KD * HID + m * D
                sp.dma_start(q_in[0:w, c:c + D], a["wq_down"][r0:r0 + w, :]).then_inc(*mark16("qd_in"))
            sp.wait_ge(*at("x", 3, NT - 1))
            sp.dma_start(wqkv, a["wqkv"]).then_inc(*mark16("wqkv_in"))
            sp.dma_start(wout, a["wout"]).then_inc(*mark16("wout_in"))

            def stack_rows(c):
                b, m = divmod(c, KD)
                tok = slice(b * SEQ, (b + 1) * SEQ)
                heads = slice(8 * m, 8 * m + 8)
                for i in (Q, K):
                    sp.wait_ge(*at("qk_parts", 2 * c + i))
                    for s in range(3):
                        sp.dma_start(part_dram[i, heads, s, :, tok], parts[i][:, m, s, tok])\
                            .then_inc(*mark16(f"part_out{c}{i}"))
                for i in (Q, K):
                    sp.wait_ge(*at(f"part_out{c}{i}"))
                    if c == 0:
                        sp.wait_ge(*at("x", 4, NT - 1))
                    for s, part, count in RUNS[i]:
                        sp.dma_start(stack[i][s * HD:(s + count) * HD, heads, tok],
                                     part_dram[i, heads, part:part + count, :, tok].rearrange("h s r t -> (s r) h t"))\
                            .then_inc(*mark16(f"stack_in{c}{i}"))

            def maxima_rows(gr):
                b, h0 = gr * HG // NH, gr * HG % NH
                sp.wait_ge(*at("smax_t", gr))
                sp.dma_start(smax_dram[gr], smax_t[:, gr % 2, :]).then_inc(*mark16(f"smax_out{gr % 2}", gr))
                sp.wait_ge(*at(f"smax_out{gr % 2}", gr))
                sp.dma_start(stack[Q][KS:KS + 3, h0:h0 + HG, b * SEQ:(b + 1) * SEQ],
                             smax_dram[gr].rearrange("(s h) t -> s h t", s=3)).then_inc(*mark16(f"smax_in{gr % 2}", gr))

            stack_rows(0)
            stack_rows(1)
            for gr in range(NG):
                maxima_rows(gr)
                if gr + 2 < NB * KD:
                    stack_rows(gr + 2)

            for j in range(NT):
                sp.wait_ge(*at("x", LAST, j))
                sp.dma_start(out_v[:, j, :], x[:, j, :]).then_inc(*mark16("out"))
            sp.wait_ge(*at("out"))

        @block.gpsimd
        def _(pool):
            g = nc.gpsimd

            def triangle(dst, cmp, mult, step, fill):
                g.affine_select(out=dst, in_=dst, compare_op=cmp, fill=fill, base=0,
                                pattern=[[step, P]], channel_multiplier=mult).then_inc(*mark("const"))

            g.memset(ident[:], 0.0).then_inc(*mark("cleared"))
            g.memset(identb[:], 0.0).then_inc(*mark("cleared"))
            g.memset(earlier[:], 1.0).then_inc(*mark("cleared"))
            g.memset(hide_qk[:], 0.0).then_inc(*mark("cleared"))
            g.memset(minus_half[:], -0.5).then_inc(*mark("cleared"))
            g.memset(ones[:], 1.0).then_inc(*mark("const"))
            pool.wait_ge(*at("cleared"))
            triangle(ident[:], ALU.not_equal, 1, -1, 1.0)
            g.affine_select(out=identb[:], in_=identb[:], compare_op=ALU.not_equal, fill=1.0, base=0,
                            pattern=[[-1, P]], channel_multiplier=1).then_inc(*mark("const", "ident"))
            triangle(earlier[:], ALU.is_gt, -1, 1, 0.0)
            triangle(hide_qk[:], ALU.is_ge, 1, -1, MASKED)
            g.iota(own_int[:], pattern=[[-1, EQ]], base=0, channel_multiplier=1).then_inc(*mark("own_int"))
            g.iota(iota_a[:], pattern=[[1, SLOT_A], [0, EQ]], base=0, channel_multiplier=0,
                   allow_small_or_imprecise_dtypes=True).then_inc(*mark("const"))
            g.iota(iota_b[:], pattern=[[1, SLOT_B], [0, E]], base=0, channel_multiplier=0,
                   allow_small_or_imprecise_dtypes=True).then_inc(*mark("const"))
            g.iota(token_id[:], pattern=[[P, NT], [0, E]], base=0, channel_multiplier=1,
                   allow_small_or_imprecise_dtypes=True).then_inc(*mark("const"))
            g.iota(row_base[:], pattern=[[-CAP, E]], base=E * CAP, channel_multiplier=0,
                   allow_small_or_imprecise_dtypes=True).then_inc(*mark("const"))

            def rstd_half(n, h):
                pool.wait_ge(*at("veps", n, h))
                g.tensor_tensor(rstd[:, TH * h:TH * h + TH], veps[:, TH * h:TH * h + TH], minus_half[:],
                                ALU.pow).then_inc(*mark("rstd", n, h))

            def square_shared(n, first, end):
                for u in range(first, end):
                    h, m = divmod(u, MS)
                    pool.wait_ge(*at("relu_s", n, u))
                    r = relu_s[:, u % 2, :]
                    g.tensor_tensor(hid_s[:, m, h * SEQ:(h + 1) * SEQ], r, r, ALU.mult)\
                        .then_inc(*mark("hid_s", n, u))

            def gathers(n):
                f = moe_at[n]
                for h in range(NB):
                    pool.wait_ge(*at(f"xn_out{h}", n))
                for u in range(NQ * SLOT_B):
                    if u == SLOT_B * FILLED[-1][0]:
                        square_shared(n, NB * MS - 2, NB * MS)
                    for part, filled in enumerate(FILLED):
                        if u == SLOT_B * filled[0]:
                            pool.wait_ge(*at("from_token", n, part))
                    if u >= RING_XE:
                        pool.wait_ge(*at("xe_t", n, (u - RING_XE) // 2))
                    elif n == 2:
                        pool.wait_ge(*at("state", NB * KD - 1))
                    g.indirect_dma_start(xe[:, u % RING_XE, :], None, xn_dram[f][:, :],
                                         bass.IndirectOffsetOnAxis(ap=from_token[:, u:u + 1], axis=0))\
                        .then_inc(*mark16(f"xe{u % RING_XE}", n, u))
                for g8 in range(E // 4 - 2, E // 4):
                    pool.wait_ge(*at(f"ye_out{g8 % 2}", n, g8))
                pool.wait_ge(*at("up_e", n, E // 4 - 1))
                pool.wait_ge(*at("kweight", n))
                for j in range(NT):
                    for k in range(TOPK):
                        i = j * TOPK + k
                        g.indirect_dma_start(picked[:, j, k, :], None, ye_dram[f][:, :],
                                             bass.IndirectOffsetOnAxis(ap=ye_row[:, i:i + 1], axis=0))\
                            .then_inc(*mark16(f"picked{j}", n))
                    if j == TH + 1:
                        rstd_half(n + 1, 0)

            def q_low(n):
                for u in range(DVE_LOWS if n == 3 else 0, NB * NHID):
                    b, m = divmod(u, NHID)
                    w = HID_TILES[m]
                    tok = slice(b * SEQ, (b + 1) * SEQ)
                    pool.wait_ge(*at("hid_hi", n, u))
                    g.tensor_tensor(hid_r[0:w, 1, m, tok], hid32[n][0:w, u % 2, :], hid_r[0:w, 0, m, tok].bitcast(F32),
                                    ALU.subtract).then_inc(*mark(hid_lo(n, u), n, u))
                    if n == 5 and u == 1:
                        pool.wait_ge(*at("hid_lo", n, u))
                        rstd_half(n, 1)
                    if n + 1 < LAST and u == NB * NHID - 1:
                        rstd_half(n + 1, 0)

            rstd_half(0, 0)
            rstd_half(0, 1)
            square_shared(0, 0, NB * MS - 2)
            gathers(0)
            rstd_half(1, 1)
            rstd_half(2, 0)
            rstd_half(2, 1)
            square_shared(2, 0, NB * MS - 2)
            gathers(2)
            rstd_half(3, 1)
            q_low(3)
            pool.wait_ge(*at("hid_lo", 3, NB * NHID - 1))
            rstd_half(4, 1)
            pool.wait_ge(*at("rstd", 4, 1))
            for u in range(NB * 2 * KD):
                b, m, i = u // 4, u // 2 % 2, u % 2
                tok = slice(b * SEQ, (b + 1) * SEQ)
                pool.wait_ge(*at("qk_p1", u))
                g.tensor_tensor(parts[i][:, m, 2, tok], qk_f[:, u % 4, :], parts[i][:, m, 1, tok], ALU.subtract)\
                    .then_inc(*mark("qk_parts", u))
            pool.wait_ge(*at("qk_parts", NB * 2 * KD - 1))
            pool.wait_ge(*at("x", 4, NT - 1))
            g.memset(big[KS:KS + 3, K, :], TWO_ONES).then_inc(*mark("k_ones"))
            pool.wait_ge(*at("k_ones"))
            pool.wait_ge(*at("rows_in"))
            for j in range(NT):
                pool.wait_ge(*at("xn", 4, j))
                g.tensor_tensor(x[:, j, :], x[:, j, :], out_bias[:], ALU.add).then_inc(*mark("x_bias", j))
            for pair in range(NB * NH // 2):
                for c in range(5):
                    u = pair * 5 + c
                    pool.wait_ge(*at("prob", u))
                    piece = prob(pair, c)
                    for col in [col for _, _, col in PIECES[c]]:
                        block_ = piece[:, col:col + P]
                        ins = g.affine_select(out=block_, in_=block_, compare_op=ALU.is_ge, fill=0.0, base=0,
                                              pattern=[[1, P]], channel_multiplier=-1)
                    ins.then_inc(*mark("causal", u))
                if pair == 2 * NG - 3:
                    rstd_half(5, 0)
            q_low(5)

        @block.scalar
        def _(act):
            s = nc.scalar

            def evac_xnT(n, b):
                for u in (2 * b, 2 * b + 1):
                    act.wait_ge(*at("tr", n, u))
                    src = ps[:, u % 2, :].rearrange("p (k t) -> p k t", k=KD)
                    s.activation(xnT[:, :, u * 256:(u + 1) * 256], src, ACT.Copy).then_inc(*mark("xnT", n, u))

            def evac_ye(n, g):
                for q in range(2):
                    u = 2 * g + q
                    act.wait_ge(*at("down_e", n, u))
                    if g >= 2:
                        act.wait_ge(*at(f"ye_out{g % 2}", n, g - 2))
                    s.activation(ye[:, g % 2, 2 * q:2 * q + 2, :],
                                 ps[:, 5 + u % 3, :].rearrange("p (e d) -> p e d", e=2), ACT.Copy)\
                        .then_inc(*mark("ye", n, g, q))

            def expert_layer(n):
                def shared_relu(u):
                    act.wait_ge(*at("up_s", n, u))
                    if u >= 2:
                        act.wait_ge(*at("hid_s", n, u - 2))
                    s.activation(relu_s[:, u % 2, :], ps[:, 3 + u % 3, :], ACT.Relu)\
                        .then_inc(*mark("relu_s", n, u))

                evac_xnT(n, 0)
                if n == 2:
                    shared_relu(0)
                    shared_relu(1)
                evac_xnT(n, 1)
                act.wait_ge(*at("logits", n))
                s.activation(scores, ps[:, 2, 0:NT * E].rearrange("p (j e) -> p j e", j=NT), ACT.Tanh,
                             scale=0.5).then_inc(*mark("tanh_s", n))
                for u in range(2 if n == 2 else 0, NB * MS):
                    shared_relu(u)

                def evac_xeT(u):
                    act.wait_ge(*at("xe_t", n, u))
                    for k in range(KD):
                        s.activation(xeT_dst(u, k), xeT_src(u, k), ACT.Copy).then_inc(*mark("xeT_act", n, u, k))

                for u in range(0, UQ, 2):
                    evac_xeT(u)
                for g in range(E // 4):
                    if g == 2:
                        act.wait_ge(*at("from_token", n, len(FILLED) - 1))
                        act.wait_ge(*at("kweight", n))
                    act.wait_ge(*at("up_e", n, g))
                    if g >= 2:
                        act.wait_ge(*at("hid_e", n, g - 2))
                    s.activation(relu_e[:, g % 2, :], ps[:, 3 + g % 2, :], ACT.Relu)\
                        .then_inc(*mark("relu_e", n, g))
                    if UQ + 2 * g < NQ * UQ:
                        evac_xeT(UQ + 2 * g)
                    if g:
                        evac_ye(n, g - 1)
                evac_ye(n, E // 4 - 1)

            expert_layer(0)

            act.wait_ge(*at("rec_in"))
            s.activation(lam[:, 0, :], rec_in[:, 2, :], ACT.Abs).then_inc(*mark("lam_act", 0))
            act.wait_ge(*at("lam_act", 0))
            s.activation(lam[:, 1, :], lam[:, 0, :], ACT.Exp, scale=-1.0).then_inc(*mark("lam_act", 1))
            s.activation(lam[:, 2, :], rec_in[:, 2, :], ACT.Relu, scale=-1.0).then_inc(*mark("lam_act", 2))


            for b in range(NB):
                evac_xnT(1, b)
                tok = slice(b * SEQ, (b + 1) * SEQ)
                if b == 0:
                    act.wait_ge(*at("rec_vec"))
                    for g8 in range(E // 4 - 2, E // 4):
                        act.wait_ge(*at(f"ye_out{g8 % 2}", 0, g8))
                for m in range(KD):
                    u = KD * b + m
                    act.wait_ge(*at("proj_r", u))
                    s.activation(decay[:, m, tok], ps[:, 2 + 2 * (u % 2), :], ACT.Tanh, scale=0.5,
                                 bias=lam[:, 8, m:m + 1]).then_inc(*mark("tanh_r", u))
                    act.wait_ge(*at("proj_i", u))
                    s.activation(drive[:, m, tok], ps[:, 3 + 2 * (u % 2), :], ACT.Tanh, scale=0.5,
                                 bias=lam[:, 9, m:m + 1]).then_inc(*mark("tanh_i", u))
                    act.wait_ge(*at("tanh_r", u))
                    s.activation(decay[:, m, tok], decay[:, m, tok], ACT.Exp, scale=lam[:, 10, m:m + 1],
                                 bias=lam[:, 10, m:m + 1]).then_inc(*mark("decay", u))
                    act.wait_ge(*at("decay", u))
                    s.activation(state[:, m, tok], decay[:, m, tok], ACT.Square).then_inc(*mark("decay2", u))
                for m in range(KD):
                    u = KD * b + m
                    act.wait_ge(*at("decay2", u))
                    s.activation(state[:, m, tok], state[:, m, tok], ACT.Sqrt, scale=-1.0, bias=1.0)\
                        .then_inc(*mark("gain", u))

            expert_layer(2)

            def x_high(n, u):
                act.wait_ge(*at("tr", n, u))
                s.activation(xr[n][:, 0, :, u * 256:(u + 1) * 256],
                             ps[:, u % 2, :].rearrange("p (k t) -> p k t", k=KD), ACT.Copy)\
                    .then_inc(*mark("x_hi", n, u))

            def quantised(n, evac_ctx=None, evac_ctxT=None):
                def hid_high(u):
                    b, m = divmod(u, NHID)
                    w = HID_TILES[m]
                    act.wait_ge(*at("hid32", n, u))
                    s.activation(hid_r[0:w, 0, m, b * SEQ:(b + 1) * SEQ], hid32[n][0:w, u % 2, :], ACT.Copy)\
                        .then_inc(*mark("hid_hi", n, u))

                act.wait_ge(*at("scol"))
                if n == 3:
                    x_high(n, 0)
                    x_high(n, 1)
                for b in range(NB):
                    for u in range(b * NHID, (b + 1) * NHID):
                        w = HID_TILES[u % NHID]
                        act.wait_ge(*at("q_gate", n, u))
                        if u >= 2:
                            act.wait_ge(*at("gated", n, u - 2))
                        s.activation(tanh_q[0:w, u % 2, :], ps[0:w, 2 + 2 * (u % 2), :], ACT.Tanh,
                                     scale=sg_half[0:w, u % NHID:u % NHID + 1]).then_inc(*mark("tanh_q", n, u))
                        if n == 5 and u == 0:
                            evac_ctx(NG - 1)
                        if u % NHID:
                            hid_high(u - 1)
                        if n == 5 and u == 1:
                            evac_ctxT(1)
                    if b == 0:
                        x_high(n, 2)
                        x_high(n, 3)
                    hid_high((b + 1) * NHID - 1)

            quantised(3)

            act.wait_ge(*at("qkb"))
            for u in range(NB * 2 * KD):
                if u % (2 * KD) == 0:
                    evac_xnT(4, u // (2 * KD))
                b, m, i = u // 4, u // 2 % 2, u % 2
                act.wait_ge(*at("proj_qk", u))
                if u >= 4:
                    act.wait_ge(*at("qk_parts", u - 4))
                s.activation(qk_f[:, u % 4, :], ps[:, 4 + u % 2, :], ACT.Identity,
                             scale=(0.25 if i == Q else 1.0), bias=qk_bias[:, i, m:m + 1])\
                    .then_inc(*mark("qk_f", u))
                act.wait_ge(*at("qk_f", u))
                s.activation(parts[i][:, m, 0, b * SEQ:(b + 1) * SEQ], qk_f[:, u % 4, :], ACT.Copy)\
                    .then_inc(*mark("qk_p0", u))

            def evac_ctx(gr):
                act.wait_ge(*at("pv", gr))
                if gr >= 2:
                    act.wait_ge(*at("ctx_mm", gr - 2))
                s.activation(ctx_u[gr % 2], ps[:, 6, :], ACT.Copy).then_inc(*mark("ctx_u", gr))

            def evac_ctxT(b):
                for u in (2 * b, 2 * b + 1):
                    act.wait_ge(*at("ctx_tr", u))
                    src = ps[:, u % 2, :].rearrange("p (k t) -> p k t", k=KD)
                    s.activation(xnT[:, :, u * 256:(u + 1) * 256], src, ACT.Copy).then_inc(*mark("ctxT", u))

            for pair in range(NB * NH // 2):
                for c in range(5):
                    u = pair * 5 + c
                    act.wait_ge(*at("st", u))
                    if pair >= PAIRS:
                        act.wait_ge(*at("pv", (pair - PAIRS) // 2))
                    s.activation(prob(pair, c), ps[:, 4 + u % 2, :], ACT.Exp)\
                        .then_inc(*mark("prob", u))
                    if c == 3 and pair % 2 == 0 and pair:
                        evac_ctx(pair // 2 - 1)
                    if c == 1 and pair == 2 * (NG - LAG):
                        evac_ctxT(0)
                    if c == 2 and pair == 2 * (NG - 1):
                        x_high(5, 0)
                        x_high(5, 1)
            quantised(5, evac_ctx, evac_ctxT)

        @block.vector
        def _(dve):
            v = nc.vector
            links = [0]

            def link(ins):
                links[0] += 1
                ins.then_inc(*mark("dve_step"))
                dve.wait_ge(counts.sem("dve_step"), links[0])

            def tile_stats(n, j):
                dve.wait_ge(*(at("x", n, j) if n else at(f"x_in{j}")))
                v.bn_stats(stats[:, j, :], x[:, j, :]).then_inc(*mark("stats", n, j))

            def ln_stats(n, h, done=0):
                for j in range(TH * h + done, TH * h + TH):
                    tile_stats(n, j)
                dve.wait_ge(*at("stats", n, TH * h + TH - 1))
                for j in range(TH * h, TH * h + TH):
                    last = v.bn_aggr(mv[:, j, :], stats[:, j, :])
                link(last)
                half = slice(TH * h, TH * h + TH)
                v.tensor_scalar(veps[:, half], mv[:, half, 1], EPS, None, ALU.add).then_inc(*mark("veps", n, h))

            def ln_norm(n, h):
                dve.wait_ge(*at("rstd", n, h))
                if n - 1 in moe_at:
                    dve.wait_ge(*at(f"xn_out{h}", n - 1))
                if n == 5:
                    dve.wait_ge(*at("ctx_tr", 2 * h + 1))
                for j in range(TH * h, TH * h + TH):
                    v.tensor_scalar(xn[:, j, :], x[:, j, :], mv[:, j, 0:1], rstd[:, j:j + 1],
                                    ALU.subtract, ALU.mult).then_inc(*mark("xn", n, j))

            def route(n):
                dve.wait_ge(*at("tanh_s", n))
                link(v.tensor_scalar(scores, scores, 0.5, 0.5, ALU.mult, ALU.add))
                dve.wait_ge(*at("bias_in"))
                link(v.tensor_tensor(corrected, scores, bias_corr[:].unsqueeze(1).to_broadcast([P, NT, E]), ALU.add))
                pairs = corrected.rearrange("p j (g q) -> p (j g) q", q=2)
                v.tensor_tensor(hi, pairs[:, :, 0], pairs[:, :, 1], ALU.max)
                link(v.tensor_tensor(lo, pairs[:, :, 0], pairs[:, :, 1], ALU.min))
                hi2 = hi.rearrange("p (g q) -> p g q", q=2)
                lo2 = lo.rearrange("p (g q) -> p g q", q=2)
                v.tensor_tensor(m1, hi2[:, :, 0], hi2[:, :, 1], ALU.max)
                v.tensor_tensor(mh, hi2[:, :, 0], hi2[:, :, 1], ALU.min)
                link(v.tensor_tensor(ml, lo2[:, :, 0], lo2[:, :, 1], ALU.max))
                link(v.tensor_tensor(mh, mh, ml, ALU.max))
                v.memset(gscore[:, :, EG:12], SENTINEL)
                link(v.tensor_tensor(gscore[:, :, 0:EG], m1.rearrange("p (j g) -> p j g", j=NT),
                                     mh.rearrange("p (j g) -> p j g", j=NT), ALU.add))
                for j in range(NT):
                    last = v.max(top8[:, j, :], gscore[:, j, 0:EG])
                link(last)
                link(v.memset(top8[:, :, TOPK:8], SENTINEL))
                for j in range(NT):
                    last = v.match_replace(gpick[:, j, :], top8[:, j, :], gscore[:, j, :], PICKED)
                link(last)
                link(v.tensor_scalar(gmask, gpick[:, :, 0:EG], PICKED, None, ALU.is_equal))
                v.memset(masked[:, :, E:36], SENTINEL)
                link(v.tensor_tensor(masked[:, :, 0:E].rearrange("p j (g q) -> p j g q", q=EPG),
                                     corrected.rearrange("p j (g q) -> p j g q", q=EPG),
                                     gmask.unsqueeze(3).to_broadcast([P, NT, EG, EPG]), ALU.mult))
                for j in range(NT):
                    last = v.max(top8[:, j, :], masked[:, j, 0:E])
                link(last)
                link(v.memset(top8[:, :, TOPK:8], SENTINEL))
                for j in range(NT):
                    last = v.match_replace(epick[:, j, :], top8[:, j, :], masked[:, j, :], PICKED)
                link(last)
                v.tensor_scalar(used_b, epick[:, :, 0:E], PICKED, None, ALU.is_equal).then_inc(*mark("used_b", n))
                link(v.tensor_scalar(used, epick[:, :, 0:E], PICKED, None, ALU.is_equal))
                link(v.tensor_tensor(weight, used, scores, ALU.mult))
                link(v.tensor_reduce(wsum, weight, AX.X, ALU.add))
                link(v.tensor_scalar(wsum, wsum, 1e-20, None, ALU.add))
                link(v.reciprocal(wrec, wsum))
                link(v.tensor_scalar(wrec, wrec, 0.5 * SCALE, None, ALU.mult))
                v.tensor_tensor(weight, weight, wrec.unsqueeze(2).to_broadcast([P, NT, E]), ALU.mult)
                link(v.tensor_scalar(row_code, used, -FAR, FAR, ALU.mult, ALU.add))
                dve.wait_ge(*at("pos", n))
                v.tensor_tensor(slot, ps[:, 2, 0:NT * E].rearrange("p (j e) -> p j e", j=NT), row_code, ALU.add)\
                    .then_inc(*mark("slot", n))
                dve.wait_ge(*at("slot", n))
                link(v.tensor_copy(slot_i, slot.rearrange("p j e -> p (j e)")))
                link(v.tensor_scalar(part_i, slot_i, SLOT_A - 1, None, ALU.bitwise_and))
                v.tensor_copy(slot_a, part_i.rearrange("p (j e) -> p j e", j=NT))
                link(v.tensor_scalar(slot_i, slot_i, SLOT_A.bit_length() - 1, None, ALU.logical_shift_right))
                link(v.tensor_copy(slot_b, slot_i.rearrange("p (j e) -> p j e", j=NT)))

                def onehots(part):
                    for q in FILLED[part]:
                        own = slice(EQ * q, EQ * (q + 1))
                        shape = [P, NT, SLOT_A, EQ]
                        v.tensor_tensor(is_a[:, q], slot_a[:, :, own].unsqueeze(2).to_broadcast(shape),
                                        iota_a[:].unsqueeze(1).to_broadcast(shape), ALU.is_equal)
                    own = slice(EQ * FILLED[part][0], EQ * (FILLED[part][-1] + 1))
                    shape = [P, NT, SLOT_B, own.stop - own.start]
                    link(v.tensor_tensor(is_b[:, :, :, own], slot_b[:, :, own].unsqueeze(2).to_broadcast(shape),
                                         iota_b[:, :, own].unsqueeze(1).to_broadcast(shape), ALU.is_equal))
                    v.tensor_tensor(is_b[:, :, :, own], is_b[:, :, :, own],
                                    token_id[:, :, own].unsqueeze(2).to_broadcast(shape), ALU.mult)\
                        .then_inc(*mark("onehot", n, part))

                def inverse(part):
                    dve.wait_ge(*at("inv_mm", n, part))
                    u = slice(SLOT_B * FILLED[part][0], SLOT_B * (FILLED[part][-1] + 1))
                    count = u.stop - u.start
                    found = ps[:, 2, u.start * EQ:u.stop * EQ].rearrange("p (u e) -> p u e", e=EQ)
                    v.tensor_tensor(inv[:, u, :], found,
                                    own_expert[:].unsqueeze(1).to_broadcast([P, count, EQ]), ALU.mult)\
                        .then_inc(*mark("inv", n, part))
                    dve.wait_ge(*at("inv", n, part))
                    link(v.tensor_reduce(inv_sum[:, u], inv[:, u, :], AX.X, ALU.add))
                    v.tensor_copy(from_token[:, u], inv_sum[:, u]).then_inc(*mark("from_token", n, part))

                onehots(0)
                link(v.tensor_scalar(row_code, slot, CAP - 1.0, None, ALU.min))
                link(v.tensor_tensor(row_code, row_base[:].unsqueeze(1).to_broadcast([P, NT, E]), row_code,
                                     ALU.subtract))
                inverse(0)
                onehots(1)
                inverse(1)
                onehots(2)
                link(v.tensor_tensor(row_code, row_code, used, ALU.mult))
                for j in range(NT):
                    last = v.max(top8[:, j, :], row_code[:, j, :])
                link(last)
                link(v.tensor_scalar(slot, slot, float(CAP), None, ALU.is_lt))
                link(v.tensor_tensor(weight, weight, slot, ALU.mult))
                inverse(2)
                v.tensor_scalar(ye_row.rearrange("p (j k) -> p j k", j=NT), top8[:, :, 0:TOPK], -1.0,
                                float(E * CAP), ALU.mult, ALU.add)

            def kept_weights(n):
                link(v.tensor_tensor(ksel, row_code.unsqueeze(2).to_broadcast([P, NT, TOPK, E]),
                                     top8[:, :, 0:TOPK].unsqueeze(3).to_broadcast([P, NT, TOPK, E]), ALU.is_equal))
                link(v.tensor_tensor(ksel, ksel, weight.unsqueeze(2).to_broadcast([P, NT, TOPK, E]), ALU.mult))
                v.tensor_reduce(kweight.rearrange("p (j k) -> p j k", j=NT), ksel, AX.X, ALU.add)\
                    .then_inc(*mark("kweight", n))

            def expert_layer(n, between=None):
                route(n)

                def evac_xeT(u):
                    dve.wait_ge(*at("xe_t", n, u))
                    for k in range(KD):
                        v.tensor_copy(xeT_dst(u, k), xeT_src(u, k)).then_inc(*mark("xeT_dve", n, u, k))

                for u in range(1, UQ, 2):
                    evac_xeT(u)
                for g in range(E // 4):
                    if g == 1:
                        kept_weights(n)
                    dve.wait_ge(*at("relu_e", n, g))
                    if g >= 2:
                        dve.wait_ge(*at("down_e", n, 2 * (g - 2) + 1))
                    v.tensor_tensor(hid_e[:, g % 2, :], relu_e[:, g % 2, :], relu_e[:, g % 2, :], ALU.mult)\
                        .then_inc(*mark("hid_e", n, g))
                    if UQ + 2 * g < NQ * UQ:
                        evac_xeT(UQ + 2 * g + 1)
                if n == 0:
                    vectors()

                def shared_out(u):
                    dve.wait_ge(*at("down_s", n, u))
                    v.scalar_tensor_tensor(x[:, 2 * u:2 * u + 2, :],
                                           ps[:, 3 + u % 2, :].rearrange("p (j d) -> p j d", j=2),
                                           0.5, x[:, 2 * u:2 * u + 2, :], ALU.mult, ALU.add)\
                        .then_inc(*mark("shared_out", n, u))

                def combine(j):
                    dve.wait_ge(*at(f"picked{j}", n))
                    dve.wait_ge(*at("shared_out", n, j // 2))
                    if j == 0:
                        dve.wait_ge(*at("kweight", n))
                    for k in range(TOPK):
                        i = j * TOPK + k
                        last = v.scalar_tensor_tensor(x[:, j, :], picked[:, j, k, :], kweight[:, i:i + 1],
                                                      x[:, j, :], ALU.mult, ALU.add)
                        if k < TOPK - 1:
                            link(last)
                    last.then_inc(*mark("x", n + 1, j))
                    tile_stats(n + 1, j)

                shared_out(0)
                shared_out(1)
                for j in range(NT):
                    combine(j)
                    if j < 2:
                        shared_out(2 + j)
                    if n == 2 and 1 <= j < TH:
                        quantised_weights(j - 1)
                    if j == TH - 1:
                        ln_stats(n + 1, 0, TH)
                    if j == TH:
                        ln_norm(n + 1, 0)
                    if j >= TH and between:
                        between(j)
                ln_stats(n + 1, 1, TH)

            def quantised_weights(i):
                if i == 0:
                    dve.wait_ge(*at("shared_out", 2, NT // 2 - 1))
                if i < 2:
                    dve.wait_ge(*at(("qg_in", "qu_in")[i]))
                    part = slice(i * KD * HID, (i + 1) * KD * HID)
                    v.tensor_scalar(qw[:, part], q_in[:, part], -ZERO_POINT, None, ALU.add)\
                        .then_inc(*mark("q_weights"))
                else:
                    dve.wait_ge(*at("qd_in"))
                    for c0, n_, w in ((0, 2, 128), (2, 4, 112)):
                        part = slice(2 * KD * HID + c0 * D, 2 * KD * HID + (c0 + n_) * D)
                        v.tensor_scalar(qw[0:w, part], q_in[0:w, part], -ZERO_POINT, None, ALU.add)\
                            .then_inc(*mark("q_weights"))

            def vectors():
                dve.wait_ge(*at("rec_in"))
                v.tensor_scalar(lam[:, 8, :], rec_in[:, 0, :], 0.5, None, ALU.mult)
                v.tensor_scalar(lam[:, 9, :], rec_in[:, 1, :], 0.5, None, ALU.mult)
                dve.wait_ge(*at("lam_act", 2))
                link(v.tensor_scalar(lam[:, 3, :], lam[:, 1, :], 2.0, None, ALU.add))
                link(v.reciprocal(lam[:, 4, :], lam[:, 3, :]))
                link(v.tensor_tensor(lam[:, 5, :], lam[:, 1, :], lam[:, 4, :], ALU.mult))
                link(v.tensor_tensor(lam[:, 6, :], lam[:, 5, :], lam[:, 5, :], ALU.mult))
                link(v.tensor_scalar(lam[:, 7, :], lam[:, 6, :], 1.0 / 19.0, None, ALU.mult))
                for i in range(8, 0, -1):
                    link(v.scalar_tensor_tensor(lam[:, 7, :], lam[:, 7, :], 1.0 / (2 * i + 1), lam[:, 6, :],
                                                ALU.add, ALU.mult))
                link(v.scalar_tensor_tensor(lam[:, 7, :], lam[:, 7, :], 1.0, lam[:, 5, :], ALU.add, ALU.mult))
                link(v.scalar_tensor_tensor(lam[:, 11, :], lam[:, 7, :], 2.0, lam[:, 2, :], ALU.mult, ALU.add))
                v.tensor_scalar(lam[:, 10, :], lam[:, 11, :], -4.0, None, ALU.mult).then_inc(*mark("rec_vec"))

                dve.wait_ge(*at("rows_in"))
                v.tensor_scalar(sd_row[:], sd_row[:], 0.5, None, ALU.mult)
                dve.wait_ge(*at("qkb_in"))
                v.tensor_scalar(qk_bias[:, 0, :], qk_bias[:, 0, :], 0.25, None, ALU.mult).then_inc(*mark("qkb"))
                dve.wait_ge(*at("scol_in"))
                for w, c0, c1 in ((128, 0, 2), (112, 2, NHID)):
                    link(v.tensor_scalar(sg_half[0:w, c0:c1], sg_col[0:w, c0:c1], 0.5, None, ALU.mult))
                    v.tensor_tensor(sgu_half[0:w, c0:c1], sg_half[0:w, c0:c1], su_col[0:w, c0:c1], ALU.mult)\
                        .then_inc(*mark("scol"))

            dve.wait_ge(*at("own_int"))
            link(v.tensor_scalar(own_int[:], own_int[:], EQ - 1, None, ALU.bitwise_and))
            link(v.tensor_scalar(own_expert[:], own_int[:], 0, None, ALU.is_equal))
            ln_stats(0, 0)
            ln_stats(0, 1)
            ln_norm(0, 0)
            ln_norm(0, 1)

            def gate_input(u):
                b, m = divmod(u, KD)
                tok = slice(b * SEQ, (b + 1) * SEQ)
                dve.wait_ge(*at("tanh_i", u))
                v.scalar_tensor_tensor(drive[:, m, tok], drive[:, m, tok], 1.0, xnT[:, m, tok],
                                       ALU.add, ALU.mult).then_inc(*mark("drive0", u))

            def scan(b):
                for m in range(KD):
                    u = KD * b + m
                    tok = slice(b * SEQ, (b + 1) * SEQ)
                    dve.wait_ge(*at("gain", u))
                    dve.wait_ge(*at("drive0", u))
                    link(v.scalar_tensor_tensor(drive[:, m, tok], drive[:, m, tok], 0.5, state[:, m, tok],
                                                ALU.mult, ALU.mult))
                    v.tensor_tensor_scan(state[:, m, tok], decay[:, m, tok], drive[:, m, tok], 0.0,
                                         ALU.mult, ALU.add).then_inc(*mark("state", u))

            def recurred(b):
                for q in (2 * b, 2 * b + 1):
                    dve.wait_ge(*at("state_t", q))
                    for j in (2 * q, 2 * q + 1):
                        v.tensor_tensor(x[:, j, :], x[:, j, :], ps[:, 6 + q % 2, (j % 2) * D:(j % 2 + 1) * D],
                                        ALU.add).then_inc(*mark("x", 2, j))
                ln_stats(2, b)

            expert_layer(0)
            gate_input(0)
            ln_norm(1, 1)
            gate_input(1)
            scan(0)
            recurred(0)
            gate_input(2)
            gate_input(3)
            ln_norm(2, 0)
            scan(1)
            recurred(1)
            ln_norm(2, 1)

            def x_low(n, b):
                for u in (2 * b, 2 * b + 1):
                    dve.wait_ge(*at("x_hi", n, u))
                    tok = slice(u * 256, (u + 1) * 256)
                    v.tensor_tensor(xr[n][:, 1, :, tok], ps[:, u % 2, :].rearrange("p (k t) -> p k t", k=KD),
                                    xr[n][:, 0, :, tok].bitcast(F32), ALU.subtract).then_inc(*mark("x_lo", n, u))

            def hidden(n, u):
                b, m = divmod(u, NHID)
                w = HID_TILES[m]
                dve.wait_ge(*at("tanh_q", n, u))
                v.scalar_tensor_tensor(gated[n][0:w, u % 2, :], tanh_q[0:w, u % 2, :], 1.0,
                                       ps[0:w, 2 + 2 * (u % 2), :], ALU.add, ALU.mult)\
                    .then_inc(*mark("gated", n, u))
                dve.wait_ge(*at("q_up", n, u))
                dve.wait_ge(*at("gated", n, u))
                if u >= 2:
                    dve.wait_ge(*at(hid_lo(n, u - 2), n, u - 2))
                v.scalar_tensor_tensor(hid32[n][0:w, u % 2, :], ps[0:w, 3 + 2 * (u % 2), :],
                                       sgu_half[0:w, m:m + 1], gated[n][0:w, u % 2, :],
                                       ALU.mult, ALU.mult).then_inc(*mark("hid32", n, u))

            def hidden_low(n, u):
                b, m = divmod(u, NHID)
                w = HID_TILES[m]
                tok = slice(b * SEQ, (b + 1) * SEQ)
                dve.wait_ge(*at("hid_hi", n, u))
                v.tensor_tensor(hid_r[0:w, 1, m, tok], hid32[n][0:w, u % 2, :], hid_r[0:w, 0, m, tok].bitcast(F32),
                                ALU.subtract).then_inc(*mark(hid_lo(n, u), n, u))

            def quantised_out(n, q):
                dve.wait_ge(*at("q_down", n, q))
                if q:
                    dve.wait_ge(*at("x", n + 1, 2 * q - 1))
                link(v.tensor_tensor(scaled, ps[:, 6 + q % 2, :].rearrange("p (j d) -> p j d", j=2),
                                     sd_row[:].unsqueeze(1).to_broadcast([P, 2, D]), ALU.mult))
                for j in (2 * q, 2 * q + 1):
                    v.tensor_tensor(x[:, j, :], x[:, j, :], scaled[:, j % 2, :], ALU.add)\
                        .then_inc(*mark("x", n + 1, j))

            def quantised_second(n):
                x_low(n, 1)
                for u in range(NHID, NB * NHID):
                    hidden(n, u)
                    if u == NHID + 2:
                        quantised_out(n, 0)
                    if u == NHID + 3:
                        quantised_out(n, 1)
                    if u == NHID + 5 and n + 1 < LAST:
                        ln_stats(n + 1, 0)
                if n + 1 < LAST:
                    ln_norm(n + 1, 0)
                quantised_out(n, 2)
                quantised_out(n, 3)
                if n + 1 < LAST:
                    ln_stats(n + 1, 1)
                    ln_norm(n + 1, 1)

            def before_quantised(j):
                if j == TH:
                    x_low(3, 0)
                if j == TH + 1:
                    hidden(3, 0)
                if j == TH + 2:
                    for u in (1, 2):
                        hidden(3, u)
                        hidden_low(3, u - 1)
            expert_layer(2, before_quantised)
            hidden(3, 3)
            ln_norm(3, 1)
            hidden(3, 4)
            hidden(3, 5)
            quantised_second(3)


            def split_qk(u):
                b, m, i = u // 4, u // 2 % 2, u % 2
                tok = slice(b * SEQ, (b + 1) * SEQ)
                f = qk_f[:, u % 4, :]
                dve.wait_ge(*at("qk_p0", u))
                link(v.tensor_tensor(f, f, parts[i][:, m, 0, tok], ALU.subtract))
                v.tensor_copy(parts[i][:, m, 1, tok], f).then_inc(*mark("qk_p1", u))

            def values(w):
                dve.wait_ge(*at("proj_v", w))
                dst = val[:, 2 * w:2 * w + 2, 0:NH * VW].rearrange("p j (h c) -> p j h c", h=NH)[:, :, :, 0:HD]
                v.tensor_tensor(dst,
                                ps[:, 6 + w % 2, :].rearrange("p (j h c) -> p j h c", j=2, h=NH),
                                v_bias[:].rearrange("p (h c) -> p h c", h=NH).unsqueeze(1)
                                .to_broadcast([P, 2, NH, HD]), ALU.add).then_inc(*mark("val", w))

            def maxima(gr, i):
                qt, h0, k = MAX_UNITS[i]
                u = gr * NMU + i
                dve.wait_ge(*at("s_max", u))
                v.tensor_reduce(smax[:, gr % 2, qt, h0:h0 + k], max_view(u, qt), AX.X, ALU.max)\
                    .then_inc(*mark("smax", u))

            for b in range(NB):
                for u in range(4 * b, 4 * b + 4):
                    split_qk(u)
                    if u >= EARLY_AT:
                        maxima(0, u - EARLY_AT)
                if b == 0:
                    v.memset(val, 1.0).then_inc(*mark("val_ones"))
                    dve.wait_ge(*at("val_ones"))
                values(2 * b)
                if b == 1:
                    maxima(0, EARLY - 1)
                values(2 * b + 1)

            def split_maxima(gr):
                r = gr % 2
                dve.wait_ge(*at("smax", (gr + 1) * NMU - 1))
                if gr >= 2:
                    dve.wait_ge(*at("smax_tr", gr - 2))
                link(v.tensor_scalar(smax_p[:, r, :, 0, :], smax[:, r], -1.0, None, ALU.mult))
                link(v.scalar_tensor_tensor(smax_r[:], smax[:, r], -1.0, smax_p[:, r, :, 0, :],
                                            ALU.mult, ALU.subtract))
                link(v.tensor_copy(smax_p[:, r, :, 1, :], smax_r[:]))
                v.tensor_tensor(smax_p[:, r, :, 2, :], smax_r[:], smax_p[:, r, :, 1, :], ALU.subtract)\
                    .then_inc(*mark("smax_p", gr))

            def store_maxima(gr):
                dve.wait_ge(*at("smax_tr", gr))
                if gr >= 2:
                    dve.wait_ge(*at(f"smax_out{gr % 2}", gr - 2))
                v.tensor_copy(smax_t[:, gr % 2, :], smax_bank).then_inc(*mark("smax_t", gr))

            def context(gr):
                b, h0 = gr * HG // NH, gr * HG % NH
                dve.wait_ge(*at("ctx_mm", gr))
                src = ps[:, 7, :].rearrange("p (q h c) -> p q h c", q=TH, h=HG)
                link(v.reciprocal(den[:, gr % 2], src[:, :, :, HD]))
                dst = ctx_n[:, TH * b:TH * b + TH, HD * h0:HD * (h0 + HG)].rearrange("p q (h c) -> p q h c", h=HG)
                v.tensor_tensor(dst, src[:, :, :, 0:HD], den[:, gr % 2].unsqueeze(3).to_broadcast([P, TH, HG, HD]),
                                ALU.mult).then_inc(*mark("ctx", gr))

            def attended(b):
                for q in (2 * b, 2 * b + 1):
                    dve.wait_ge(*at("attn_out", q))
                    dve.wait_ge(*at("x_bias", NT - 1))
                    for j in (2 * q, 2 * q + 1):
                        v.tensor_tensor(x[:, j, :], x[:, j, :], ps[:, OUT_BANK[q], (j % 2) * D:(j % 2 + 1) * D],
                                        ALU.add).then_inc(*mark("x", 5, j))
                ln_stats(5, b)

            for gr in range(NG + LAG):
                if gr == NG + 1:
                    ln_norm(5, 0)
                for i in range(NMU):
                    if gr < NG and (gr or i >= EARLY):
                        maxima(gr, i)
                    if i == 1 and 0 < gr <= NG:
                        store_maxima(gr - 1)
                    if i == 3 and LAG < gr < NG + LAG:
                        context(gr - LAG - 1)
                if gr < NG:
                    split_maxima(gr)
                if gr == NG:
                    attended(0)
            x_low(5, 0)
            for u in range(NHID):
                hidden(5, u)
                if u == 0:
                    context(NG - 1)
                if u == 2:
                    attended(1)
                    ln_norm(5, 1)
            quantised_second(5)

        @block.tensor
        def _(pe):
            t = nc.tensor
            reader = {}

            def take(bank, *read):
                if bank in reader:
                    pe.wait_ge(*at(*reader[bank]))
                reader[bank] = read

            def keep_clock(bank, count):
                if bank in reader:
                    pe.wait_ge(*at(*reader[bank]))
                for _ in range(count):
                    t.matmul(ps[:, bank, :], ones[:], ones[:].unsqueeze(1).to_broadcast([P, 4, P]),
                             start=True, stop=True)

            def transposes(n, b, read="xnT"):
                for u in (2 * b, 2 * b + 1):
                    take(u % 2, read, n, u)
                    for j in (2 * u, 2 * u + 1):
                        pe.wait_ge(*at("xn", n, j))
                        for k in range(KD):
                            last = t.transpose(ps[:, u % 2, k * 256 + (j % 2) * P:k * 256 + (j % 2 + 1) * P],
                                               xn[:, j, k * P:(k + 1) * P], ident[:])
                    last.then_inc(*mark("tr", n, u))

            def logits(n, b):
                pe.wait_ge(*at("gate_in"))
                if b == 0:
                    take(2, "tanh_s", n)
                for j in range(TH * b, TH * b + TH):
                    pe.wait_ge(*at("xnT", n, j // 2))
                    for k in range(KD):
                        last = t.matmul(ps[:, 2, j * E:(j + 1) * E], xnT[:, k, j * P:(j + 1) * P], gate_w[:, k, :],
                                        start=(k == 0), stop=(k == KD - 1))
                if b == NB - 1:
                    last.then_inc(*mark("logits", n))

            def shared_up(n, u):
                h, m = divmod(u, MS)
                take(3 + u % 3, "relu_s", n, u)
                for k in range(KD):
                    last = t.matmul(ps[:, 3 + u % 3, :], sup_w[:, k, m * P:(m + 1) * P],
                                    xnT[:, k, h * SEQ:(h + 1) * SEQ], start=(k == 0), stop=(k == KD - 1))
                last.then_inc(*mark("up_s", n, u))

            def expert_layer(n):
                for u in range(2 if n == 2 else 0, MS):
                    shared_up(n, u)
                pe.wait_ge(*at("const"))
                pe.wait_ge(*at("used_b", n))
                take(2, "slot", n)
                used_flat = used_b.rearrange("p j e -> p (j e)")
                t.matmul(ps[:, 2, 0:NT * E], earlier[:], used_flat, start=True, stop=False)
                for i in range(1, NT):
                    last = t.matmul(ps[:, 2, i * E:NT * E], ones[:], used_flat[:, 0:(NT - i) * E],
                                    start=False, stop=(i == NT - 1))
                last.then_inc(*mark("pos", n))
                shared_up(n, MS)
                shared_up(n, MS + 1)
                take(2, "inv", n, len(FILLED) - 1)
                for part, filled in enumerate(FILLED):
                    pe.wait_ge(*at("onehot", n, part))
                    for q in filled:
                        own = slice(EQ * q, EQ * (q + 1))
                        for j in range(NT):
                            last = t.matmul(ps[:, 2, q * SLOT_B * EQ:(q + 1) * SLOT_B * EQ],
                                            is_a[:, q, j].rearrange("p a e -> p (a e)"), is_b[:, j, :, own],
                                            start=(j == 0), stop=(j == NT - 1))
                    last.then_inc(*mark("inv_mm", n, part))
                    if part < 2:
                        shared_up(n, MS + 2 + part)
                def up(g):
                    take(3 + g % 2, "relu_e", n, g)
                    pe.wait_ge(*at(f"up_in{g // 2}"))
                    last_u = (g + 1) * UQ - 1
                    pe.wait_ge(*at("xeT_act", n, last_u - 1, KD - 1))
                    pe.wait_ge(*at("xeT_dve", n, last_u, KD - 1))
                    for e in range(4 * g, 4 * g + 4):
                        rhs = xeT[e // EQ][:, :, e % EQ, :, :].rearrange("p k b a -> p k (b a)")
                        for k in range(KD):
                            last = t.matmul(ps[:, 3 + g % 2, (e % 4) * CAP:(e % 4 + 1) * CAP], up_w[:, k, e, :],
                                            rhs[:, k, :], start=(k == 0), stop=(k == KD - 1))
                    last.then_inc(*mark("up_e", n, g))

                def down(g):
                    pe.wait_ge(*at("hid_e", n, g))
                    pe.wait_ge(*at(f"down_in{g // 2}"))
                    for q in range(2):
                        u = 2 * g + q
                        take(5 + u % 3, "ye", n, g, q)
                        for e in (4 * g + 2 * q, 4 * g + 2 * q + 1):
                            last = t.matmul(ps[:, 5 + u % 3, (e % 2) * D:(e % 2 + 1) * D],
                                            hid_e[:, g % 2, (e % 4) * CAP:(e % 4 + 1) * CAP], down_w[:, e, :],
                                            start=True, stop=True)
                        last.then_inc(*mark("down_e", n, u))

                def transpose_slots(u):
                    take(u % 2, *(("xeT_dve" if u % 2 else "xeT_act"), n, u, KD - 1))
                    for g in (2 * u, 2 * u + 1):
                        pe.wait_ge(*at(f"xe{g % RING_XE}", n, g))
                        for k in range(KD):
                            c = (g % 2) * 256 + k * P
                            last = t.transpose(ps[:, u % 2, c:c + P], xe[:, g % RING_XE, k * P:(k + 1) * P],
                                               ident[:])
                    last.then_inc(*mark("xe_t", n, u))

                for u in range(UQ):
                    transpose_slots(u)
                for g in range(E // 4):
                    up(g)
                    for u in range(UQ + 2 * g, min(UQ + 2 * g + 2, NQ * UQ)):
                        transpose_slots(u)
                    if g:
                        down(g - 1)
                down(E // 4 - 1)
                pe.wait_ge(*at("sdown_in"))
                for u in range(NT // 2):
                    bank = 3 + u % 2
                    take(bank, "shared_out", n, u)
                    pe.wait_ge(*at("hid_s", n, NB * MS - 1))
                    for j in (2 * u, 2 * u + 1):
                        for m in range(MS):
                            last = t.matmul(ps[:, bank, (j % 2) * D:(j % 2 + 1) * D], hid_s[:, m, j * P:(j + 1) * P],
                                            sdown_w[:, m, :], start=(m == 0), stop=(m == MS - 1))
                    last.then_inc(*mark("down_s", n, u))

            pe.wait_ge(*at("const", "ident"))
            keep_clock(7, 12)
            for b in range(NB):
                transposes(0, b)
                logits(0, b)
            pe.wait_ge(*at("sup_in"))
            expert_layer(0)

            def gates(b):
                transposes(1, b)
                pe.wait_ge(*at("wa_in"))
                pe.wait_ge(*at("wx_in"))
                for m in range(KD):
                    u = KD * b + m
                    pe.wait_ge(*at("xnT", 1, 2 * b + 1))
                    for w, name, bank, read in ((wa, "proj_r", 2 + 2 * (u % 2), "tanh_r"),
                                                (wx, "proj_i", 3 + 2 * (u % 2), "tanh_i")):
                        take(bank, read, u)
                        for k in range(KD):
                            last = t.matmul(ps[:, bank, :], w[:, k, m * P:(m + 1) * P],
                                            xnT[:, k, b * SEQ:(b + 1) * SEQ], start=(k == 0), stop=(k == KD - 1))
                        last.then_inc(*mark(name, u))

            def states(b):
                for q in (2 * b, 2 * b + 1):
                    pe.wait_ge(*at("state", KD * b + KD - 1))
                    take(6 + q % 2, "x", 2, 2 * q + 1)
                    for j in (2 * q, 2 * q + 1):
                        for m in range(KD):
                            c = (j % 2) * D + m * P
                            last = t.transpose(ps[:, 6 + q % 2, c:c + P], state[:, m, j * P:(j + 1) * P], ident[:])
                    last.then_inc(*mark("state_t", q))

            gates(0)
            gates(1)
            states(0)
            transposes(2, 0)
            logits(2, 0)
            states(1)
            for u in range(2):
                shared_up(2, u)
            transposes(2, 1)
            logits(2, 1)
            expert_layer(2)

            def quantised(n):
                if n == 3:
                    transposes(n, 0, "x_lo")
                pe.wait_ge(*at("q_weights"))

                def down(q, tiles):
                    if tiles[0] == 0:
                        take(6 + q % 2, "x", n + 1, 2 * q + 1)
                    pe.wait_ge(*at("hid_lo", n, q // 2 * NHID + tiles[-1]))
                    for j in (2 * q, 2 * q + 1):
                        for m in tiles:
                            w = HID_TILES[m]
                            for part in range(2):
                                last = t.matmul(ps[:, 6 + q % 2, (j % 2) * D:(j % 2 + 1) * D],
                                                hid_r[0:w, part, m, j * P:(j + 1) * P], qd_w[0:w, m, :],
                                                start=(j == 2 * q and m == 0 and part == 0),
                                                stop=(j == 2 * q + 1 and m == NHID - 1 and part == 1))
                    if tiles[-1] == NHID - 1:
                        last.then_inc(*mark("q_down", n, q))

                for u in range(NB * NHID):
                    b, m = divmod(u, NHID)
                    if m == 0:
                        if b:
                            transposes(n, b, "x_lo")
                        pe.wait_ge(*at("x_lo", n, 2 * b + 1))
                    c, w = HID_AT[m], HID_TILES[m]
                    for wt, name, bank, read in ((qg_w, "q_gate", 2 + 2 * (u % 2), "gated"),
                                                 (qu_w, "q_up", 3 + 2 * (u % 2), "hid32")):
                        take(bank, read, n, u)
                        for k in range(KD):
                            for part in range(2):
                                last = t.matmul(ps[0:w, bank, :], wt[:, k, c:c + w],
                                                xr[n][:, part, k, b * SEQ:(b + 1) * SEQ],
                                                start=(k == 0 and part == 0), stop=(k == KD - 1 and part == 1))
                        last.then_inc(*mark(name, n, u))
                    if n == 5 and u == 0:
                        for kt in range(TH):
                            weighted_values(NG - 1, kt)
                        transpose_context(NG - 1)
                    if n == 5 and u == 1:
                        transpose_attended(1)
                    if n == 5 and u == 2:
                        project_out(1)
                    if u in (NHID + 2, NHID + 3):
                        down(u - NHID - 2, range(NHID))
                    if u == NB * NHID - 1:
                        down(2, range(NHID - 2))
                down(3, range(NHID - 2))
                for m in (NHID - 2, NHID - 1):
                    down(2, (m,))
                    down(3, (m,))
                if n + 1 < LAST:
                    transposes(n + 1, 0)

            quantised(3)

            def scores_max(gr, i):
                qt, h0, count = MAX_UNITS[i]
                u = gr * NMU + i
                b, head = gr * HG // NH, gr * HG % NH + h0
                if i == 0 and gr % 2 == 0:
                    pe.wait_ge(*at(f"stack_in{gr // 2}{Q}"))
                    pe.wait_ge(*at(f"stack_in{gr // 2}{K}"))
                first = 2 * (u % 2)
                take(first, "smax", u)
                if qt:
                    take(first + 1, "smax", u)
                width = (qt + 1) * P
                per_bank = {3: 1, 2: 1, 1: 2, 0: 4}[qt]
                q0 = b * SEQ + qt * P
                for c in range(count):
                    bank, col = first + c // per_bank, (c % per_bank) * width
                    t.matmul(ps[:, bank, col:col + width], stack[Q][0:KS, head + c, q0:q0 + P],
                             stack[K][0:KS, head + c, b * SEQ:b * SEQ + width], start=True, stop=False)
                    last = t.matmul(ps[:, bank, col + width - P:col + width], identb[:], hide_qk[:],
                                    start=False, stop=True)
                last.then_inc(*mark("s_max", u))

            pe.wait_ge(*at("wqkv_in"))
            for b in range(NB):
                if b:
                    transposes(4, b)
                pe.wait_ge(*at("xnT", 4, 2 * b + 1))
                for u in range(4 * b, 4 * b + 4):
                    m, i = u // 2 % 2, u % 2
                    take(4 + u % 2, "qk_f", u)
                    for k in range(KD):
                        c = i * D + m * P
                        last = t.matmul(ps[:, 4 + u % 2, :], wqkv[:, k, c:c + P], xnT[:, k, b * SEQ:(b + 1) * SEQ],
                                        start=(k == 0), stop=(k == KD - 1))
                    last.then_inc(*mark("proj_qk", u))
                    if u >= EARLY_AT:
                        scores_max(0, u - EARLY_AT)
                for w in (2 * b, 2 * b + 1):
                    take(6 + w % 2, "val", w)
                    for j in (2 * w, 2 * w + 1):
                        for k in range(KD):
                            last = t.matmul(ps[:, 6 + w % 2, (j % 2) * D:(j % 2 + 1) * D],
                                            xnT[:, k, j * P:(j + 1) * P], wqkv[:, k, 2 * D:3 * D],
                                            start=(k == 0), stop=(k == KD - 1))
                    last.then_inc(*mark("proj_v", w))
                    if w == 2:
                        scores_max(0, EARLY - 1)

            def transpose_maxima(gr):
                pe.wait_ge(*at("smax_p", gr))
                take(7, "smax_t", gr)
                for qt in range(TH):
                    last = t.transpose(smax_bank[:, qt * P:(qt + 1) * P],
                                       smax_p[:, gr % 2, qt, :, :].rearrange("p s h -> p (s h)"), identb[:])
                last.then_inc(*mark("smax_tr", gr))

            def scores_exp(pair, c):
                b, h = divmod(pair * 2, NH)
                if c == 0 and pair % 2 == 0:
                    pe.wait_ge(*at(f"smax_in{pair // 2 % 2}", pair // 2))
                    pe.wait_ge(*at("k_ones"))
                u = pair * 5 + c
                bank = 4 + u % 2
                take(bank, "prob", u)
                for hh, kt, col in PIECES[c]:
                    k0 = b * SEQ + kt * P
                    width = SEQ - kt * P
                    last = t.matmul(ps[:, bank, col:col + width], stack[K][0:KS + 3, h + hh, k0:k0 + P],
                                    stack[Q][0:KS + 3, h + hh, k0:k0 + width], start=True, stop=True)
                last.then_inc(*mark("st", u))

            def weighted_values(gr, kt):
                b, h = divmod(gr * HG, NH)
                if kt == 0:
                    pe.wait_ge(*at("causal", 10 * gr + 9))
                    pe.wait_ge(*at("val", 2 * b + 1))
                    take(6, "ctx_u", gr)
                for hh in range(HG):
                    piece, col = PLACE[hh % 2, kt]
                    first = (h + hh) * VW
                    last = t.matmul(ps[32 * hh:32 * hh + 32, 6, kt * P:SEQ], val[:, TH * b + kt, first:first + 32],
                                    prob(2 * gr + hh // 2, piece)[:, col:col + SEQ - kt * P],
                                    start=(kt == 0), stop=(kt == TH - 1))
                if kt == TH - 1:
                    last.then_inc(*mark("pv", gr))

            def transpose_context(gr):
                pe.wait_ge(*at("ctx_u", gr))
                take(7, "ctx", gr)
                for qt in range(TH):
                    last = t.transpose(ps[:, 7, qt * P:(qt + 1) * P], ctx_u[gr % 2][:, qt * P:(qt + 1) * P], ident[:])
                last.then_inc(*mark("ctx_mm", gr))

            def transpose_attended(b):
                for u in (2 * b, 2 * b + 1):
                    take(u % 2, "ctxT", u)
                    pe.wait_ge(*at("ctx", (b + 1) * (NG // NB) - 1))
                    for j in (2 * u, 2 * u + 1):
                        for k in range(KD):
                            last = t.transpose(ps[:, u % 2, k * 256 + (j % 2) * P:k * 256 + (j % 2 + 1) * P],
                                               ctx_n[:, j, k * P:(k + 1) * P], ident[:])
                    last.then_inc(*mark("ctx_tr", u))

            def project_out(b):
                pe.wait_ge(*at("wout_in"))
                for q in (2 * b, 2 * b + 1):
                    take(OUT_BANK[q], "x", 5, 2 * q + 1)
                    pe.wait_ge(*at("ctxT", q))
                    for j in (2 * q, 2 * q + 1):
                        for k in range(KD):
                            last = t.matmul(ps[:, OUT_BANK[q], (j % 2) * D:(j % 2 + 1) * D],
                                            xnT[:, k, j * P:(j + 1) * P], wout[:, k, :],
                                            start=(k == 0), stop=(k == KD - 1))
                    last.then_inc(*mark("attn_out", q))

            for gr in range(NG + LAG):
                live = gr >= LAG
                group = gr - LAG
                done = {step: 0 for step in "MEWTC"}
                for step in SCHEDULE:
                    i = done[step]
                    done[step] += 1
                    if step == "M" and gr < NG and (gr or i >= EARLY):
                        scores_max(gr, i)
                    elif step == "M" and (gr, i) == (NG, 0):
                        transpose_attended(0)
                    elif step == "M" and (gr, i) == (NG, 2):
                        project_out(0)
                    elif step == "M" and (gr, i) == (NG + 1, 1):
                        transposes(5, 0, "x_lo")
                    elif step == "E" and live:
                        scores_exp(2 * group + i // 5, i % 5)
                    elif step == "W" and group > 0:
                        weighted_values(group - 1, i)
                    elif step == "T" and 0 < gr <= NG:
                        transpose_maxima(gr - 1)
                    elif step == "C" and group > 0:
                        transpose_context(group - 1)
            quantised(5)


def _layouts(inputs):
    def rows(w, k):
        return w.reshape(k, P, *w.shape[1:]).swapaxes(0, 1)

    f = {k: np.asarray(v) for k, v in inputs.items()}
    wqkv = f["L1_attn_W_qkv"].reshape(D, NH, 3, HD).transpose(0, 2, 1, 3).reshape(D, 3 * D)
    bqkv = f["L1_attn_b_qkv"].reshape(NH, 3, HD).transpose(1, 0, 2).reshape(3, D)
    out = {
        "x": f["L0_attn_x"],
        "gate": rows(f["L0_ffn_gate_w"].T, KD),
        "bias_corr": f["L0_ffn_bias_corr"],
        "sup": rows(f["L0_ffn_shared_up_w"].T, KD),
        "sdown": rows(f["L0_ffn_shared_down_w"].T, MS),
        "up": rows(f["L0_ffn_up_w"].transpose(2, 0, 1), KD),
        "down": f["L0_ffn_down_w"].transpose(2, 0, 1),
        "wa": rows(f["L0_attn_Wa"].T, KD),
        "wx": rows(f["L0_attn_Wx"].T, KD),
        "ba": rows(f["L0_attn_ba"], KD),
        "bx": rows(f["L0_attn_bx"], KD),
        "lam": rows(f["L0_attn_Lam"], KD),
        "wqkv": rows(wqkv, KD),
        "bq": rows(bqkv[0], KD),
        "bk": rows(bqkv[1], KD),
        "bv": bqkv[2],
        "wout": rows(f["L1_attn_W_out"], KD),
        "bout": f["L1_attn_b_out"],
        "wq_gate": rows(f["L1_ffn_wq_gate"].T, KD),
        "wq_up": rows(f["L1_ffn_wq_up"].T, KD),
        "wq_down": f["L1_ffn_wq_down"].T,
        "s_gate": f["L1_ffn_s_gate"].reshape(HID, 1),
        "s_up": f["L1_ffn_s_up"].reshape(HID, 1),
        "s_down": f["L1_ffn_s_down"],
    }
    return {k: np.ascontiguousarray(v) for k, v in out.items()}


def kernel(**inputs):
    import concourse.bacc as bacc
    from concourse.bass_utils import run_bass_kernel_spmd

    arrays = _layouts(inputs)
    counts = Counts()
    for _ in range(2):
        nc = bacc.Bacc("TRN2", target_bir_lowering=False, num_devices=1)
        args = {k: nc.dram_tensor(f"in_{k}", v.shape, mybir.dt.from_np(v.dtype), kind="ExternalInput").ap()
                for k, v in arrays.items()}
        args["out"] = nc.dram_tensor("out_0", (NB, SEQ, D), F32, kind="ExternalOutput").ap()
        build(nc, args, counts)
    r = run_bass_kernel_spmd(nc, [{f"in_{k}": v for k, v in arrays.items()}], core_ids=[0])
    return r.results[0]["out_0"]
```
